# Optimizing a Trainium2 kernel written in Bass

```python
import numpy as np
import jax
import jax.numpy as jnp

def _softmax(x, axis=-1):
    return jax.nn.softmax(x, axis=axis)

def _gelu(x):
    return jax.nn.gelu(x, approximate=True)

def _silu(x):
    return jax.nn.silu(x)

def _sigmoid(x):
    return jax.nn.sigmoid(x)

def _layernorm(x, axis=-1, eps=1e-05):
    m = jnp.mean(x, axis=axis, keepdims=True)
    v = jnp.var(x, axis=axis, keepdims=True)
    return (x - m) / jnp.sqrt(v + eps)

def _scatter_add(tgt, idx, src, axis=0):
    return tgt.at[idx].add(src)

def _segment_sum(src, seg, n):
    return jax.ops.segment_sum(src, seg, n)
kernel_name = 'mk_gnn_ffn_d1_gnn_r8_d68960'

def setup_inputs(seed: int=0):
    np.random.seed(seed)
    _w = jnp.asarray

    def _rec_inputs():
        import jax
        import jax.numpy as jnp
        _gk = jax.random.key(seed)
        x = -0.0003929 + 0.9999 * jax.random.normal(jax.random.fold_in(_gk, 1), (1250, 1024), jnp.float32)
        src = jax.random.randint(jax.random.fold_in(_gk, 2), (40000,), 0, 1250, jnp.int32)
        dst = jnp.minimum((1250 * jax.random.uniform(jax.random.fold_in(_gk, 3), (40000,)) ** 2.0).astype(jnp.int32), 9999)
        _o = jnp.argsort(dst, stable=True)
        src = src[_o]
        dst = dst[_o]
        return (x, src, dst)
    x, src, dst = _rec_inputs()

    def _L0_gnn_setup():
        import jax, jax.numpy as jnp
        import numpy as np
        N_NODES = 2048
        HID_IN = 1024
        HID_MID = 1500
        N_EDGES = 16384

        def _gcn_conv(x, W, b, src, dst, inv_sqrt_deg, n_nodes):
            h = x @ W
            norm = inv_sqrt_deg[src] * inv_sqrt_deg[dst]
            msg = h[src] * norm[:, None]
            out = jax.ops.segment_sum(msg, dst, num_segments=n_nodes)
            return out + b
        key = jax.random.key(seed)
        k1, k2, k3, k4, k5, k6 = jax.random.split(key, 6)
        x = jax.random.normal(k1, (N_NODES, HID_IN), dtype=jnp.float32)
        edge_index = jax.random.randint(k2, (2, N_EDGES), 0, N_NODES, dtype=jnp.int64)
        W1 = jax.random.normal(k3, (HID_IN, HID_MID), dtype=jnp.float32) / np.sqrt(HID_IN)
        b1 = jnp.zeros((HID_MID,), dtype=jnp.float32)
        W2 = jax.random.normal(k4, (HID_MID, HID_IN), dtype=jnp.float32) / np.sqrt(HID_MID)
        b2 = jnp.zeros((HID_IN,), dtype=jnp.float32)
        return {'x': x, 'edge_index': edge_index, 'W1': W1, 'b1': b1, 'W2': W2, 'b2': b2}
    _L0_gnn_all = _L0_gnn_setup()
    _L0_gnn_in = {k: v for k, v in _L0_gnn_all.items() if k in ('W1', 'b1', 'W2', 'b2')}
    del _L0_gnn_all

    def _L0_ffn_setup():
        import jax, jax.numpy as jnp
        import numpy as np
        B, C, D, O = (4, 512, 1024, 1024)
        PROJ = 256
        RANKS = [1, 2, 4, 8]
        E = len(RANKS)
        CLAMP_MAX = float(np.log(1.0 / 0.01))

        def _l2norm(v, axis):
            return v / jnp.maximum(jnp.linalg.norm(v, axis=axis, keepdims=True), 1e-12)
        key = jax.random.key(seed)
        ks = jax.random.split(key, 16)
        inp = {'x': jax.random.normal(ks[0], (B, C, D), dtype=jnp.float32), 'W': jax.random.normal(ks[1], (O, D), dtype=jnp.float32) / np.sqrt(D), 'Wp': jax.random.normal(ks[2], (PROJ, D), dtype=jnp.float32) / np.sqrt(D), 'bp': jnp.zeros((PROJ,), dtype=jnp.float32), 'sim': jax.random.normal(ks[3], (PROJ, E), dtype=jnp.float32) * 0.01, 'temp': jnp.full((1,), np.log(1.0 / 0.5), dtype=jnp.float32)}
        for i, r in enumerate(RANKS):
            inp[f'Wd{i}'] = jax.random.normal(ks[4 + 2 * i], (r, D), dtype=jnp.float32) / r
            inp[f'Wu{i}'] = jax.random.normal(ks[5 + 2 * i], (O, r), dtype=jnp.float32) * 0.01
        return inp
    _L0_ffn_all = _L0_ffn_setup()
    _L0_ffn_in = {k: v for k, v in _L0_ffn_all.items() if k in ('W', 'Wp', 'bp', 'sim', 'temp', 'Wd0', 'Wu0', 'Wd1', 'Wu1', 'Wd2', 'Wu2', 'Wd3', 'Wu3')}
    del _L0_ffn_all
    return {'x': x, 'src': src, 'dst': dst, 'L0_gnn_W1': _L0_gnn_in['W1'], 'L0_gnn_b1': _L0_gnn_in['b1'], 'L0_gnn_W2': _L0_gnn_in['W2'], 'L0_gnn_b2': _L0_gnn_in['b2'], 'L0_ffn_W': _L0_ffn_in['W'], 'L0_ffn_Wp': _L0_ffn_in['Wp'], 'L0_ffn_bp': _L0_ffn_in['bp'], 'L0_ffn_sim': _L0_ffn_in['sim'], 'L0_ffn_temp': _L0_ffn_in['temp'], 'L0_ffn_Wd0': _L0_ffn_in['Wd0'], 'L0_ffn_Wu0': _L0_ffn_in['Wu0'], 'L0_ffn_Wd1': _L0_ffn_in['Wd1'], 'L0_ffn_Wu1': _L0_ffn_in['Wu1'], 'L0_ffn_Wd2': _L0_ffn_in['Wd2'], 'L0_ffn_Wu2': _L0_ffn_in['Wu2'], 'L0_ffn_Wd3': _L0_ffn_in['Wd3'], 'L0_ffn_Wu3': _L0_ffn_in['Wu3']}

def reference(x, src, dst, L0_gnn_W1, L0_gnn_b1, L0_gnn_W2, L0_gnn_b2, L0_ffn_W, L0_ffn_Wp, L0_ffn_bp, L0_ffn_sim, L0_ffn_temp, L0_ffn_Wd0, L0_ffn_Wu0, L0_ffn_Wd1, L0_ffn_Wu1, L0_ffn_Wd2, L0_ffn_Wu2, L0_ffn_Wd3, L0_ffn_Wu3):
    import jax
    import jax.numpy as jnp

    def _L0_gnn_ref(x, edge_index, W1, b1, W2, b2):
        import jax, jax.numpy as jnp
        import numpy as np
        N_NODES = 2048
        HID_IN = 1024
        HID_MID = 1500
        N_EDGES = 16384

        def _gcn_conv(x, W, b, src, dst, inv_sqrt_deg, n_nodes):
            h = x @ W
            norm = inv_sqrt_deg[src] * inv_sqrt_deg[dst]
            msg = h[src] * norm[:, None]
            out = jax.ops.segment_sum(msg, dst, num_segments=n_nodes)
            return out + b
        n = x.shape[0]
        loops = jnp.arange(n, dtype=edge_index.dtype)
        src = jnp.concatenate([edge_index[0], loops])
        dst = jnp.concatenate([edge_index[1], loops])
        deg = jax.ops.segment_sum(jnp.ones_like(dst, dtype=x.dtype), dst, num_segments=n)
        inv_sqrt_deg = jnp.where(deg > 0, jax.lax.rsqrt(jnp.maximum(deg, 1.0)), 0.0)
        h = _gcn_conv(x, W1, b1, src, dst, inv_sqrt_deg, n)
        h = jax.nn.relu(h)
        out = _gcn_conv(h, W2, b2, src, dst, inv_sqrt_deg, n)
        return out

    def _L0_ffn_ref(x, W, Wp, bp, sim, temp, Wd0, Wu0, Wd1, Wu1, Wd2, Wu2, Wd3, Wu3):
        import jax, jax.numpy as jnp
        import numpy as np
        B, C, D, O = (4, 512, 1024, 1024)
        PROJ = 256
        RANKS = [1, 2, 4, 8]
        E = len(RANKS)
        CLAMP_MAX = float(np.log(1.0 / 0.01))

        def _l2norm(v, axis):
            return v / jnp.maximum(jnp.linalg.norm(v, axis=axis, keepdims=True), 1e-12)
        base = jnp.einsum('bcd,od->bco', x, W)
        xf = x.reshape(-1, x.shape[-1])
        proj = _l2norm(xf @ Wp.T + bp, axis=1)
        simn = _l2norm(sim, axis=0)
        scale = jnp.exp(jnp.minimum(temp, CLAMP_MAX))
        logits = proj @ simn * scale
        lw = jax.nn.softmax(logits, axis=1)
        top1 = jnp.argmax(lw, axis=1)
        ret = jnp.where(jnp.arange(E)[None, :] == top1[:, None], lw, 0.0)
        ret = ret.reshape(x.shape[0], x.shape[1], E)
        downs = (Wd0, Wd1, Wd2, Wd3)
        ups = (Wu0, Wu1, Wu2, Wu3)
        l = jnp.stack([jnp.einsum('bcr,or->bco', jnp.einsum('bcd,rd->bcr', x, d), u) for d, u in zip(downs, ups)], axis=2)
        res = jnp.sum(ret[..., None] * l, axis=2)
        return base + res
    edge_index = jnp.stack([src, dst])
    x = x + _L0_gnn_ref(_layernorm(x, axis=-1), edge_index, L0_gnn_W1, L0_gnn_b1, L0_gnn_W2, L0_gnn_b2)
    x = x + _L0_ffn_ref(_layernorm(x, axis=-1)[None], L0_ffn_W, L0_ffn_Wp, L0_ffn_bp, L0_ffn_sim, L0_ffn_temp, L0_ffn_Wd0, L0_ffn_Wu0, L0_ffn_Wd1, L0_ffn_Wu1, L0_ffn_Wd2, L0_ffn_Wu2, L0_ffn_Wd3, L0_ffn_Wu3)[0]
    return x

_drawn_inputs = setup_inputs


def setup_inputs(seed=0):
    import zlib

    import numpy as np

    out = dict(_drawn_inputs(seed))
    spreads = {'L0_gnn_b1': (0.0, 0.1), 'L0_gnn_b2': (0.0, 0.1), 'L0_ffn_bp': (0.0, 0.764)}
    factors = {'L0_ffn_Wd1': 2.838,
     'L0_ffn_Wu1': 2.953,
     'L0_ffn_Wd2': 3.667,
     'L0_ffn_Wu2': 3.677,
     'L0_ffn_Wd3': 6.079,
     'L0_ffn_Wu3': 6.054}
    for name, (base, spread) in spreads.items():
        noise = np.random.default_rng([zlib.crc32(name.encode()), seed]).standard_normal(out[name].shape)
        drawn = base * np.exp(spread * noise) if base else spread * noise
        out[name] = jnp.asarray(drawn.astype(out[name].dtype))
    for name, factor in factors.items():
        out[name] = (out[name] * factor).astype(out[name].dtype)
    return out
```

```python
from contextlib import ExitStack
from math import sqrt

import numpy as np
import concourse.bass as bass
from concourse import mybir

ALU = mybir.AluOpType
ACT = mybir.ActivationFunctionType
F32 = mybir.dt.float32
F16 = mybir.dt.float16
I32 = mybir.dt.int32
AX_X = mybir.AxisListType.X

P = 128
N = 1250
D = 1024
MID = 1500
E = 40000
PROJ = 256
RANKS = (1, 2, 4, 8)
NEXP = len(RANKS)
R = sum(RANKS)
PD = PROJ + R
CLAMP_MAX = float(np.log(1.0 / 0.01))

NT = -(-N // P)
FT = D // P
MT = -(-MID // P)
W = 32
NWIN = NT * P // W
WPT = P // W
KEYS = NT * W
NCH = -(-E // P)
CG = -(-NCH // P)
CROWS = CG * P
DSPLIT = [(0, 417), (417, 417), (834, 416)]
MIDP = MT * P
HALF = MIDP // 2
GP = 96

X_SCALE = 1024.0
T1_SCALE = 8.0

KG = 4
KRING = 16
SRING = 32
SLOTS = MT + 1


def feature_pieces(i):
    out, c, end = [], i * FSLOT, min((i + 1) * FSLOT, NCH)
    while c < end:
        n = min(end - c, P - c % P)
        out.append((c // P, c % P, n, (c - i * FSLOT) * P))
        c += n
    return out


def rows(t, n):
    return min(P, n - t * P)


def expected_ranges():
    out = []
    for w in range(NWIN):
        u0, u1 = (min(1.0, sqrt(v * W / N)) for v in (w, w + 1))
        first = (E * u0 - 4.5 * sqrt(E * u0 * (1 - u0))) / P
        end = (E * u1 + 4.5 * sqrt(E * u1 * (1 - u1))) / P
        out.append((max(0, min(int(first), NCH - 1)), min(NCH, int(end) + 1)))
    return out


RANGES = expected_ranges()
STEPS = [(w, c) for w, (a, b) in enumerate(RANGES) for c in range(a, b)]
LAST_STEP = {c: n for n, (_, c) in enumerate(STEPS)}
NSTEPS = len(STEPS)
FIRST_STEP = {}
for n, (_, c) in enumerate(STEPS):
    FIRST_STEP.setdefault(c, n)
assert sorted(LAST_STEP) == list(range(NCH))

SG = 4
NSG = -(-NCH // SG)
FSLOT = 24
NF = -(-NCH // FSLOT)
AHEAD = 5
ISSUE = {}
for g in range(NSG):
    ISSUE.setdefault(FIRST_STEP[SG * (g - AHEAD)] if g >= AHEAD else 0, []).append(g)
for g in range(SRING // SG, NSG):
    last = max(LAST_STEP[c] for c in range(SG * g - SRING, SG * g - SRING + SG))
    later = min(n for n, gs in ISSUE.items() if g + 2 in gs) if g + 2 < NSG else FIRST_STEP[SG * g]
    assert last // KG * KG + KG <= min(later, FIRST_STEP[SG * g]), (g, last, later)


DEG_AT, ROOT_AT, SCALE_AT, SOURCE_AT, LO_AT = ({NWIN: []} for _ in range(5))
for g in range(NT):
    w0 = WPT * g + WPT + 1
    for table, w in ((DEG_AT, w0), (ROOT_AT, w0 + 1), (SCALE_AT, max(w0 + 3, 18 + g // 3)),
                     (SOURCE_AT, max(w0 + 3, 19 + 2 * g)), (LO_AT, max(w0 + 5, 22 + 2 * g))):
        table.setdefault(min(w, NWIN), []).append(g)
SQ_A = 8
SQ_AT = {29 + i: (i,) for i in range(SQ_A)}
W1_AT = {f: range(3 * (f - 2), min(3 * (f - 1), 2 * FT)) for f in range(2, FT)}
W2_AT = {7: (0, 1, 2), 8: (3, 4, 5), 9: (6, 7, 8), 10: (9, 10), 11: (11,)}


def build(nc, x, src_rows, dst_rows, ranges, line, W1, b1, W2, b2, WT, WpdT, bp, simT, temp, WuT, out):
    with ExitStack() as ctx:
        def sb(name, shape, dt):
            return ctx.enter_context(nc.sbuf_tensor(name, shape, dt))

        def sem(name):
            return ctx.enter_context(nc.semaphore(name))

        adj = sb("adj", [P, NT, NT * P], F16)
        arena2 = sb("arena2", [P, 2 * NT * D + NT * NT * P], F16)
        arena3 = sb("arena3", [P, SLOTS * 2048], F16)
        arena4 = sb("arena4", [P, 2 * NT * D], F16)

        class Carve:
            def __init__(self, arena, size):
                self.arena, self.at, self.size = arena, 0, size

            def take(self, n, dt=F16):
                words = n * (2 if dt != F16 else 1)
                v = self.arena[:, self.at:self.at + words]
                self.at += words
                assert self.at <= self.size, (self.at, self.size)
                return v if dt == F16 else v.bitcast(dt)

        A2, A3, A4 = 2 * NT * D + NT * NT * P, SLOTS * 2048, 2 * NT * D
        c = Carve(arena2, A2)
        xs_hi = c.take(NT * D).rearrange("p (t f) -> p t f", t=NT)
        xs_lo = c.take(NT * D).rearrange("p (t f) -> p t f", t=NT)
        adj_rest = c.take(NT * NT * P).rearrange("p (t d) -> p t d", t=NT)
        c = Carve(arena2, A2)
        hT = [c.take(MT * N).rearrange("p (m d) -> p m d", m=MT) for _ in range(2)]
        c = Carve(arena2, A2)
        x2 = c.take(NT * D, F32).rearrange("p (t f) -> p t f", t=NT)
        yT_hi = c.take(FT * NT * P).rearrange("p (k d) -> p k d", k=FT)
        wpd_hi = c.take(FT * PD).rearrange("p (k n) -> p k n", k=FT)
        c = Carve(arena3, A3)
        x_raw = c.take(NT * D, F32).rearrange("p (t f) -> p t f", t=NT)
        feat_rows = c.take(2 * FSLOT * P).rearrange("p (s n) -> p s n", s=2)
        slots = arena3[:, :].rearrange("p (s n) -> p s n", s=SLOTS)
        w1_slot = [slots[:, m + 1, :].rearrange("p (h k n) -> p h k n", h=2, k=FT) for m in range(MT)]
        w2_slot = [slots[:, k, :].rearrange("p (h n) -> p h n", h=2) for k in range(MT)]
        c = Carve(arena3, A3)
        yT_lo = c.take(FT * NT * P).rearrange("p (k d) -> p k d", k=FT)
        wpd_lo = c.take(FT * PD + 8)[:, 0:FT * PD].rearrange("p (k n) -> p k n", k=FT)
        at = c.at
        rest2 = c.take(NT * NT * P).rearrange("p (t d) -> p t d", t=NT)
        c.at = at
        w_hi = c.take(FT * D).rearrange("p (k n) -> p k n", k=FT)
        c = Carve(arena4, A4)
        src_hot = c.take(SRING * P).rearrange("p (s n) -> p s n", s=SRING)
        key_hot = c.take(KRING * KEYS).rearrange("p (s n) -> p s n", s=KRING)
        feat = [c.take(CROWS).rearrange("p (j e) -> p j e", j=CG) for _ in range(3)]
        key_col = c.take(CROWS, F32)
        src_col = c.take(CROWS, F32)
        src_i, dst_i, up_i, low_i = (c.take(CROWS, I32).rearrange("p (j e) -> p j e", j=CG) for _ in range(4))
        dkey, keyf, srcf = (c.take(CROWS, F32).rearrange("p (j e) -> p j e", j=CG) for _ in range(3))
        chunk_up, chunk_down = (c.take(CROWS, F32) for _ in range(2))
        touch = [keyf.rearrange("p j e -> p (j e)"), srcf.rearrange("p j e -> p (j e)"), dkey.rearrange("p j e -> p (j e)")]
        touch2 = c.take(CROWS, F32)
        c = Carve(arena4, A4)
        t1T = [c.take(FT * N).rearrange("p (k d) -> p k d", k=FT) for _ in range(2)]
        c = Carve(arena4, A4)
        z = [c.take(NT * D).rearrange("p (t f) -> p t f", t=NT) for _ in range(2)]
        c = Carve(arena4, A4)
        w_lo = c.take(FT * D).rearrange("p (k n) -> p k n", k=FT)
        g_rows = c.take(NT * GP).rearrange("p (t r) -> p t r", t=NT)
        gT = c.take(NT * P).rearrange("p (t d) -> p t d", t=NT)
        res = [c.take(D, F32) for _ in range(2)]
        scratch = c.take(PROJ, F32)
        pr = [c.take(PROJ, F32) for _ in range(2)]
        down = c.take(NT * R, F32).rearrange("p (t r) -> p t r", t=NT)
        gated = c.take(NT * R, F32).rearrange("p (t r) -> p t r", t=NT)
        wu_raw = c.take(D, F32)
        wu = c.take(D)

        stage = sb("stage", [P, 2, D], F32)
        junk = sb("junk", [P, D], mybir.dt.bfloat16)
        val = sb("val", [P, 2, 512], F32)
        row_bc = sb("row_bc", [P, 1280], F32)
        sim_bc = row_bc[:, 0:D].rearrange("p (e n) -> p e n", e=NEXP)
        bp_bc = row_bc[:, D:D + PROJ]
        ident = sb("ident", [P, P], F32)
        ident16 = sb("ident16", [P, P], F16)
        minus16 = sb("minus16", [P, P], F16)
        ones = sb("ones", [P, P], F32)
        ones16 = sb("ones16", [P, NWIN], F16)
        zero16 = sb("zero16", [P, W], F16)
        iota16 = sb("iota16", [P, KEYS], F16)
        diag16 = val[:, :, :].rearrange("p a b -> p (a b)").bitcast(F16)[:, 0:2 * CG * P]\
            .rearrange("p (k j n) -> p k j n", k=2, j=CG)
        line16 = sb("line16", [P, P], F16)
        win_key = sb("win_key", [P, NWIN], F32)
        win_edge = sb("win_edge", [P, 2], F32)
        rng_sb = sb("rng_sb", [P, 2], F32)
        flag_i = sb("flag_i", [1, 2], I32)
        cols = sb("cols", [P, 176], F32)
        used_cols = [0]

        def col(n):
            used_cols[0] += n
            assert used_cols[0] <= 176
            return cols[:, used_cols[0] - n:used_cols[0]]

        cmin, cmax, bcol, badc = col(CG), col(CG), col(2), col(2)
        xsum, xss, nmean, rstd = col(NT), col(NT), col(NT), col(NT)
        sdeg, isd, xscale, xbias = col(NT), col(NT), col(NT), col(NT)
        rstd2, degv, ntmp = col(NT), col(NT), col(1)
        eps_c, bigc, temp_c, tempe = col(1), col(2), col(1), col(1)
        b1c, b1s = col(MT), col(MT)
        small = sb("small", [P, 320], F32)
        used_small = [0]

        def sm(n):
            used_small[0] += n
            assert used_small[0] <= 320
            return small[:, used_small[0] - n:used_small[0]]

        w1_ss, w2_ss, w_ss, wpd_ss = sm(2 * FT), sm(MT), sm(FT), sm(FT)
        t1_ss, h_ss = sm(3 * FT), sm(3 * MT)
        sums = sm(8)
        norms = sm(8)
        bound, pw, ipw, coef = sm(8), sm(8), sm(8), sm(8)
        zcoef, ocoef = sm(NT), sm(NT)
        stats, mv, lnr = sm(12), sm(2), sm(4)
        W1_, B1_, T1_, W2_, H_, PD_, WW_, WU_ = range(8)
        Z_, G_ = B1_, T1_
        C_H, C_P, C_B, C_L = range(4)
        gate = sb("gate", [P, 13, NT, NEXP], F32)
        dots, logit, ex, prob, hit, keep, pick = (gate[:, i] for i in range(7))
        pss, pnorm, gmax, gsum, pscale = (gate[:, 7 + i].rearrange("p t e -> p (t e)")[:, 0:NT] for i in range(5))
        simss, simr, tempv = gate[:, 12, 0], gate[:, 12, 1], gate[:, 12, 2, 0:1]

        bank = [ctx.enter_context(nc.psum_tensor(f"bank{i}", [P, 512], F32)) for i in range(8)]
        rest_dram = nc.dram_tensor("adj_rest_dram", (P, NT * NT * P), F16, kind="Internal").ap()

        S = {}

        class Sems:
            def __getitem__(self, name):
                if name not in S:
                    S[name] = sem(name)
                return S[name]

        S_ = Sems()
        x_in = [sem(f"x_in{t}") for t in range(NT)]
        xr_in = [sem(f"xr_in{t}") for t in range(NT)]
        feat_in = [sem(f"feat_in{i}") for i in range(2)]
        stage_in = [sem(f"stage_in{i}") for i in range(2)]
        out_done = [sem(f"out_done{i}") for i in range(2)]

        class Link:
            def __init__(self, eng, s):
                self.eng, self.s, self.n = eng, S_[s], 0

            def __call__(self, ins):
                self.n += 1
                ins.then_inc(self.s, 1)
                self.eng.wait_ge(self.s, self.n)

        loads = [("sq", "W1", k, h * HALF, HALF) for k in range(FT) for h in range(2)]
        loads += [("split", "W1", k, h * HALF, HALF) for k in range(FT) for h in range(2)]
        loads += [("sq", "W2", k, 0, D) for k in range(MT)]
        loads += [("split", "W2", k, 0, D) for k in range(MT)]
        loads += [("sq", "Wpd", k, 0, PD) for k in range(FT)]
        loads += [("sq", "W", k, 0, D) for k in range(FT)]
        loads += [("split", "Wpd", k, 0, PD) for k in range(FT)]
        loads += [("split", "W", k, 0, D) for k in range(FT)]
        dram = {"W1": W1, "W2": W2, "Wpd": WpdT, "W": WT}
        nrows = {"W1": D, "W2": MID, "Wpd": D, "W": D}
        squares = [0]
        for kind, *_ in loads:
            squares.append(squares[-1] + (kind == "sq"))

        def stage_freed(eng, i):
            if loads[i][0] == "sq":
                eng.wait_ge(S_["stage_sq"], squares[i + 1])
            else:
                eng.wait_ge(S_["stage_lo"], i + 1 - squares[i + 1])

        def places(a, k, c0):
            if a == "W1":
                v = arena3[:, :].rearrange("p (s h k n) -> p s h k n", s=SLOTS, h=2, k=FT)
                q = slice(1 + c0 // P, 1 + (c0 + HALF) // P)
                return v[:, q, 0, k, :], v[:, q, 1, k, :], W1_
            if a == "W2":
                return w2_slot[k][:, 0, :], w2_slot[k][:, 1, :], W2_
            if a == "Wpd":
                return wpd_hi[:, k, :], wpd_lo[:, k, :], PD_
            return w_hi[:, k, :], w_lo[:, k, :], WW_

        NCONST = 15
        block = ctx.enter_context(nc.Block())

        @block.sync
        def _(sp):
            sp.dma_start(dst_i[:], dst_rows.rearrange("(j p) e -> p j e", p=P)).then_inc(S_["edges_in"], 16)
            sp.dma_start(src_i[:], src_rows.rearrange("(j p) e -> p j e", p=P)).then_inc(S_["edges_in"], 16)
            sp.dma_start(rng_sb[0:NWIN, :], ranges).then_inc(S_["ranges_in"], 16)
            sp.dma_start(line16[:], line).then_inc(S_["line_in"], 16)
            for t in range(NT):
                m = rows(t, N)
                sp.dma_start(x_raw[0:m, t, :], x[t * P:t * P + m, :]).then_inc(x_in[t], 16)
            for i, (kind, a, k, c0, n) in enumerate(loads):
                if i >= 2:
                    stage_freed(sp, i - 2)
                m = rows(k, nrows[a])
                sp.dma_start(stage[0:m, i % 2, 0:n], dram[a][k * P:k * P + m, c0:c0 + n])\
                    .then_inc(stage_in[i % 2], 16)

        @block.gpsimd
        def _(gp):
            gp.memset(ident[:], 0.0).then_inc(S_["consts_z"], 1)
            gp.memset(ident16[:], 0.0).then_inc(S_["consts_z"], 1)
            gp.memset(minus16[:], 0.0).then_inc(S_["consts_z"], 1)
            gp.wait_ge(S_["consts_z"], 3)
            for m, v in ((ident, 1.0), (ident16, 1.0), (minus16, -1.0)):
                gp.affine_select(out=m[:], in_=m[:], compare_op=ALU.not_equal, fill=v, base=0,
                                 pattern=[[-1, P]], channel_multiplier=1).then_inc(S_["consts"], 1)
            for o, pattern, base, mult in ((iota16[:], [[1, KEYS]], 0, 0), (win_key[:], [[KEYS, NWIN]], 0, 0),
                                           (win_edge[:], [[W, 2]], 0, W), (chunk_up, [[1, CROWS]], 1, 0),
                                           (chunk_down, [[-1, CROWS]], CROWS, 0)):
                gp.iota(o, pattern, base=base, channel_multiplier=mult,
                        allow_small_or_imprecise_dtypes=True).then_inc(S_["consts"], 1)
            for o, v in ((zero16[:], 0.0), (ones16[:], 1.0), (ones[:], 1.0), (small[:], 0.0), (gate[:], 0.0), (cols[:], 0.0)):
                gp.memset(o, v).then_inc(S_["consts"], 1)
            gp.wait_ge(S_["consts"], 14)
            gp.memset(eps_c, 1e-5).then_inc(S_["consts"], 1)
            gp.dma_start(b1c, b1).then_inc(S_["b1_in"], 16)
            gp.memset(feat_rows, 1.0).then_inc(S_["feat_ones"], 1)
            gp.wait_ge(S_["feat_ones"], 1)
            gp.wait_ge(S_["feat_made"], 1)
            gp.wait_ge(S_["flag_set"], 1)
            bad = gp.value_load(flag_i[0:1, 0:1], min_val=0, max_val=2 * NWIN)
            with gp.If(bad == 0):
                for i in range(NF):
                    if i >= 2:
                        gp.wait_ge(S_["score_made"], min(NSG, FSLOT // SG * (i - 1)))
                    for k in range(3):
                        for j, r0, n, at in feature_pieces(i):
                            gp.dma_start(feat_rows[k:k + 1, i % 2, at:at + n * P], feat[k][r0:r0 + n, j, :])\
                                .then_inc(feat_in[i % 2], 16)
            with gp.Else():
                gp.nop()
            gp.wait_ge(S_["rest_made"], NWIN)
            gp.dma_start(rest_dram, adj_rest.rearrange("p t d -> p (t d)")).then_inc(S_["spilled"], 16)
            gp.wait_ge(S_["t1_lo"], 3 * FT)
            gp.dma_start(row_bc[:, 0:D], b2.partition_broadcast(P)).then_inc(S_["b2_in"], 16)
            gp.wait_ge(S_["z_mm"], NT)
            for t in range(NT):
                m = rows(t, N)
                gp.dma_start(x2[0:m, t, :], x[t * P:t * P + m, :]).then_inc(xr_in[t], 16)
            gp.wait_ge(S_["spilled"], 16)
            gp.dma_start(rest2.rearrange("p t d -> p (t d)"), rest_dram).then_inc(S_["rest_in"], 16)
            gp.wait_ge(S_["b2_in"], 16)
            for t in range(NT):
                m = rows(t, N)
                gp.wait_ge(xr_in[t], 16)
                gp.tensor_tensor(x2[0:m, t, :], x2[0:m, t, :], row_bc[0:m, 0:D], ALU.add).then_inc(S_["x2_b"], 1)
            gp.wait_ge(S_["x2_b"], NT)
            gp.dma_start(sim_bc[:], simT.partition_broadcast(P)).then_inc(S_["sim_in"], 16)
            gp.dma_start(bp_bc[:], bp.partition_broadcast(P)).then_inc(S_["sim_in"], 16)
            gp.dma_start(temp_c, temp.partition_broadcast(P)).then_inc(S_["sim_in"], 16)
            gp.wait_ge(S_["o_mm"], NT)
            gp.memset(wu_raw[0:GP, :], 0.0).then_inc(S_["link_p"], 1)
            gp.memset(g_rows[:], 0.0).then_inc(S_["link_p"], 1)
            gp.wait_ge(S_["link_p"], 2)
            for q in range(3):
                gp.dma_start(wu_raw[32 * q:32 * q + R, :], WuT).then_inc(S_["wu_in"], 16)
            for t in range(NT):
                m = rows(t, N)
                gp.wait_ge(S_["res_made"], t + 1)
                gp.dma_start(out[t * P:t * P + m, :], res[t % 2][0:m, :]).then_inc(out_done[t % 2], 16)
            for s in out_done:
                gp.wait_ge(s, 16 * NT // 2)

        @block.vector
        def _(dve):
            V = nc.vector
            link = Link(dve, "link_v")

            dve.wait_ge(S_["edges_in"], 32)
            dve.wait_ge(S_["consts"], NCONST)
            V.tensor_reduce(cmin, dst_i, AX_X, ALU.min)
            link(V.tensor_reduce(cmax, dst_i, AX_X, ALU.max))
            for j in range(CG):
                V.tensor_scalar(diag16[:, 0, j, :], ident16[:], cmin[:, j:j + 1], None, ALU.mult)
                last = V.tensor_scalar(diag16[:, 1, j, :], ident16[:], cmax[:, j:j + 1], None, ALU.mult)
            last.then_inc(S_["chunk_ends"], 1)
            V.tensor_scalar(up_i, dst_i, W.bit_length() - 1, None, ALU.logical_shift_right)
            link(V.tensor_scalar(low_i, dst_i, W - 1, None, ALU.bitwise_and))
            link(V.scalar_tensor_tensor(dkey, up_i, float(KEYS), low_i, ALU.mult, ALU.add))
            V.tensor_scalar(up_i, src_i, P.bit_length() - 1, None, ALU.logical_shift_right)
            link(V.tensor_scalar(low_i, src_i, P - 1, None, ALU.bitwise_and))
            V.scalar_tensor_tensor(keyf, up_i, float(W), dkey, ALU.mult, ALU.add)
            link(V.tensor_copy(srcf, low_i))
            V.tensor_copy(feat[2], low_i).then_inc(S_["keys_ready"], 1)
            link(V.tensor_tensor(up_i, low_i, low_i, ALU.mult))
            link(V.tensor_scalar(low_i, up_i, 15, None, ALU.bitwise_and))
            link(V.tensor_scalar(up_i, up_i, 4, None, ALU.logical_shift_right))
            V.tensor_copy(feat[0], up_i)
            V.tensor_copy(feat[1], low_i).then_inc(S_["feat_made"], 1)
            for i, c in enumerate((src_col, key_col)):
                dve.wait_ge(S_["turned"], i + 1)
                V.tensor_copy(c, bank[4][:, 0:CROWS]).then_inc(S_["turned_used"], 1)
            dve.wait_ge(S_["turned_used"], 2)

            dve.wait_ge(S_["range_done"], 1)
            q = slice(0, NWIN)
            link(V.tensor_scalar(touch[0][q, :], bank[5][q, 0:CROWS], win_edge[q, 1:2], None, ALU.is_lt))
            link(V.scalar_tensor_tensor(touch[1][q, :], bank[6][q, 0:CROWS], win_edge[q, 0:1], touch[0][q, :],
                                        ALU.is_ge, ALU.mult))
            V.tensor_tensor(touch[0][q, :], touch[1][q, :], chunk_up[q, :], ALU.mult)
            link(V.tensor_tensor(touch2[q, :], touch[1][q, :], chunk_down[q, :], ALU.mult))
            V.tensor_reduce(bcol[q, 0:1], touch[0][q, :], AX_X, ALU.max)
            link(V.tensor_reduce(bcol[q, 1:2], touch2[q, :], AX_X, ALU.max))
            dve.wait_ge(S_["ranges_in"], 16)
            link(V.tensor_tensor(badc[q, :], bcol[q, :], rng_sb[q, :], ALU.is_gt))
            V.tensor_tensor(badc[q, 0:1], badc[q, 0:1], badc[q, 1:2], ALU.add).then_inc(S_["range_cols"], 1)
            dve.wait_ge(S_["flag_sum"], 1)
            V.tensor_copy(flag_i[0:1, 0:1], bank[5][0:1, 400:401]).then_inc(S_["flag_set"], 1)
            dve.wait_ge(S_["flag_set"], 1)

            def scale_source(g, link):
                dve.wait_ge(S_["sdeg_done"], g + 1)
                V.tensor_scalar(sdeg[:, g:g + 1], sdeg[:, g:g + 1], 1.0, None, ALU.max)
                link(V.tensor_scalar(degv[:, g:g + 1], degv[:, g:g + 1], 1.0, None, ALU.max))
                invert_root(sdeg[:, g:g + 1], degv[:, g:g + 1], isd[:, g:g + 1], ntmp, link)
                link(V.scalar_tensor_tensor(xscale[:, g:g + 1], isd[:, g:g + 1], X_SCALE, rstd2[:, g:g + 1],
                                            ALU.mult, ALU.mult))
                V.tensor_tensor(xbias[:, g:g + 1], xscale[:, g:g + 1], nmean[:, g:g + 1], ALU.mult)\
                    .then_inc(S_["isd_done"], 1)

            def source_lo(g):
                m = rows(g, N)
                dve.wait_ge(S_["xhi_made"], g + 1)
                V.tensor_tensor(xs_lo[0:m, g, :], x_raw[0:m, g, :], xs_hi[0:m, g, :], ALU.subtract)\
                    .then_inc(S_["xlo_made"], 1)

            def invert_root(root, square, out, tmp, link):
                link(V.reciprocal(out, root))
                link(V.tensor_tensor(tmp, out, out, ALU.mult))
                link(V.tensor_tensor(tmp, tmp, square, ALU.mult))
                link(V.tensor_scalar(tmp, tmp, -0.5, 1.5, ALU.mult, ALU.add))
                link(V.tensor_tensor(out, out, tmp, ALU.mult))

            def invert_std(link):
                dve.wait_ge(S_["x_std"], 1)
                link(V.tensor_scalar(xss, xss, 1.0 / D, 1e-5, ALU.mult, ALU.add))
                invert_root(rstd, xss, rstd2, xsum, link)

            def short_path():
                link = Link(dve, "link_fast")
                n = 0
                for w, (a, b) in enumerate(RANGES):
                    for c in range(a, b):
                        if n % KG == 0 and n >= KRING:
                            dve.wait_ge(S_["key_used"], (n - KRING) // KG + 1)
                        ins = V.tensor_scalar(key_hot[:, n % KRING, :], iota16[:], float(KEYS * w),
                                              key_col[:, c:c + 1], ALU.add, ALU.is_equal)
                        if n % KG == KG - 1 or n == NSTEPS - 1:
                            ins.then_inc(S_["key_made"], 1)
                        n += 1
                    if w == 13:
                        invert_std(link)
                    for g in SCALE_AT.get(w, ()):
                        scale_source(g, link)
                    for g in LO_AT.get(w, ()):
                        source_lo(g)
                for g in SCALE_AT[NWIN]:
                    scale_source(g, link)
                    if g >= 1 and g - 1 in LO_AT[NWIN]:
                        source_lo(g - 1)
                source_lo(NT - 1)

            def long_path():
                link = Link(dve, "link_slow")
                with dve.Fori(0, NWIN) as w:
                    with dve.Fori(0, NCH) as c:
                        dve.wait_ge(S_["slow_used"], w * NCH + c + 1)
                        V.tensor_scalar(src_hot[:, 0, :], iota16[:, 0:P], src_col[:, bass.ds(c, 1)], None, ALU.is_equal)
                        V.tensor_scalar(key_hot[:, 0, :], iota16[:], win_key[:, bass.ds(w, 1)],
                                        key_col[:, bass.ds(c, 1)], ALU.add, ALU.is_equal)\
                            .then_inc(S_["slow_made"], 1)
                invert_std(link)
                for g in range(NT):
                    scale_source(g, link)
                for g in range(NT):
                    source_lo(g)

            bad = dve.value_load(flag_i[0:1, 0:1], min_val=0, max_val=2 * NWIN)
            with dve.If(bad == 0):
                short_path()
            with dve.Else():
                long_path()

            link(V.tensor_scalar(xss, sdeg, 45.0, None, ALU.is_gt))
            V.tensor_reduce(bigc[:, 0:1], xss, AX_X, ALU.max).then_inc(S_["big_col"], 1)
            for j in range(3):
                if j == 2:
                    dve.wait_ge(S_["bcast_made"], 1)
                for i in range(4 * j, min(4 * j + 4, NT)):
                    ins = V.tensor_scalar(val[:, j % 2, (i % 4) * P:(i % 4 + 1) * P], ident[:], isd[:, i:i + 1],
                                          None, ALU.mult)
                ins.then_inc(S_["diag_made"], 1)
                if j == 0:
                    dve.wait_ge(S_["big_sum"], 1)
                    V.tensor_copy(flag_i[0:1, 1:2], bank[6][0:1, 0:1]).then_inc(S_["big_set"], 1)

            def pow2(cs, link):
                link(V.tensor_scalar(bound[:, cs], bound[:, cs], 1e-30, None, ALU.max))
                link(V.tensor_scalar(ipw.bitcast(I32)[:, cs], bound.bitcast(I32)[:, cs], 0x7F800000, None,
                                     ALU.bitwise_and))
                link(V.tensor_scalar(pw.bitcast(I32)[:, cs], ipw.bitcast(I32)[:, cs], -1.0, float(268 << 23),
                                     ALU.mult, ALU.add))
                link(V.tensor_scalar(ipw.bitcast(I32)[:, cs], ipw.bitcast(I32)[:, cs], float(-(14 << 23)), None,
                                     ALU.add))

            def split_lo(i):
                kind, a, k, c0, n = loads[i]
                m = rows(k, nrows[a])
                dve.wait_ge(S_["stage_hi"], i + 1 - squares[i + 1])
                hi, lo, p = places(a, k, c0)
                src = stage[0:m, i % 2, 0:n]
                if a == "W1":
                    src = src.rearrange("p (s n) -> p s n", n=P)
                V.scalar_tensor_tensor(lo[0:m], src, pw[0:m, p:p + 1], hi[0:m], ALU.mult, ALU.subtract)\
                    .then_inc(S_["stage_lo"], 1)

            def norms_ready(n):
                dve.wait_ge(S_["norm_done"], n)

            def t1_val(i):
                f, (n0, n) = i // 3, DSPLIT[i % 3]
                if i % 3 == 0:
                    dve.wait_ge(S_["t1_mm"], f + 1)
                if i == 0:
                    dve.wait_ge(S_["bcast_used"], 3)
                if i >= 2:
                    dve.wait_ge(S_["t1_lo"], i - 1)
                V.tensor_tensor(val[:, i % 2, 0:n], bank[3 * (f % 2) + i % 3][:, 0:n], row_bc[:, n0:n0 + n], ALU.mult)\
                    .then_inc(S_["t1_val"], 1)

            def t1_lo(i):
                f, (n0, n) = i // 3, DSPLIT[i % 3]
                dve.wait_ge(S_["t1_hi"], i + 1)
                V.tensor_tensor(t1T[1][:, f, n0:n0 + n], val[:, i % 2, 0:n], t1T[0][:, f, n0:n0 + n], ALU.subtract)\
                    .then_inc(S_["t1_lo"], 1)

            n1 = [i for i, l in enumerate(loads) if l[0] == "split" and l[1] == "W1"]
            for f in range(FT):
                for j in range(3):
                    i = 3 * f + j
                    t1_val(i)
                    if i >= 1:
                        t1_lo(i - 1)
                if f == 1:
                    norms_ready(1)
                    link(V.tensor_copy(bound[:, 0:1], norms[:, W1_:W1_ + 1]))
                    pow2(slice(0, 1), link)
                    V.tensor_copy(coef[:, 4:5], coef[:, 4:5]).then_inc(S_["w1_scaled"], 1)
                for i in W1_AT.get(f, ()):
                    split_lo(n1[i])
            t1_lo(3 * FT - 1)

            norms_ready(2)
            link(V.tensor_tensor(bound[:, H_:H_ + 1], norms[:, T1_:T1_ + 1], norms[:, W1_:W1_ + 1], ALU.mult))
            link(V.scalar_tensor_tensor(bound[:, H_:H_ + 1], bound[:, H_:H_ + 1], 1.0 / T1_SCALE,
                                        norms[:, B1_:B1_ + 1], ALU.mult, ALU.add))
            pow2(slice(H_, H_ + 1), link)
            link(V.scalar_tensor_tensor(coef[:, C_H:C_H + 1], ipw[:, W1_:W1_ + 1], 1.0 / T1_SCALE, pw[:, H_:H_ + 1],
                                        ALU.mult, ALU.mult))
            V.tensor_scalar(b1s, b1c, pw[:, H_:H_ + 1], None, ALU.mult).then_inc(S_["h_coef"], 1)
            n2 = [i for i, l in enumerate(loads) if l[0] == "split" and l[1] == "W2"]
            for mt in range(MT):
                m = rows(mt, MID)
                for j in range(3):
                    i, (n0, n) = 3 * mt + j, DSPLIT[j]
                    dve.wait_ge(S_["h_hi"], i + 1)
                    V.tensor_tensor(hT[1][0:m, mt, n0:n0 + n], val[0:m, i % 2, 0:n], hT[0][0:m, mt, n0:n0 + n],
                                    ALU.subtract).then_inc(S_["h_lo"], 1)
                if mt == 6:
                    norms_ready(3)
                    link(V.tensor_copy(bound[:, W2_:W2_ + 1], norms[:, W2_:W2_ + 1]))
                    pow2(slice(W2_, W2_ + 1), link)
                    V.tensor_copy(coef[:, 5:6], coef[:, 5:6]).then_inc(S_["w2_scaled"], 1)
                for k in W2_AT.get(mt, ()):
                    split_lo(n2[k])

            norms_ready(4)
            zc = slice(Z_, Z_ + 1)
            link(V.scalar_tensor_tensor(bound[:, zc], norms[:, H_:H_ + 1], ipw[:, H_:H_ + 1], norms[:, W2_:W2_ + 1],
                                        ALU.mult, ALU.mult))
            pow2(zc, link)
            link(V.tensor_tensor(coef[:, 6:7], ipw[:, H_:H_ + 1], ipw[:, W2_:W2_ + 1], ALU.mult))
            link(V.tensor_tensor(coef[:, 6:7], coef[:, 6:7], pw[:, zc], ALU.mult))
            V.tensor_scalar(zcoef, isd, coef[:, 6:7], None, ALU.mult).then_inc(S_["z_coef"], 1)
            link(V.tensor_scalar(ocoef, isd, ipw[:, zc], None, ALU.mult))
            for t in range(NT):
                m = rows(t, N)
                for j in range(2):
                    i = 2 * t + j
                    dve.wait_ge(S_["z_hi"], i + 1)
                    V.tensor_tensor(z[1][0:m, t, j * 512:(j + 1) * 512], val[0:m, i % 2, :],
                                    z[0][0:m, t, j * 512:(j + 1) * 512], ALU.subtract).then_inc(S_["z_lo"], 1)
            norms_ready(5)
            link(V.tensor_copy(bound[:, PD_:WW_ + 1], norms[:, PD_:WW_ + 1]))
            link(V.tensor_scalar(bound[:, G_:G_ + 1], norms[:, PD_:PD_ + 1], 32.0, None, ALU.mult))
            pow2(slice(G_, G_ + 1), link)
            pow2(slice(PD_, WW_ + 1), link)
            V.tensor_scalar(coef[:, C_P:C_P + 1], ipw[:, PD_:PD_ + 1], 1.0 / X_SCALE, None, ALU.mult)
            V.tensor_scalar(coef[:, C_B:C_B + 1], ipw[:, WW_:WW_ + 1], 1.0 / X_SCALE, None, ALU.mult)\
                .then_inc(S_["f_coef"], 1)

            def x2_tile(t):
                m = rows(t, N)
                dve.wait_ge(S_["o_mm"], t + 1)
                dve.wait_ge(S_["x2_b"], t + 1)
                for j in range(2):
                    o = x2[0:m, t, j * 512:(j + 1) * 512]
                    ins = V.scalar_tensor_tensor(o, bank[2 * (t % 3) + j][0:m, :], ocoef[0:m, t:t + 1], o,
                                                 ALU.mult, ALU.add)
                    if j == 1:
                        ins.then_inc(S_["x2_done"], 1)
                dve.wait_ge(S_["x2_done"], t + 1)
                for j in range(2):
                    ins = V.bn_stats(stats[0:m, 6 * j:6 * j + 6], x2[0:m, t, j * 512:(j + 1) * 512])
                link(ins)
                V.bn_aggr(mv[0:m, :], stats[0:m, :].rearrange("p (a b) -> p a b", a=2)).then_inc(S_["ln_var"], 1)
                dve.wait_ge(S_["ln_std"], t + 1)
                link(V.tensor_scalar(mv[0:m, 1:2], mv[0:m, 1:2], 1e-5, None, ALU.add))
                invert_root(lnr[0:m, 0:1], mv[0:m, 1:2], lnr[0:m, 1:2], ntmp[0:m, :], link)
                link(V.tensor_scalar(lnr[0:m, 2:3], lnr[0:m, 1:2], X_SCALE, None, ALU.mult))
                V.scalar_tensor_tensor(lnr[0:m, 3:4], mv[0:m, 0:1], -1.0, lnr[0:m, 2:3], ALU.mult, ALU.mult)\
                    .then_inc(S_["ln_coef"], 1)

            def yT_lo_tile(t):
                m = rows(t, N)
                for j in range(2):
                    dve.wait_ge(S_["yt_hi"], 2 * t + j + 1)
                    V.tensor_tensor(yT_lo[:, 4 * j:4 * j + 4, t * P:t * P + m],
                                    bank[6 + j][:, :].rearrange("p (k d) -> p k d", k=4)[:, :, 0:m],
                                    yT_hi[:, 4 * j:4 * j + 4, t * P:t * P + m], ALU.subtract)\
                        .then_inc(S_["yt_lo"], 1)

            npd = [i for i, l in enumerate(loads) if l[0] == "split" and l[1] == "Wpd"]
            for t in range(NT):
                x2_tile(t)
                if t >= 1:
                    yT_lo_tile(t - 1)
                if t < 4:
                    for k in (2 * t, 2 * t + 1):
                        split_lo(npd[k])
                if t == 5:
                    dve.wait_ge(S_["sim_norm"], 1)
                    link(V.tensor_scalar(simss, simr, 1e-12, None, ALU.max))
                    link(V.reciprocal(simss, simss))
                    for e in range(NEXP):
                        ins = V.tensor_scalar(sim_bc[:, e, :], sim_bc[:, e, :], simss[:, e:e + 1], None, ALU.mult)
                    link(ins)
                    link(V.tensor_scalar(tempv, temp_c, CLAMP_MAX, None, ALU.min))
            yT_lo_tile(NT - 1)

            dve.wait_ge(S_["o_mm"], NT)
            V.memset(down[:, NT - 1, :], 0.0)
            nw = [i for i, l in enumerate(loads) if l[0] == "split" and l[1] == "W"]
            for t in range(NT):
                m = rows(t, N)
                b = bank[(t + 2) % 6]
                dve.wait_ge(S_["p_mm"], t + 1)
                if t >= 2:
                    dve.wait_ge(S_["p_sq"], t - 1)
                V.scalar_tensor_tensor(pr[t % 2][0:m, :], b[0:m, 0:PROJ], coef[0:m, C_P:C_P + 1], bp_bc[0:m, :],
                                       ALU.mult, ALU.add).then_inc(S_["p_val"], 1)
                V.tensor_scalar(down[0:m, t, :], b[0:m, PROJ:PD], coef[0:m, C_P:C_P + 1], None, ALU.mult)\
                    .then_inc(S_["p_used"], 1)
                dve.wait_ge(S_["p_val"], t + 1)
                for e in range(NEXP):
                    V.tensor_tensor_reduce(out=scratch[0:m, :], in0=pr[t % 2][0:m, :], in1=sim_bc[0:m, e, :],
                                           scale=1.0, scalar=0.0, op0=ALU.mult, op1=ALU.add,
                                           accum_out=dots[0:m, t, e:e + 1]).then_inc(S_["dots_made"], 1)
                    dve.wait_ge(S_["dots_made"], NEXP * t + e + 1)
                if t < FT:
                    split_lo(nw[t])

            dve.wait_ge(S_["dots_made"], NT * NEXP)
            dve.wait_ge(S_["p_norm"], 1)

            def each(v):
                return v.unsqueeze(2).to_broadcast([P, NT, NEXP])

            link(V.tensor_scalar(pnorm, pnorm, 1e-12, None, ALU.max))
            link(V.reciprocal(pscale, pnorm))
            dve.wait_ge(S_["temp_exp"], 1)
            link(V.tensor_tensor(logit, dots, each(pscale), ALU.mult))
            link(V.tensor_scalar(logit, logit, tempe, None, ALU.mult))
            link(V.tensor_reduce(gmax, logit, AX_X, ALU.max))
            V.tensor_tensor(logit, logit, each(gmax), ALU.subtract).then_inc(S_["exp_in"], 1)
            dve.wait_ge(S_["exp_out"], 1)
            link(V.tensor_reduce(gsum, ex, AX_X, ALU.add))
            link(V.reciprocal(gsum, gsum))
            link(V.tensor_tensor(prob, ex, each(gsum), ALU.mult))
            link(V.tensor_reduce(gmax, prob, AX_X, ALU.max))
            link(V.tensor_tensor(hit, prob, each(gmax), ALU.is_equal))
            link(V.memset(keep, 1.0))
            for e in range(1, NEXP):
                link(V.tensor_tensor(keep[:, :, e], keep[:, :, e - 1], hit[:, :, e - 1], ALU.is_gt))
            link(V.tensor_tensor(pick, hit, keep, ALU.mult))
            link(V.tensor_tensor(pick, pick, prob, ALU.mult))
            link(V.tensor_scalar(pick, pick, pw[:, G_:G_ + 1], None, ALU.mult))
            r0 = 0
            for e, r in enumerate(RANKS):
                ins = V.tensor_tensor(gated[:, :, r0:r0 + r], down[:, :, r0:r0 + r],
                                      pick[:, :, e:e + 1].to_broadcast([P, NT, r]), ALU.mult)
                r0 += r
            link(ins)
            dve.wait_ge(S_["link_p"], 2)
            V.tensor_copy(g_rows[:, :, 32:32 + R], gated)
            link(V.tensor_copy(g_rows[:, :, 0:R], gated))
            V.tensor_tensor(g_rows[:, :, 64:64 + R], gated, g_rows[:, :, 0:R], ALU.subtract).then_inc(S_["g_made"], 1)
            norms_ready(6)
            link(V.tensor_copy(bound[:, WU_:WU_ + 1], norms[:, WU_:WU_ + 1]))
            pow2(slice(WU_, WU_ + 1), link)
            link(V.tensor_tensor(coef[:, C_L:C_L + 1], ipw[:, WU_:WU_ + 1], ipw[:, G_:G_ + 1], ALU.mult))
            link(V.tensor_scalar(wu_raw[0:GP, :], wu_raw[0:GP, :], pw[0:GP, WU_:WU_ + 1], None, ALU.mult))
            link(V.tensor_copy(wu[0:GP, :], wu_raw[0:GP, :]))
            V.tensor_tensor(wu[32:64, :], wu_raw[32:64, :], wu[32:64, :], ALU.subtract).then_inc(S_["wu_done"], 1)
            dve.wait_ge(S_["gt_mm"], 1)
            for j in range(2):
                ins = V.tensor_copy(gT[0:GP, 5 * j:5 * j + 5, :],
                                    bank[6 + j][:, :].bitcast(F16)[0:GP, 0:5 * P].rearrange("p (t d) -> p t d", t=5))
            ins.then_inc(S_["gt_made"], 1)

            for t in range(NT):
                m = rows(t, N)
                dve.wait_ge(S_["b_mm"], t + 1)
                if t >= 2:
                    dve.wait_ge(out_done[t % 2], 16 * (t // 2))
                q = 4 * (t % 2)
                for j in range(2):
                    V.scalar_tensor_tensor(res[t % 2][0:m, j * 512:(j + 1) * 512], bank[q + j][0:m, :],
                                           coef[0:m, C_B:C_B + 1], x2[0:m, t, j * 512:(j + 1) * 512],
                                           ALU.mult, ALU.add).then_inc(S_["res_half"], 1)
                dve.wait_ge(S_["res_half"], 2 * t + 2)
                for j in range(2):
                    o = res[t % 2][0:m, j * 512:(j + 1) * 512]
                    ins = V.scalar_tensor_tensor(o, bank[q + 2 + j][0:m, :], coef[0:m, C_L:C_L + 1], o,
                                                 ALU.mult, ALU.add)
                ins.then_inc(S_["res_made"], 1)

        @block.scalar
        def _(act):
            A = nc.scalar.activation
            link = Link(act, "link_a")
            last_note = [None]

            def note_free():
                if last_note[0]:
                    act.wait_ge(S_[last_note[0][0]], last_note[0][1])

            def noted(name, value):
                last_note[0] = (name, value)

            def x_stats(t, link):
                m = rows(t, N)
                act.wait_ge(x_in[t], 16)
                if t == 0:
                    act.wait_ge(S_["consts"], NCONST)
                link(A(junk[0:m, :], x_raw[0:m, t, :], ACT.Copy, accum_out=xsum[0:m, t:t + 1]))
                link(A(nmean[0:m, t:t + 1], xsum[0:m, t:t + 1], ACT.Copy, scale=-1.0 / D))
                link(A(junk[0:m, :], x_raw[0:m, t, :], ACT.Square, bias=nmean[0:m, t:t + 1],
                       accum_out=xss[0:m, t:t + 1]))

            def x_std():
                A(rstd, xss, ACT.Sqrt, bias=eps_c, scale=1.0 / D).then_inc(S_["x_std"], 1)

            def square(i):
                kind, a, k, c0, n = loads[i]
                m = rows(k, nrows[a])
                ss = {"W1": w1_ss, "W2": w2_ss, "W": w_ss, "Wpd": wpd_ss}[a]
                q = 2 * k + c0 // HALF if a == "W1" else k
                act.wait_ge(stage_in[i % 2], 16 * (i // 2 + 1))
                note_free()
                A(junk[0:m, 0:n], stage[0:m, i % 2, 0:n], ACT.Square, accum_out=ss[0:m, q:q + 1])\
                    .then_inc(S_["stage_sq"], 1)
                noted("stage_sq", squares[i + 1])

            def add_up(q, v):
                note_free()
                last_note[0] = None
                return A(junk[:, 0:v.shape[1]], v, ACT.Copy, accum_out=sums[:, q:q + 1])

            def norm(n, q0, q1):
                act.wait_ge(S_["norm_sum"], n)
                A(norms[:, q0:q1], bank[7][:, 0:q1 - q0], ACT.Sqrt).then_inc(S_["norm_done"], 1)

            def split_hi(i):
                kind, a, k, c0, n = loads[i]
                m = rows(k, nrows[a])
                act.wait_ge(stage_in[i % 2], 16 * (i // 2 + 1))
                hi, lo, p = places(a, k, c0)
                src = stage[0:m, i % 2, 0:n]
                if a == "W1":
                    src = src.rearrange("p (s n) -> p s n", n=P)
                A(hi[0:m], src, ACT.Copy, scale=pw[0:m, p:p + 1]).then_inc(S_["stage_hi"], 1)

            def degree_root(g):
                act.wait_ge(S_["deg_done"], g + 1)
                A(degv[:, g:g + 1], bank[7][:, g:g + 1], ACT.Copy)
                A(sdeg[:, g:g + 1], bank[7][:, g:g + 1], ACT.Sqrt).then_inc(S_["sdeg_done"], 1)

            def source(g, link):
                m = rows(g, N)
                act.wait_ge(S_["isd_done"], g + 1)
                link(A(x_raw[0:m, g, :], x_raw[0:m, g, :], ACT.Identity, bias=xbias[0:m, g:g + 1],
                       scale=xscale[0:m, g:g + 1]))
                A(xs_hi[0:m, g, :], x_raw[0:m, g, :], ACT.Copy).then_inc(S_["xhi_made"], 1)

            def take(w, j=None):
                act.wait_ge(S_["win_done"], w + 1)
                b = bank[w % WPT if j is None else j]
                A(adj[:, :, bass.ds(w * W, W)], b[:, 0:KEYS].rearrange("p (t d) -> p t d", t=NT), ACT.Copy)\
                    .then_inc(S_["adj_made"], 1)

            def take_rest(w, j=None):
                act.wait_ge(S_["sub_done"], w + 1)
                b = bank[w % WPT if j is None else j]
                A(adj_rest[:, :, bass.ds(w * W, W)], b[:, 0:KEYS].rearrange("p (t d) -> p t d", t=NT), ACT.Copy)\
                    .then_inc(S_["rest_made"], 1)

            act.wait_ge(S_["flag_set"], 1)
            bad = act.value_load(flag_i[0:1, 0:1], min_val=0, max_val=2 * NWIN)
            with act.If(bad == 0):
                flink = Link(act, "link_fast_a")

                def source_hots(g):
                    n = min(SG, NCH - SG * g)
                    if g * SG >= SRING:
                        last = max(LAST_STEP[c] for c in range(SG * g - SRING, SG * g - SRING + n))
                        act.wait_ge(S_["key_used"], last // KG + 1)
                    act.wait_ge(S_["score_made"], g + 1)
                    q = SG * g % SRING
                    A(src_hot[:, q:q + n, :].rearrange("p s n -> p (s n)"), bank[5 + g % 2][:, 0:n * P], ACT.Relu)\
                        .then_inc(S_["src_made"], 1)

                step = 0
                for w in range(NWIN):
                    for n in range(step, step + RANGES[w][1] - RANGES[w][0]):
                        for g in ISSUE.get(n, ()):
                            source_hots(g)
                    step += RANGES[w][1] - RANGES[w][0]
                    take(w)
                    if w >= 1:
                        take_rest(w - 1)
                    if w < NT:
                        x_stats(w, flink)
                    if w == NT:
                        x_std()
                    for i in SQ_AT.get(w, ()):
                        square(i)
                    for g in ROOT_AT.get(w, ()):
                        degree_root(g)
                    for g in SOURCE_AT.get(w, ()):
                        source(g, flink)
                take_rest(NWIN - 1)
                for g in ROOT_AT[NWIN]:
                    degree_root(g)
                for g in SOURCE_AT[NWIN]:
                    source(g, flink)
                note_free()
            with act.Else():
                last_note[0] = None
                slink = Link(act, "link_slow_a")
                with act.Fori(0, NT) as g:
                    for j in range(WPT):
                        take(WPT * g + j, j)
                        take_rest(WPT * g + j, j)
                for t in range(NT):
                    x_stats(t, slink)
                x_std()
                for i in range(SQ_A):
                    square(i)
                for g in range(NT):
                    degree_root(g)
                for g in range(NT):
                    source(g, slink)

                note_free()
            last_note[0] = None

            for j in range(3):
                act.wait_ge(S_["bcast_made"], j + 1)
                n = min(512, NT * P - 512 * j)
                A(row_bc[:, 512 * j:512 * j + n], bank[6 + j % 2][:, 0:n], ACT.Copy, scale=T1_SCALE / X_SCALE)\
                    .then_inc(S_["bcast_used"], 1)
            for i in range(SQ_A, 2 * FT):
                square(i)
            link(add_up(W1_, w1_ss))
            act.wait_ge(S_["b1_in"], 16)
            A(junk[:, 0:MT], b1c, ACT.Square, accum_out=sums[:, B1_:B1_ + 1]).then_inc(S_["norm_in"], 1)
            noted("norm_in", 1)

            n1 = [i for i, l in enumerate(loads) if l[0] == "split" and l[1] == "W1"]
            for f in range(FT):
                for j in range(3):
                    i, (n0, n) = 3 * f + j, DSPLIT[j]
                    act.wait_ge(S_["t1_val"], i + 1)
                    A(t1T[0][:, f, n0:n0 + n], val[:, i % 2, 0:n], ACT.Copy).then_inc(S_["t1_hi"], 1)
                    act.wait_ge(S_["t1_hi"], i + 1)
                    note_free()
                    A(junk[:, 0:n], t1T[0][:, f, n0:n0 + n], ACT.Square, accum_out=t1_ss[:, i:i + 1])\
                        .then_inc(S_["t1_sq"], 1)
                    noted("t1_sq", i + 1)
                if f == 1:
                    norm(1, W1_, B1_ + 1)
                    act.wait_ge(S_["w1_scaled"], 1)
                for i in W1_AT.get(f, ()):
                    split_hi(n1[i])
            act.wait_ge(S_["t1_sq"], 3 * FT)
            add_up(T1_, t1_ss).then_inc(S_["norm_in"], 1)
            noted("norm_in", 2)
            norm(2, T1_, T1_ + 1)
            act.wait_ge(S_["h_coef"], 1)

            n2 = [i for i, l in enumerate(loads) if l[0] == "split" and l[1] == "W2"]
            s2 = [i for i, l in enumerate(loads) if l[0] == "sq" and l[1] == "W2"]
            for mt in range(MT):
                m = rows(mt, MID)
                act.wait_ge(S_["h_mm"], mt + 1)
                if mt == 0:
                    act.wait_ge(S_["t1_lo"], 3 * FT)
                    act.wait_ge(S_["spilled"], 16)
                for j in range(3):
                    i, (n0, n) = 3 * mt + j, DSPLIT[j]
                    if i >= 2:
                        act.wait_ge(S_["h_lo"], i - 1)
                    A(val[0:m, i % 2, 0:n], bank[3 * (mt % 2) + j][0:m, 0:n], ACT.Relu, bias=b1s[0:m, mt:mt + 1],
                      scale=coef[0:m, C_H:C_H + 1]).then_inc(S_["h_val"], 1)
                    act.wait_ge(S_["h_val"], i + 1)
                    A(hT[0][0:m, mt, n0:n0 + n], val[0:m, i % 2, 0:n], ACT.Copy).then_inc(S_["h_hi"], 1)
                    act.wait_ge(S_["h_hi"], i + 1)
                    note_free()
                    A(junk[0:m, 0:n], hT[0][0:m, mt, n0:n0 + n], ACT.Square, accum_out=h_ss[0:m, i:i + 1])\
                        .then_inc(S_["h_sq"], 1)
                    noted("h_sq", i + 1)
                if mt < 6:
                    for k in (2 * mt, 2 * mt + 1):
                        square(s2[k])
                if mt == 5:
                    act.wait_ge(S_["stage_sq"], squares[s2[-1] + 1])
                    add_up(W2_, w2_ss).then_inc(S_["norm_in"], 1)
                    noted("norm_in", 3)
                if mt == 6:
                    norm(3, W2_, W2_ + 1)
                    act.wait_ge(S_["w2_scaled"], 1)
                for k in W2_AT.get(mt, ()):
                    act.wait_ge(S_["h_mm"], k)
                    split_hi(n2[k])
            act.wait_ge(S_["h_sq"], 3 * MT)
            add_up(H_, h_ss).then_inc(S_["norm_in"], 1)
            noted("norm_in", 4)
            norm(4, H_, H_ + 1)
            act.wait_ge(S_["z_coef"], 1)

            spd = [i for i, l in enumerate(loads) if l[0] == "sq" and l[1] == "Wpd"]
            sw = [i for i, l in enumerate(loads) if l[0] == "sq" and l[1] == "W"]
            for t in range(NT):
                m = rows(t, N)
                act.wait_ge(S_["z_mm"], t + 1)
                if t == 0:
                    act.wait_ge(S_["h_lo"], 3 * MT)
                for j in range(2):
                    i = 2 * t + j
                    if i >= 2:
                        act.wait_ge(S_["z_lo"], i - 1)
                    A(val[0:m, i % 2, :], bank[2 * (t % 3) + j][0:m, :], ACT.Copy, scale=zcoef[0:m, t:t + 1])\
                        .then_inc(S_["z_val"], 1)
                    act.wait_ge(S_["z_val"], i + 1)
                    A(z[0][0:m, t, j * 512:(j + 1) * 512], val[0:m, i % 2, :], ACT.Copy).then_inc(S_["z_hi"], 1)
                if t < 4:
                    for k in (2 * t, 2 * t + 1):
                        square(spd[k])
                for k in {4: (0, 1, 2), 5: (3, 4, 5), 6: (6, 7)}.get(t, ()):
                    square(sw[k])
                if t == 6:
                    act.wait_ge(S_["stage_sq"], squares[-1])
                    link(add_up(PD_, wpd_ss))
                    add_up(WW_, w_ss).then_inc(S_["norm_in"], 1)
                    noted("norm_in", 5)
            norm(5, PD_, WW_ + 1)
            act.wait_ge(S_["f_coef"], 1)

            def yT_hi_tile(t):
                m = rows(t, N)
                for j in range(2):
                    act.wait_ge(S_["yt_mm"], 2 * t + j + 1)
                    A(yT_hi[:, 4 * j:4 * j + 4, t * P:t * P + m],
                      bank[6 + j][:, :].rearrange("p (k d) -> p k d", k=4)[:, :, 0:m], ACT.Copy)\
                        .then_inc(S_["yt_hi"], 1)

            npd = [i for i, l in enumerate(loads) if l[0] == "split" and l[1] == "Wpd"]
            for t in range(NT):
                m = rows(t, N)
                act.wait_ge(S_["ln_var"], t + 1)
                A(lnr[0:m, 0:1], mv[0:m, 1:2], ACT.Sqrt, bias=eps_c[0:m, :]).then_inc(S_["ln_std"], 1)
                act.wait_ge(S_["ln_coef"], t + 1)
                if t == 0:
                    act.wait_ge(S_["z_lo"], 2 * NT)
                else:
                    act.wait_ge(S_["yt_mm"], 2 * t)
                A(val[0:m, :, :].rearrange("p a b -> p (a b)"), x2[0:m, t, :], ACT.Identity, bias=lnr[0:m, 3:4],
                  scale=lnr[0:m, 2:3]).then_inc(S_["y_made"], 1)
                if t >= 1:
                    yT_hi_tile(t - 1)
                if t < 4:
                    for k in (2 * t, 2 * t + 1):
                        split_hi(npd[k])
                if t == 4:
                    act.wait_ge(S_["sim_in"], 48)
                    note_free()
                    for e in range(NEXP):
                        link(A(junk[:, 0:PROJ], sim_bc[:, e, :], ACT.Square, accum_out=simss[:, e:e + 1]))
                    last_note[0] = None
                    A(simr, simss, ACT.Sqrt).then_inc(S_["sim_norm"], 1)
            yT_hi_tile(NT - 1)

            nw = [i for i, l in enumerate(loads) if l[0] == "split" and l[1] == "W"]
            act.wait_ge(S_["o_mm"], NT)
            for t in range(NT):
                m = rows(t, N)
                act.wait_ge(S_["p_val"], t + 1)
                note_free()
                A(junk[0:m, 0:PROJ], pr[t % 2][0:m, :], ACT.Square, accum_out=pss[0:m, t:t + 1])\
                    .then_inc(S_["p_sq"], 1)
                noted("p_sq", t + 1)
                if t < FT:
                    split_hi(nw[t])
                if t == FT:
                    act.wait_ge(S_["wu_in"], 48)
                    note_free()
                    A(junk[0:R, 0:D], wu_raw[0:R, :], ACT.Square, accum_out=sums[0:R, WU_:WU_ + 1])\
                        .then_inc(S_["norm_in"], 1)
                    noted("norm_in", 6)
            norm(6, WU_, WU_ + 1)
            act.wait_ge(S_["p_sq"], NT)
            A(pnorm, pss, ACT.Sqrt).then_inc(S_["p_norm"], 1)
            A(tempe, tempv, ACT.Exp).then_inc(S_["temp_exp"], 1)
            act.wait_ge(S_["exp_in"], 1)
            A(ex, logit, ACT.Exp).then_inc(S_["exp_out"], 1)

        @block.tensor
        def _(pe):
            T = nc.tensor

            pe.wait_ge(S_["consts"], NCONST)
            pe.wait_ge(S_["chunk_ends"], 1)
            for k in range(2):
                for j in range(CG):
                    ins = T.matmul(bank[5 + k][0:NWIN, j * P:(j + 1) * P], ones16[:], diag16[:, k, j, :],
                                   start=True, stop=True)
            ins.then_inc(S_["range_done"], 1)
            pe.wait_ge(S_["keys_ready"], 1)
            for i, v in enumerate((srcf, keyf)):
                if i:
                    pe.wait_ge(S_["turned_used"], 1)
                for j in range(CG):
                    ins = T.transpose(bank[4][:, j * P:(j + 1) * P], v[:, j, :], ident[:])
                ins.then_inc(S_["turned"], 1)
            pe.wait_ge(S_["range_cols"], 1)
            T.matmul(bank[5][0:1, 400:401], badc[0:NWIN, 0:1], ones[0:NWIN, 0:1], start=True, stop=True)\
                .then_inc(S_["flag_sum"], 1)

            def close_window(j, t):
                T.matmul(bank[j][:, bass.ds(t * W, W)], ident16[:], ident16[:, j * W:(j + 1) * W],
                         start=False, stop=True, skip_group_check=True).then_inc(S_["win_done"], 1)

            def open_window(j):
                T.matmul(bank[j][:, 0:W], ident16[:], zero16[:], start=True, stop=False, skip_group_check=True)

            def subtract(w, j):
                pe.wait_ge(S_["adj_made"], w + 1)
                T.matmul(bank[j][:, 0:KEYS], minus16[:], adj[:, :, bass.ds(w * W, W)], start=False, stop=True,
                         skip_group_check=True).then_inc(S_["sub_done"], 1)

            def degrees(g):
                pe.wait_ge(S_["rest_made"], WPT * (g + 1))
                if g:
                    pe.wait_ge(S_["sdeg_done"], g)
                for i, a in enumerate((adj, adj_rest)):
                    for t in range(NT):
                        ins = T.matmul(bank[7][:, g:g + 1], a[:, t, g * P:(g + 1) * P], ones16[:, 0:1],
                                       start=(i == 0 and t == 0), stop=(i == 1 and t == NT - 1))
                ins.then_inc(S_["deg_done"], 1)

            pe.wait_ge(S_["flag_set"], 1)
            bad = pe.value_load(flag_i[0:1, 0:1], min_val=0, max_val=2 * NWIN)
            with pe.If(bad == 0):
                feat_count = [0, 0]

                def scores(g):
                    i = SG * g // FSLOT
                    if SG * g % FSLOT == 0:
                        feat_count[i % 2] += 3 * len(feature_pieces(i))
                        pe.wait_ge(feat_in[i % 2], 16 * feat_count[i % 2])
                    if g >= 2:
                        pe.wait_ge(S_["src_made"], g - 1)
                    for c in range(SG * g, min(SG * g + SG, NCH)):
                        q = c % SG * P
                        f = (c - i * FSLOT) * P
                        ins = T.matmul(bank[5 + g % 2][:, q:q + P], feat_rows[:, i % 2, f:f + P], line16[:],
                                       start=True, stop=True)
                    ins.then_inc(S_["score_made"], 1)

                pe.wait_ge(S_["line_in"], 16)
                n = 0
                for w, (a, b) in enumerate(RANGES):
                    j = w % WPT
                    if w >= WPT:
                        pe.wait_ge(S_["rest_made"], w - WPT + 1)
                    for c in range(a, b):
                        for g in ISSUE.get(n, ()):
                            scores(g)
                        if FIRST_STEP[c] == n and c % SG == 0:
                            pe.wait_ge(S_["src_made"], c // SG + 1)
                        if n % KG == 0:
                            pe.wait_ge(S_["key_made"], n // KG + 1)
                        ins = T.matmul(bank[j][:, 0:KEYS], src_hot[:, c % SRING, :], key_hot[:, n % KRING, :],
                                       start=(c == a), stop=False, skip_group_check=True)
                        if n % KG == KG - 1:
                            ins.then_inc(S_["key_used"], 1)
                        n += 1
                    close_window(j, w // WPT)
                    if w >= 1:
                        subtract(w - 1, (w - 1) % WPT)
                    for g in DEG_AT.get(w, ()):
                        degrees(g)
                subtract(NWIN - 1, (NWIN - 1) % WPT)
                for g in DEG_AT[NWIN]:
                    degrees(g)
            with pe.Else():
                pe.sem_inc(S_["slow_used"], 1)

                def slow_windows(g):
                    for j in range(WPT):
                        w = WPT * g + j
                        open_window(j)
                        with pe.Fori(0, NCH) as c:
                            pe.wait_ge(S_["slow_made"], w * NCH + c + 1)
                            T.matmul(bank[j][:, 0:KEYS], src_hot[:, 0, :], key_hot[:, 0, :], start=False, stop=True,
                                     skip_group_check=True).then_inc(S_["slow_used"], 1)
                        close_window(j, g)
                        subtract(w, j)

                slow_windows(0)
                with pe.Fori(1, NT) as g:
                    pe.wait_ge(S_["rest_made"], WPT * g)
                    slow_windows(g)
                for g in range(NT):
                    degrees(g)

            def norm_mm(n, q0, q1):
                pe.wait_ge(S_["norm_in"], n)
                if n == 1:
                    pe.wait_ge(S_["bcast_used"], 3)
                else:
                    pe.wait_ge(S_["norm_done"], n - 1)
                T.matmul(bank[7][:, 0:q1 - q0], ones[:], sums[:, q0:q1], start=True, stop=True)\
                    .then_inc(S_["norm_sum"], 1)

            def t1_group(f, t, last=False):
                m = rows(t, N)
                for p, xp in enumerate((xs_hi, xs_lo)):
                    for j, (n0, n) in enumerate(DSPLIT):
                        ins = T.matmul(bank[3 * (f % 2) + j][:, 0:n], xp[0:m, t, f * P:(f + 1) * P],
                                       adj[0:m, t, n0:n0 + n], start=(t == 0 and p == 0), stop=(last and p == 1),
                                       skip_group_check=True)
                return ins

            def t1_rest(f):
                with pe.If(big > 0):
                    for t in range(NT):
                        m = rows(t, N)
                        for xp in (xs_hi, xs_lo):
                            for j, (n0, n) in enumerate(DSPLIT):
                                T.matmul(bank[3 * (f % 2) + j][:, 0:n], xp[0:m, t, f * P:(f + 1) * P],
                                         adj_rest[0:m, t, n0:n0 + n], start=False, stop=False, skip_group_check=True)

            big = None
            for f in range(FT):
                if f == 0:
                    pe.wait_ge(S_["rest_made"], NWIN)
                if f >= 2:
                    pe.wait_ge(S_["t1_val"], 3 * (f - 1))
                for t in range(NT):
                    if f == 0:
                        pe.wait_ge(S_["xlo_made"], t + 1)
                    if t == NT - 1:
                        if f == 0:
                            pe.wait_ge(S_["big_col"], 1)
                            T.matmul(bank[6][0:1, 0:1], bigc[:, 0:1], ones[:, 0:1], start=True, stop=True)\
                                .then_inc(S_["big_sum"], 1)
                            pe.wait_ge(S_["big_set"], 1)
                            big = pe.value_load(flag_i[0:1, 1:2], min_val=0, max_val=P)
                        t1_rest(f)
                    ins = t1_group(f, t, t == NT - 1)
                ins.then_inc(S_["t1_mm"], 1)
                if f == 0:
                    for j in range(3):
                        pe.wait_ge(S_["diag_made"], j + 1)
                        if j == 2:
                            pe.wait_ge(S_["bcast_used"], 1)
                        for i in range(4 * j, min(4 * j + 4, NT)):
                            q = (i % 4) * P
                            ins = T.matmul(bank[6 + j % 2][:, q:q + P], ones[:], val[:, j % 2, q:q + P],
                                           start=True, stop=True)
                        ins.then_inc(S_["bcast_made"], 1)
                if f == 1:
                    norm_mm(1, W1_, B1_ + 1)

            for mt in range(MT):
                m = rows(mt, MID)
                if mt < 2:
                    pe.wait_ge(S_["t1_lo"], 3 * FT)
                    pe.wait_ge(S_["stage_lo"], 2 * FT)
                else:
                    pe.wait_ge(S_["h_val"], 3 * (mt - 1))
                for k in range(FT):
                    for q, (wp, tp) in enumerate(((0, 0), (0, 1), (1, 0))):
                        for j, (n0, n) in enumerate(DSPLIT):
                            ins = T.matmul(bank[3 * (mt % 2) + j][0:m, 0:n], w1_slot[mt][:, wp, k, 0:m],
                                           t1T[tp][:, k, n0:n0 + n], start=(k == 0 and q == 0),
                                           stop=(k == FT - 1 and q == 2))
                ins.then_inc(S_["h_mm"], 1)
                if mt == 0:
                    norm_mm(2, T1_, T1_ + 1)
                if mt == 6:
                    norm_mm(3, W2_, W2_ + 1)

            for t in range(NT):
                m = rows(t, N)
                if t == 0:
                    pe.wait_ge(S_["h_lo"], 3 * MT)
                if t >= 3:
                    pe.wait_ge(S_["z_val"], 2 * (t - 2))
                for k in range(MT):
                    K = rows(k, MID)
                    if t == 0:
                        pe.wait_ge(S_["stage_lo"], 2 * FT + k + 1)
                    for q, (hp, wp) in enumerate(((0, 0), (0, 1), (1, 0))):
                        for j in range(2):
                            ins = T.matmul(bank[2 * (t % 3) + j][0:m, :], hT[hp][0:K, k, t * P:t * P + m],
                                           w2_slot[k][0:K, wp, j * 512:(j + 1) * 512], start=(k == 0 and q == 0),
                                           stop=(k == MT - 1 and q == 2))
                ins.then_inc(S_["z_mm"], 1)
                if t == 0:
                    norm_mm(4, H_, H_ + 1)
                if t == 8:
                    norm_mm(5, PD_, WW_ + 1)

            def turn(t):
                m = rows(t, N)
                pe.wait_ge(S_["y_made"], t + 1)
                for j in range(2):
                    if t >= 1:
                        pe.wait_ge(S_["yt_lo"], 2 * (t - 1) + j + 1)
                    for i in range(4):
                        k = 4 * j + i
                        ins = T.transpose(bank[6 + j][:, i * P:i * P + m], val[0:m, k // 4, i * P:(i + 1) * P],
                                          ident[0:m, 0:m])
                    ins.then_inc(S_["yt_mm"], 1)

            def conv2(t, s, a, first, last):
                m, K = rows(t, N), rows(s, N)
                for p in range(2):
                    for j in range(2):
                        ins = T.matmul(bank[2 * (t % 3) + j][0:m, :], a[0:K, s, t * P:t * P + m],
                                       z[p][0:K, s, j * 512:(j + 1) * 512], start=(first and p == 0),
                                       stop=(last and p == 1), skip_group_check=True)
                return ins

            pe.wait_ge(S_["norm_done"], 5)
            for t in range(NT):
                if t < 3:
                    pe.wait_ge(S_["z_val"], 2 * (NT - 2 + min(t, 2)) if t else 2 * NT - 4)
                else:
                    pe.wait_ge(S_["x2_done"], t - 2)
                for s in range(NT):
                    if t == 0:
                        pe.wait_ge(S_["z_lo"], 2 * s + 2)
                    if s == NT - 1:
                        with pe.If(big > 0):
                            pe.wait_ge(S_["rest_in"], 16)
                            for s2 in range(NT):
                                conv2(t, s2, rest2, False, False)
                    ins = conv2(t, s, adj, s == 0, s == NT - 1)
                ins.then_inc(S_["o_mm"], 1)
                if t >= 1:
                    turn(t - 1)

            def project(t):
                m = rows(t, N)
                b = bank[(t + 2) % 6]
                pe.wait_ge(S_["x2_done"], min(NT, 8 + t // 2))
                if t >= 6:
                    pe.wait_ge(S_["p_used"], t - 5)
                pe.wait_ge(S_["yt_lo"], 2 * t + 2)
                for k in range(FT):
                    for q, (yp, wp) in enumerate(((yT_hi, wpd_hi), (yT_hi, wpd_lo), (yT_lo, wpd_hi))):
                        ins = T.matmul(b[0:m, 0:PD], yp[:, k, t * P:t * P + m], wp[:, k, :],
                                       start=(k == 0 and q == 0), stop=(k == FT - 1 and q == 2))
                ins.then_inc(S_["p_mm"], 1)

            pe.wait_ge(S_["stage_lo"], 2 * FT + MT + FT)
            for t in range(NT):
                if t == 2:
                    turn(NT - 1)
                project(t)

            for t in range(NT):
                m = rows(t, N)
                q0 = 4 * (t % 2)
                if t < 2:
                    pe.wait_ge(S_["p_used"], (8, NT)[t])
                else:
                    pe.wait_ge(S_["res_made"], t - 1)
                for k in range(FT):
                    if t == 0:
                        pe.wait_ge(S_["stage_lo"], 2 * FT + MT + FT + k + 1)
                    for q, (yp, wp) in enumerate(((yT_hi, w_hi), (yT_hi, w_lo), (yT_lo, w_hi))):
                        for j in range(2):
                            T.matmul(bank[q0 + j][0:m, :], yp[:, k, t * P:t * P + m], wp[:, k, j * 512:(j + 1) * 512],
                                     start=(k == 0 and q == 0), stop=(k == FT - 1 and q == 2))
                if t == 0:
                    norm_mm(6, WU_, WU_ + 1)
                    pe.wait_ge(S_["norm_done"], 6)
                    pe.wait_ge(S_["g_made"], 1)
                    pe.wait_ge(S_["yt_lo"], 2 * NT)
                    for i in range(NT):
                        ins = T.transpose(bank[6 + i // 5][:, :].bitcast(F16)[0:GP, (i % 5) * P:(i % 5 + 1) * P],
                                          g_rows[:, i, :], ident16[:])
                    ins.then_inc(S_["gt_mm"], 1)
                    pe.wait_ge(S_["gt_made"], 1)
                    pe.wait_ge(S_["wu_done"], 1)
                for j in range(2):
                    ins = T.matmul(bank[q0 + 2 + j][0:m, :], gT[0:GP, t, 0:m], wu[0:GP, j * 512:(j + 1) * 512],
                                   start=True, stop=True)
                ins.then_inc(S_["b_mm"], 1)


def square_line():
    l = np.arange(P)
    out = np.zeros((P, P), np.float16)
    out[0], out[1], out[2], out[3], out[4] = -16, -1, 2 * l, -(l * l // 16 * 16), 1 - l * l % 16
    return out


def kernel(**inputs):
    import concourse.bacc as _bacc
    from concourse.bass_utils import run_bass_kernel_spmd as _run

    g = {k: np.asarray(v) for k, v in inputs.items()}
    pad = CROWS * P - E
    w1 = np.zeros((D, MIDP), np.float32)
    w1[:, :MID] = g["L0_gnn_W1"]
    b1 = np.zeros(MIDP, np.float32)
    b1[:MID] = g["L0_gnn_b1"]
    arrays = {
        "x": g["x"],
        "src": np.concatenate([g["src"], np.zeros(pad, g["src"].dtype)]).reshape(CROWS, P),
        "dst": np.concatenate([g["dst"], np.full(pad, NWIN * W, g["dst"].dtype)]).reshape(CROWS, P),
        "ranges": np.array([[b, CROWS - a] for a, b in RANGES], np.float32),
        "line": square_line(),
        "W1": w1, "b1": b1.reshape(MT, P).T, "W2": g["L0_gnn_W2"], "b2": g["L0_gnn_b2"],
        "WT": g["L0_ffn_W"].T,
        "WpdT": np.concatenate([g["L0_ffn_Wp"]] + [g[f"L0_ffn_Wd{i}"] for i in range(NEXP)]).T,
        "bp": g["L0_ffn_bp"], "simT": g["L0_ffn_sim"].T, "temp": g["L0_ffn_temp"],
        "WuT": np.concatenate([g[f"L0_ffn_Wu{i}"].T for i in range(NEXP)]),
    }
    arrays = {k: np.ascontiguousarray(v) for k, v in arrays.items()}
    nc = _bacc.Bacc("TRN2", target_bir_lowering=False, num_devices=1)
    args = [nc.dram_tensor("in_" + k, v.shape, mybir.dt.from_np(v.dtype), kind="ExternalInput").ap()
            for k, v in arrays.items()]
    o = nc.dram_tensor("out", (N, D), F32, kind="ExternalOutput").ap()
    build(nc, *args, o)
    r = _run(nc, [{"in_" + k: v for k, v in arrays.items()}], core_ids=[0])
    return r.results[0]["out"]
```

```python
from contextlib import ExitStack
from math import sqrt

import numpy as np
import concourse.bass as bass
from concourse import mybir

ALU = mybir.AluOpType
ACT = mybir.ActivationFunctionType
F32 = mybir.dt.float32
F16 = mybir.dt.float16
I32 = mybir.dt.int32
AX_X = mybir.AxisListType.X

P = 128
N = 1250
D = 1024
MID = 1500
E = 40000
PROJ = 256
RANKS = (1, 2, 4, 8)
NEXP = len(RANKS)
R = sum(RANKS)
PD = PROJ + R
CLAMP_MAX = float(np.log(1.0 / 0.01))

NT = -(-N // P)
FT = D // P
MT = -(-MID // P)
W = 32
NWIN = NT * P // W
WPT = P // W
KEYS = NT * W
NCH = -(-E // P)
CG = -(-NCH // P)
CROWS = CG * P
DSPLIT = [(0, 417), (417, 417), (834, 416)]
MIDP = MT * P
HALF = MIDP // 2
GP = 96

X_SCALE = 1024.0
T1_SCALE = 8.0

KG = 4
KRING = 16
SRING = 32
SLOTS = MT + 1


def rows(t, n):
    return min(P, n - t * P)


def window_slots():
    out = []
    for w in range(NWIN):
        u0, u1 = (min(1.0, sqrt(v * W / N)) for v in (w, w + 1))
        p = u1 - u0
        out.append(int(E * p + 5 * sqrt(E * p * (1 - p)) + P - 2) // P + 1)
    return out


WSLOTS = window_slots()
WFIRST = [sum(WSLOTS[:w]) for w in range(NWIN + 1)]
NSLOT = WFIRST[NWIN]
assert NSLOT <= 512
NG = -(-NSLOT // KG)
NBLK = -(-NSLOT // P)
REST_WINS = [w for w in range(NWIN) if P * WSLOTS[w] + 1 > 2048]
REST_TILES = 1 + max(REST_WINS) // WPT
assert REST_WINS == list(range(WPT * REST_TILES))

FSLOT = 24
NF = -(-NSLOT // FSLOT)
AHEAD = 5


def feature_pieces(i):
    out, c, end = [], i * FSLOT, min((i + 1) * FSLOT, NSLOT)
    while c < end:
        n = min(end - c, P - c % P)
        out.append((c // P, c % P, n, (c - i * FSLOT) * P))
        c += n
    return out


def by_group(pairs):
    out = {NG: []}
    for group, item in pairs:
        out.setdefault(min(group, NG), []).append(item)
    return out


def tile_ends(tiles, later):
    return [(WFIRST[WPT * g + WPT + (g < REST_TILES)] // KG + later, g) for g in tiles]


ACT_STATS = 6
STATS_AT = by_group((2 + 6 * t, t) for t in range(ACT_STATS))
BN_AT = by_group((6 + 8 * (t - ACT_STATS), t) for t in range(ACT_STATS, NT))
STATS_END = 36
POOL_LO = 7
BATCHES = ((0, 2), (2, 4), (4, 6), (6, 8))
LAST = 8
DEG_AT = by_group(tile_ends(range(NT), 3))
OUT_AT = by_group(tile_ends(range(NT), 4))
VAL_AT, HI_AT = (by_group((max(STATS_END + 8, group) + 2 * (g - b0), g) for b0, b1 in BATCHES for g in range(b0, b1)
                          for group, _ in tile_ends([b1 - 1], later)) for later in (11, 10))
HI_AT[NG] += range(LAST, NT)
SQ_A = 6
SQ_GROUPS = [44 + 8 * i for i in range(SQ_A)]
SQ_AT = by_group((group, i) for i, group in enumerate(SQ_GROUPS))
LOAD_AT = {}
for i, group in enumerate(SQ_GROUPS):
    LOAD_AT.setdefault(min(NF - 1, group // (FSLOT // KG) + 2), []).append(i + 2)
SQ1_AT = {0: range(SQ_A, SQ_A + 3), 1: range(SQ_A + 3, SQ_A + 7), 2: range(SQ_A + 7, 2 * FT)}
W1_AT = {f: range(*v) for f, v in {3: (0, 2), 4: (2, 5), 5: (5, 9), 6: (9, 12), 7: (12, 16)}.items()}
W2_AT = {7: (0, 1, 2), 8: (3, 4, 5), 9: (6, 7, 8), 10: (9, 10), 11: (11,)}


def build(nc, x, src_rows, dst_rows, ranges, line, member, W1, b1, W2, b2, WT, WpdT, bp, simT, temp, WuT, out):
    with ExitStack() as ctx:
        def sb(name, shape, dt):
            return ctx.enter_context(nc.sbuf_tensor(name, shape, dt))

        def sem(name):
            return ctx.enter_context(nc.semaphore(name))

        adj = sb("adj", [P, NT, NT * P], F16)
        arena2 = sb("arena2", [P, 2 * NT * D + NT * NT * P], F16)
        arena3 = sb("arena3", [P, SLOTS * 2048], F16)
        arena4 = sb("arena4", [P, 2 * NT * D], F16)

        class Carve:
            def __init__(self, arena, size):
                self.arena, self.at, self.size = arena, 0, size

            def take(self, n, dt=F16):
                words = n * (2 if dt != F16 else 1)
                v = self.arena[:, self.at:self.at + words]
                self.at += words
                assert self.at <= self.size, (self.at, self.size)
                return v if dt == F16 else v.bitcast(dt)

        A2, A3, A4 = 2 * NT * D + NT * NT * P, SLOTS * 2048, 2 * NT * D
        pr = adj[:, :, 0:2 * PROJ].bitcast(F32)
        c = Carve(arena2, A2)
        xs_hi = c.take(NT * D).rearrange("p (t f) -> p t f", t=NT)
        xs_lo = c.take(NT * D).rearrange("p (t f) -> p t f", t=NT)
        adj_rest = c.take(NT * NT * P).rearrange("p (t d) -> p t d", t=NT)
        c = Carve(arena2, A2)
        hT = [c.take(MT * N).rearrange("p (m d) -> p m d", m=MT) for _ in range(2)]
        c = Carve(arena2, A2)
        x2 = c.take(NT * D, F32).rearrange("p (t f) -> p t f", t=NT)
        yT_hi = c.take(FT * NT * P).rearrange("p (k d) -> p k d", k=FT)
        wpd_hi = c.take(FT * PD).rearrange("p (k n) -> p k n", k=FT)
        c = Carve(arena3, A3)
        x_raw = c.take(NT * D, F32).rearrange("p (t f) -> p t f", t=NT)
        feat_rows = c.take(2 * FSLOT * P).rearrange("p (s n) -> p s n", s=2)
        slots = arena3[:, :].rearrange("p (s n) -> p s n", s=SLOTS)
        w1_slot = [slots[:, m + 1, :].rearrange("p (h k n) -> p h k n", h=2, k=FT) for m in range(MT)]
        w2_slot = [slots[:, k, :].rearrange("p (h n) -> p h n", h=2) for k in range(MT)]
        c = Carve(arena3, A3)
        yT_lo = c.take(FT * NT * P).rearrange("p (k d) -> p k d", k=FT)
        wpd_lo = c.take(FT * PD + 8)[:, 0:FT * PD].rearrange("p (k n) -> p k n", k=FT)
        at = c.at
        rest2 = c.take(NT * NT * P).rearrange("p (t d) -> p t d", t=NT)
        c.at = at
        w_hi = c.take(FT * D).rearrange("p (k n) -> p k n", k=FT)
        c = Carve(arena4, A4)
        src_hot = c.take(SRING * P).rearrange("p (s n) -> p s n", s=SRING)
        key_hot = c.take(KRING * KEYS).rearrange("p (s n) -> p s n", s=KRING)
        feat = c.take(3 * CROWS).rearrange("p (j k e) -> p j k e", j=CG, k=3)
        feat_blk = c.take(3 * NBLK * P).rearrange("p (b k e) -> p b k e", b=NBLK, k=3)
        keys = c.take(2 * CROWS).rearrange("p (h j e) -> p h j e", h=2, j=CG)
        pick_slot = c.take(CG * NSLOT).rearrange("p (j s) -> p j s", j=CG)
        member_sb = c.take(NSLOT)
        start16, ends16 = c.take(2), c.take(2 * CG).rearrange("p (k j) -> p k j", k=2)
        key_col = c.take(max(CROWS, NSLOT), F32)
        src_col = c.take(CROWS, F32)
        c = Carve(arena4, A4)
        chunk_up, chunk_down = (c.take(CROWS, F32) for _ in range(2))
        touch = [c.take(CROWS, F32) for _ in range(3)]
        src_i, dst_i, up_i, low_i, win_i, sq_i = (c.take(CROWS, I32).rearrange("p (j e) -> p j e", j=CG)
                                                  for _ in range(6))
        c = Carve(arena4, A4)
        t1T = [c.take(FT * N).rearrange("p (k d) -> p k d", k=FT) for _ in range(2)]
        c = Carve(arena4, A4)
        z = [c.take(NT * D).rearrange("p (t f) -> p t f", t=NT) for _ in range(2)]
        c = Carve(arena4, A4)
        w_lo = c.take(FT * D).rearrange("p (k n) -> p k n", k=FT)
        g_rows = c.take(NT * GP).rearrange("p (t r) -> p t r", t=NT)
        gT = c.take(NT * P).rearrange("p (t d) -> p t d", t=NT)
        res = [c.take(D, F32) for _ in range(2)]
        scratch = c.take(PROJ, F32)
        down = c.take(NT * R, F32).rearrange("p (t r) -> p t r", t=NT)
        gated = c.take(NT * R, F32).rearrange("p (t r) -> p t r", t=NT)
        wu_raw = c.take(D, F32)
        wu = c.take(D)

        stage = sb("stage", [P, 2, D], F32)
        junk = sb("junk", [P, D], mybir.dt.bfloat16)
        src_low = junk[:, 0:2 * CROWS].bitcast(I32).rearrange("p (j e) -> p j e", j=CG)
        val = sb("val", [P, 2, 512], F32)
        row_bc = sb("row_bc", [P, 1280], F32)
        sim_bc = row_bc[:, 0:D].rearrange("p (e n) -> p e n", e=NEXP)
        bp_bc = row_bc[:, D:D + PROJ]
        ident = sb("ident", [P, P], F32)
        ident16 = sb("ident16", [P, P], F16)
        minus16 = sb("minus16", [P, P], F16)
        ones = sb("ones", [P, P], F32)
        ones16 = sb("ones16", [P, NWIN], F16)
        zero16 = sb("zero16", [P, W], F16)
        iota16 = sb("iota16", [P, KEYS], F16)
        line16 = sb("line16", [P, P], F16)
        win_key = sb("win_key", [P, NWIN], F32)
        win_edge = sb("win_edge", [P, 2], F32)
        chunk_row = sb("chunk_row", [P, CG], F32)
        rng_sb = sb("rng_sb", [P, 1], F32)
        flag_i = sb("flag_i", [1, 2], I32)
        cols = sb("cols", [P, 176], F32)
        used_cols = [0]

        def col(n):
            used_cols[0] += n
            assert used_cols[0] <= 176
            return cols[:, used_cols[0] - n:used_cols[0]]

        cmin, cmax, bcol, badc = col(CG), col(CG), col(2), col(2)
        xsum, xss, nmean, rstd = col(NT), col(NT), col(NT), col(NT)
        isd, xscale, xbias = col(NT), col(NT), col(NT)
        degv, ntmp, minus_half, last_root, warm = col(NT), col(5), col(NT), col(NT - LAST), col(1)
        eps_c, bigc, temp_c, tempe = col(1), col(2), col(1), col(1)
        b1c, b1s = col(MT), col(MT)
        small = sb("small", [P, 320], F32)
        used_small = [0]

        def sm(n):
            used_small[0] += n
            assert used_small[0] <= 320
            return small[:, used_small[0] - n:used_small[0]]

        w1_ss, w2_ss, w_ss, wpd_ss = sm(2 * FT), sm(MT), sm(FT), sm(FT)
        t1_ss, h_ss = sm(3 * FT), sm(3 * MT)
        sums = sm(8)
        norms = sm(8)
        bound, pw, ipw, coef = sm(8), sm(8), sm(8), sm(8)
        zcoef, ocoef = sm(NT), sm(NT)
        stats, mv, lnr = sm(12), sm(2), sm(4)
        W1_, B1_, T1_, W2_, H_, PD_, WW_, WU_ = range(8)
        Z_, G_ = B1_, T1_
        C_H, C_P, C_B, C_L = range(4)
        gate = sb("gate", [P, 13, NT, NEXP], F32)
        dots, logit, ex, prob, hit, keep, pick = (gate[:, i] for i in range(7))
        pss, pnorm, gmax, gsum, pscale = (gate[:, 7 + i].rearrange("p t e -> p (t e)")[:, 0:NT] for i in range(5))
        simss, simr, tempv = gate[:, 12, 0], gate[:, 12, 1], gate[:, 12, 2, 0:1]

        bank = [ctx.enter_context(nc.psum_tensor(f"bank{i}", [P, 512], F32)) for i in range(8)]
        rest_dram = nc.dram_tensor("adj_rest_dram", (P, NT * NT * P), F16, kind="Internal").ap()

        S = {}

        class Sems:
            def __getitem__(self, name):
                if name not in S:
                    S[name] = sem(name)
                return S[name]

        S_ = Sems()
        x_in = [sem(f"x_in{t}") for t in range(NT)]
        xr_in = [sem(f"xr_in{t}") for t in range(NT)]
        feat_in = [sem(f"feat_in{i}") for i in range(2)]
        stage_in = [sem(f"stage_in{i}") for i in range(2)]
        out_done = [sem(f"out_done{i}") for i in range(2)]

        class Link:
            def __init__(self, eng, s):
                self.eng, self.s, self.n = eng, S_[s], 0

            def __call__(self, ins):
                self.n += 1
                ins.then_inc(self.s, 1)
                self.eng.wait_ge(self.s, self.n)

        loads = [("sq", "W1", k, h * HALF, HALF) for k in range(FT) for h in range(2)]
        loads += [("split", "W1", k, h * HALF, HALF) for k in range(FT) for h in range(2)]
        loads += [("sq", "W2", k, 0, D) for k in range(MT)]
        loads += [("split", "W2", k, 0, D) for k in range(MT)]
        loads += [("sq", "Wpd", k, 0, PD) for k in range(FT)]
        loads += [("sq", "W", k, 0, D) for k in range(FT)]
        loads += [("split", "Wpd", k, 0, PD) for k in range(FT)]
        loads += [("split", "W", k, 0, D) for k in range(FT)]
        dram = {"W1": W1, "W2": W2, "Wpd": WpdT, "W": WT}
        nrows = {"W1": D, "W2": MID, "Wpd": D, "W": D}
        squares = [0]
        for kind, *_ in loads:
            squares.append(squares[-1] + (kind == "sq"))

        def stage_freed(eng, i):
            if loads[i][0] == "sq":
                eng.wait_ge(S_["stage_sq"], squares[i + 1])
            else:
                eng.wait_ge(S_["stage_lo"], i + 1 - squares[i + 1])

        def places(a, k, c0):
            if a == "W1":
                v = arena3[:, :].rearrange("p (s h k n) -> p s h k n", s=SLOTS, h=2, k=FT)
                q = slice(1 + c0 // P, 1 + (c0 + HALF) // P)
                return v[:, q, 0, k, :], v[:, q, 1, k, :], W1_
            if a == "W2":
                return w2_slot[k][:, 0, :], w2_slot[k][:, 1, :], W2_
            if a == "Wpd":
                return wpd_hi[:, k, :], wpd_lo[:, k, :], PD_
            return w_hi[:, k, :], w_lo[:, k, :], WW_

        def invert_root(eng, link, square, out, tmp, root=None):
            if root is None:
                link(eng.tensor_tensor(out, square, minus_half[:, 0:square.shape[1]], ALU.pow))
            else:
                link(eng.reciprocal(out, root))
            link(eng.tensor_tensor(tmp, out, out, ALU.mult))
            link(eng.tensor_tensor(tmp, tmp, square, ALU.mult))
            link(eng.tensor_scalar(tmp, tmp, -0.5, 1.5, ALU.mult, ALU.add))
            link(eng.tensor_tensor(out, out, tmp, ALU.mult))

        def factors(eng, link, g0, g1, root=None):
            c, tmp = slice(g0, g1), ntmp[:, 2 * (g0 >= LAST):2 * (g0 >= LAST) + g1 - g0]
            if root is not None:
                eng.tensor_scalar(root, root, 1.0, None, ALU.max)
            link(eng.tensor_scalar(degv[:, c], degv[:, c], 1.0, None, ALU.max))
            invert_root(eng, link, degv[:, c], isd[:, c], tmp, root)
            link(eng.tensor_tensor(xscale[:, c], isd[:, c], rstd[:, c], ALU.mult))
            link(eng.tensor_scalar(xscale[:, c], xscale[:, c], X_SCALE, None, ALU.mult))
            return eng.tensor_tensor(xbias[:, c], xscale[:, c], nmean[:, c], ALU.mult)

        NCONST = 12
        block = ctx.enter_context(nc.Block())

        @block.sync
        def _(sp):
            sp.dma_start(dst_i[:], dst_rows.rearrange("(j p) e -> p j e", p=P)).then_inc(S_["edges_in"], 16)
            sp.dma_start(src_i[:], src_rows.rearrange("(j p) e -> p j e", p=P)).then_inc(S_["edges_in"], 16)
            sp.dma_start(rng_sb[0:NWIN, :], ranges).then_inc(S_["ranges_in"], 16)
            sp.dma_start(member_sb[0:NWIN + 1, :], member).then_inc(S_["member_in"], 16)
            sp.dma_start(line16[:], line).then_inc(S_["line_in"], 16)
            for t in range(NT):
                m = rows(t, N)
                sp.dma_start(x_raw[0:m, t, :], x[t * P:t * P + m, :]).then_inc(x_in[t], 16)

            def load(i):
                kind, a, k, c0, n = loads[i]
                if i >= 2:
                    stage_freed(sp, i - 2)
                m = rows(k, nrows[a])
                sp.dma_start(stage[0:m, i % 2, 0:n], dram[a][k * P:k * P + m, c0:c0 + n])\
                    .then_inc(stage_in[i % 2], 16)

            for i in range(2):
                load(i)
            sp.wait_ge(S_["feat_ones"], 1)
            sp.wait_ge(S_["flag_set"], 1)
            bad = sp.value_load(flag_i[0:1, 0:1], min_val=0, max_val=2 * NWIN)
            with sp.If(bad == 0):
                for i in range(NF):
                    if i >= 2:
                        sp.wait_ge(S_["score_made"], FSLOT // KG * (i - 1))
                    for b, r0, n, at in feature_pieces(i):
                        sp.wait_ge(S_["feat_out"], b + 1)
                        for k in range(3):
                            sp.dma_start(feat_rows[k:k + 1, i % 2, at:at + n * P], feat_blk[r0:r0 + n, b, k, :])\
                                .then_inc(feat_in[i % 2], 16)
                    for k in LOAD_AT.get(i, ()):
                        load(k)
            with sp.Else():
                for i in range(2, SQ_A + 2):
                    load(i)
            second_x = [i for i, l in enumerate(loads) if l[:2] == ("split", "Wpd")][2]
            for i in range(SQ_A + 2, len(loads)):
                if i == second_x:
                    sp.wait_ge(S_["z_mm"], NT)
                    for t in range(NT):
                        m = rows(t, N)
                        sp.dma_start(x2[0:m, t, :], x[t * P:t * P + m, :]).then_inc(xr_in[t], 16)
                load(i)

        @block.gpsimd
        def _(gp):
            gp.memset(ident[:], 0.0).then_inc(S_["consts_z"], 1)
            gp.memset(ident16[:], 0.0).then_inc(S_["consts_z"], 1)
            gp.memset(minus16[:], 0.0).then_inc(S_["consts_z"], 1)
            gp.wait_ge(S_["consts_z"], 3)
            for m, v in ((ident, 1.0), (ident16, 1.0), (minus16, -1.0)):
                gp.affine_select(out=m[:], in_=m[:], compare_op=ALU.not_equal, fill=v, base=0,
                                 pattern=[[-1, P]], channel_multiplier=1).then_inc(S_["consts"], 1)
            for o, pattern, base, mult in ((win_edge[:], [[W, 2]], 0, W), (chunk_row[:], [[P, CG]], 0, 1),
                                           (chunk_up, [[1, CROWS]], 1, 0), (chunk_down, [[-1, CROWS]], CROWS, 0),
                                           (iota16[:], [[1, KEYS]], 0, 0), (win_key[:], [[KEYS, NWIN]], 0, 0)):
                gp.iota(o, pattern, base=base, channel_multiplier=mult,
                        allow_small_or_imprecise_dtypes=True).then_inc(S_["consts"], 1)
            for o, v in ((zero16[:], 0.0), (ones16[:], 1.0), (ones[:], 1.0)):
                gp.memset(o, v).then_inc(S_["consts"], 1)
            gp.wait_ge(S_["cleared"], 6)
            gp.dma_start(b1c, b1).then_inc(S_["b1_in"], 16)
            gp.memset(feat_rows, 1.0).then_inc(S_["feat_ones"], 1)
            gp.wait_ge(S_["feat_ones"], 1)

            def source_lo(g):
                m = rows(g, N)
                gp.wait_ge(S_["xhi_made"], g + 1)
                gp.tensor_tensor(xs_lo[0:m, g, :], x_raw[0:m, g, :], xs_hi[0:m, g, :], ALU.subtract)\
                    .then_inc(S_["xlo_made"], 1)

            glink = Link(gp, "link_g")

            def invert_std():
                gp.wait_ge(S_["x_ss"], ACT_STATS)
                gp.wait_ge(S_["bn_made"], NT - ACT_STATS)
                glink(gp.tensor_scalar(xss, xss, 1.0 / D, 1e-5, ALU.mult, ALU.add))
                invert_root(gp, glink, xss, rstd, xsum)

            def sources():
                invert_std()
                lo = 0
                for b, (first, _) in enumerate(BATCHES):
                    gp.wait_ge(S_["degree_out"], BATCHES[b][1])
                    factors(gp, glink, *BATCHES[b]).then_inc(S_["factors_made"], 1)
                    while lo < min(first - 1, POOL_LO):
                        source_lo(lo)
                        lo += 1
                for g in range(lo, POOL_LO):
                    source_lo(g)

            rest_f32 = adj_rest.rearrange("p t d -> p (t d)").bitcast(F32)
            gp.memset(rest_f32, 0.0).then_inc(S_["rest_zero"], 1)
            gp.wait_ge(S_["flag_set"], 1)
            bad = gp.value_load(flag_i[0:1, 0:1], min_val=0, max_val=2 * NWIN)
            with gp.If(bad == 0):
                sources()
                gp.wait_ge(S_["rest_made"], len(REST_WINS))
            with gp.Else():
                gp.wait_ge(S_["rest_made"], NWIN)
                sources()
            gp.wait_ge(S_["rest_zero"], 1)
            gp.dma_start(rest_dram, adj_rest.rearrange("p t d -> p (t d)")).then_inc(S_["spilled"], 16)
            gp.wait_ge(S_["t1_lo"], 3 * FT)
            gp.dma_start(row_bc[:, 0:D], b2.partition_broadcast(P)).then_inc(S_["b2_in"], 16)
            gp.wait_ge(S_["z_mm"], NT)
            gp.wait_ge(S_["spilled"], 16)
            gp.dma_start(rest2.rearrange("p t d -> p (t d)"), rest_dram).then_inc(S_["rest_in"], 16)
            gp.wait_ge(S_["b2_in"], 16)
            for t in range(NT):
                m = rows(t, N)
                gp.wait_ge(xr_in[t], 16)
                gp.tensor_tensor(x2[0:m, t, :], x2[0:m, t, :], row_bc[0:m, 0:D], ALU.add).then_inc(S_["x2_b"], 1)
            gp.wait_ge(S_["x2_b"], NT)
            gp.dma_start(sim_bc[:], simT.partition_broadcast(P)).then_inc(S_["sim_in"], 16)
            gp.dma_start(bp_bc[:], bp.partition_broadcast(P)).then_inc(S_["sim_in"], 16)
            gp.dma_start(temp_c, temp.partition_broadcast(P)).then_inc(S_["sim_in"], 16)
            gp.wait_ge(S_["o_mm"], NT)
            gp.memset(wu_raw[0:GP, :], 0.0).then_inc(S_["link_p"], 1)
            gp.memset(g_rows[:], 0.0).then_inc(S_["link_p"], 1)
            gp.wait_ge(S_["link_p"], 2)
            for q in range(3):
                gp.dma_start(wu_raw[32 * q:32 * q + R, :], WuT).then_inc(S_["wu_in"], 16)
            for t in range(NT):
                m = rows(t, N)
                gp.wait_ge(S_["res_made"], t + 1)
                gp.dma_start(out[t * P:t * P + m, :], res[t % 2][0:m, :]).then_inc(out_done[t % 2], 16)
            for s in out_done:
                gp.wait_ge(s, 16 * NT // 2)

        @block.vector
        def _(dve):
            V = nc.vector
            link = Link(dve, "link_v")

            for o, v in ((cols[:], 0.0), (small[:], 0.0), (gate[:], 0.0), (start16, 1.0)):
                V.memset(o, v).then_inc(S_["cleared"], 1)
            dve.wait_ge(S_["cleared"], 4)
            V.memset(eps_c, 1e-5).then_inc(S_["cleared"], 1)
            V.memset(minus_half, -0.5).then_inc(S_["cleared"], 1)
            dve.wait_ge(S_["edges_in"], 32)
            V.tensor_reduce(cmin, dst_i, AX_X, ALU.min)
            link(V.tensor_reduce(cmax, dst_i, AX_X, ALU.max))
            V.tensor_copy(ends16[:, 0, :], cmin)
            V.tensor_copy(ends16[:, 1, :], cmax).then_inc(S_["chunk_ends"], 1)
            link(V.tensor_scalar(low_i, src_i, P - 1, None, ALU.bitwise_and))
            V.tensor_tensor(sq_i, low_i, low_i, ALU.mult).then_inc(S_["sources_cut"], 1)

            dve.wait_ge(S_["consts"], NCONST)
            dve.wait_ge(S_["range_done"], 1)
            q = slice(0, NWIN)
            link(V.tensor_scalar(touch[0][q, :], bank[5][q, 0:CROWS], win_edge[q, 1:2], None, ALU.is_lt))
            link(V.scalar_tensor_tensor(touch[1][q, :], bank[6][q, 0:CROWS], win_edge[q, 0:1], touch[0][q, :],
                                        ALU.is_ge, ALU.mult))
            V.tensor_tensor(touch[0][q, :], touch[1][q, :], chunk_down[q, :], ALU.mult)
            link(V.tensor_tensor(touch[2][q, :], touch[1][q, :], chunk_up[q, :], ALU.mult))
            link(V.tensor_reduce(bcol[q, 1:2], touch[0][q, :], AX_X, ALU.max))
            V.tensor_scalar(start16[q, 0:1], bcol[q, 1:2], -1.0, float(CROWS), ALU.mult, ALU.add)\
                .then_inc(S_["start_made"], 1)
            link(V.tensor_reduce(bcol[q, 0:1], touch[2][q, :], AX_X, ALU.max))
            dve.wait_ge(S_["ranges_in"], 16)
            V.scalar_tensor_tensor(badc[q, 0:1], bcol[q, 0:1], bcol[q, 1:2], rng_sb[q, :], ALU.add, ALU.is_gt)\
                .then_inc(S_["range_cols"], 1)
            dve.wait_ge(S_["flag_sum"], 1)
            V.tensor_copy(flag_i[0:1, 0:1], bank[7][0:1, 0:1]).then_inc(S_["flag_set"], 1)
            dve.wait_ge(S_["sources_cut"], 1)
            V.tensor_scalar(src_low, sq_i, 15, None, ALU.bitwise_and).then_inc(S_["sources_cut"], 1)
            dve.wait_ge(S_["sources_cut"], 2)
            V.tensor_tensor(feat[:, :, 0, :], sq_i, src_low, ALU.subtract).then_inc(S_["feat_made"], 1)
            dve.wait_ge(S_["slot_rows"], 1)
            for j in range(CG):
                ins = V.tensor_scalar(pick_slot[:, j, :], bank[4][:, 0:NSLOT], float(CROWS - 1),
                                      chunk_row[:, j:j + 1], ALU.min, ALU.is_equal)
            ins.then_inc(S_["slots_picked"], 1)
            V.tensor_scalar(win_i, dst_i, W.bit_length() - 1, None, ALU.logical_shift_right).then_inc(S_["dst_cut"], 1)
            V.tensor_scalar(up_i, src_i, P.bit_length() - 1, None, ALU.logical_shift_right)
            link(V.tensor_scalar(dst_i, dst_i, W - 1, None, ALU.bitwise_and))
            V.scalar_tensor_tensor(keys[:, 0], up_i, float(W), dst_i, ALU.mult, ALU.add).then_inc(S_["keys_ready"], 1)
            dve.wait_ge(S_["flag_set"], 1)

            def x_val(g):
                m = rows(g, N)
                if g < LAST:
                    dve.wait_ge(S_["factors_made"], 1 + [g < b1 for _, b1 in BATCHES].index(True))
                V.tensor_scalar(x_raw[0:m, g, :], x_raw[0:m, g, :], xscale[0:m, g:g + 1], xbias[0:m, g:g + 1],
                                ALU.mult, ALU.add).then_inc(S_["xval_made"], 1)

            def source_lo(g):
                m = rows(g, N)
                dve.wait_ge(S_["xhi_made"], g + 1)
                V.tensor_tensor(xs_lo[0:m, g, :], x_raw[0:m, g, :], xs_hi[0:m, g, :], ALU.subtract)\
                    .then_inc(S_["xlo_made_v"], 1)

            def x_stats(t, link):
                m = rows(t, N)
                dve.wait_ge(x_in[t], 16)
                for j in range(2):
                    ins = V.bn_stats(stats[0:m, 6 * j:6 * j + 6], x_raw[0:m, t, j * 512:(j + 1) * 512])
                link(ins)
                link(V.bn_aggr(mv[0:m, :], stats[0:m, :].rearrange("p (a b) -> p a b", a=2)))
                V.tensor_scalar(nmean[0:m, t:t + 1], mv[0:m, 0:1], -1.0, None, ALU.mult)
                V.tensor_scalar(xss[0:m, t:t + 1], mv[0:m, 1:2], float(D), None, ALU.mult).then_inc(S_["bn_made"], 1)

            def short_path():
                link = Link(dve, "link_fast")
                dve.wait_ge(S_["turned"], 1)
                V.tensor_copy(key_col[:, 0:NSLOT], bank[4][:, 0:NSLOT]).then_inc(S_["turned_used"], 1)
                dve.wait_ge(S_["turned_used"], 1)
                for w in range(NWIN):
                    for n in range(WFIRST[w], WFIRST[w + 1]):
                        if n % KG == 0:
                            for t in BN_AT.get(n // KG, ()):
                                x_stats(t, link)
                            for g in VAL_AT.get(n // KG, ()):
                                x_val(g)
                        if n % KG == 0 and n >= KRING:
                            dve.wait_ge(S_["key_used"], (n - KRING) // KG + 1)
                        ins = V.tensor_scalar(key_hot[:, n % KRING, :], iota16[:], float(KEYS * w),
                                              key_col[:, n:n + 1], ALU.add, ALU.is_equal)
                        if n % KG == KG - 1 or n == NSLOT - 1:
                            ins.then_inc(S_["key_made"], 1)
                for g in VAL_AT[NG]:
                    x_val(g)

            def long_path():
                link = Link(dve, "link_slow")
                for i, c in enumerate((key_col, src_col)):
                    dve.wait_ge(S_["turned"], i + 1)
                    V.tensor_copy(c[:, 0:CROWS], bank[4 + i][:, 0:CROWS]).then_inc(S_["turned_used"], 1)
                dve.wait_ge(S_["turned_used"], 2)
                with dve.Fori(0, NWIN) as w:
                    with dve.Fori(0, NCH) as c:
                        dve.wait_ge(S_["slow_used"], w * NCH + c + 1)
                        V.tensor_scalar(src_hot[:, 0, :], iota16[:, 0:P], src_col[:, bass.ds(c, 1)], None, ALU.is_equal)
                        V.tensor_scalar(key_hot[:, 0, :], iota16[:], win_key[:, bass.ds(w, 1)],
                                        key_col[:, bass.ds(c, 1)], ALU.add, ALU.is_equal)\
                            .then_inc(S_["slow_made"], 1)
                for t in range(ACT_STATS, NT):
                    x_stats(t, link)
                for g in range(LAST):
                    x_val(g)

            bad = dve.value_load(flag_i[0:1, 0:1], min_val=0, max_val=2 * NWIN)
            with dve.If(bad == 0):
                short_path()
            with dve.Else():
                long_path()

            dve.wait_ge(S_["degree_out"], NT)
            dve.wait_ge(S_["factors_made"], len(BATCHES))
            link(factors(V, link, LAST, NT, last_root))
            link(V.tensor_scalar(xss, degv, 2048.0, None, ALU.is_gt))
            V.tensor_reduce(bigc[:, 0:1], xss, AX_X, ALU.max).then_inc(S_["big_col"], 1)
            for g in range(LAST, NT):
                x_val(g)
            for g in range(POOL_LO, NT):
                source_lo(g)
                if g == POOL_LO:
                    dve.wait_ge(S_["big_sum"], 1)
                    V.tensor_copy(flag_i[0:1, 1:2], bank[6][0:1, 0:1]).then_inc(S_["big_set"], 1)
            for j in range(3):
                if j == 2:
                    dve.wait_ge(S_["bcast_made"], 1)
                for i in range(4 * j, min(4 * j + 4, NT)):
                    ins = V.tensor_scalar(val[:, j % 2, (i % 4) * P:(i % 4 + 1) * P], ident[:], isd[:, i:i + 1],
                                          None, ALU.mult)
                ins.then_inc(S_["diag_made"], 1)

            def pow2(cs, link):
                link(V.tensor_scalar(bound[:, cs], bound[:, cs], 1e-30, None, ALU.max))
                link(V.tensor_scalar(ipw.bitcast(I32)[:, cs], bound.bitcast(I32)[:, cs], 0x7F800000, None,
                                     ALU.bitwise_and))
                link(V.tensor_scalar(pw.bitcast(I32)[:, cs], ipw.bitcast(I32)[:, cs], -1.0, float(268 << 23),
                                     ALU.mult, ALU.add))
                link(V.tensor_scalar(ipw.bitcast(I32)[:, cs], ipw.bitcast(I32)[:, cs], float(-(14 << 23)), None,
                                     ALU.add))

            def split_lo(i):
                kind, a, k, c0, n = loads[i]
                m = rows(k, nrows[a])
                dve.wait_ge(S_["stage_hi"], i + 1 - squares[i + 1])
                hi, lo, p = places(a, k, c0)
                src = stage[0:m, i % 2, 0:n]
                if a == "W1":
                    src = src.rearrange("p (s n) -> p s n", n=P)
                V.scalar_tensor_tensor(lo[0:m], src, pw[0:m, p:p + 1], hi[0:m], ALU.mult, ALU.subtract)\
                    .then_inc(S_["stage_lo"], 1)

            def norms_ready(n):
                dve.wait_ge(S_["norm_done"], n)

            def t1_val(i):
                f, (n0, n) = i // 3, DSPLIT[i % 3]
                if i % 3 == 0:
                    dve.wait_ge(S_["t1_mm"], f + 1)
                if i == 0:
                    dve.wait_ge(S_["bcast_used"], 3)
                if i >= 2:
                    dve.wait_ge(S_["t1_lo"], i - 1)
                V.tensor_tensor(val[:, i % 2, 0:n], bank[3 * (f % 2) + i % 3][:, 0:n], row_bc[:, n0:n0 + n], ALU.mult)\
                    .then_inc(S_["t1_val"], 1)

            def t1_lo(i):
                f, (n0, n) = i // 3, DSPLIT[i % 3]
                dve.wait_ge(S_["t1_hi"], i + 1)
                V.tensor_tensor(t1T[1][:, f, n0:n0 + n], val[:, i % 2, 0:n], t1T[0][:, f, n0:n0 + n], ALU.subtract)\
                    .then_inc(S_["t1_lo"], 1)

            n1 = [i for i, l in enumerate(loads) if l[0] == "split" and l[1] == "W1"]
            for f in range(FT):
                for j in range(3):
                    i = 3 * f + j
                    t1_val(i)
                    if i >= 1:
                        t1_lo(i - 1)
                if f == 3:
                    norms_ready(1)
                    link(V.tensor_copy(bound[:, 0:1], norms[:, W1_:W1_ + 1]))
                    pow2(slice(0, 1), link)
                    V.tensor_copy(coef[:, 4:5], coef[:, 4:5]).then_inc(S_["w1_scaled"], 1)
                for i in W1_AT.get(f, ()):
                    split_lo(n1[i])
            t1_lo(3 * FT - 1)

            norms_ready(2)
            link(V.tensor_tensor(bound[:, H_:H_ + 1], norms[:, T1_:T1_ + 1], norms[:, W1_:W1_ + 1], ALU.mult))
            link(V.scalar_tensor_tensor(bound[:, H_:H_ + 1], bound[:, H_:H_ + 1], 1.0 / T1_SCALE,
                                        norms[:, B1_:B1_ + 1], ALU.mult, ALU.add))
            pow2(slice(H_, H_ + 1), link)
            link(V.scalar_tensor_tensor(coef[:, C_H:C_H + 1], ipw[:, W1_:W1_ + 1], 1.0 / T1_SCALE, pw[:, H_:H_ + 1],
                                        ALU.mult, ALU.mult))
            V.tensor_scalar(b1s, b1c, pw[:, H_:H_ + 1], None, ALU.mult).then_inc(S_["h_coef"], 1)
            n2 = [i for i, l in enumerate(loads) if l[0] == "split" and l[1] == "W2"]
            for mt in range(MT):
                m = rows(mt, MID)
                for j in range(3):
                    i, (n0, n) = 3 * mt + j, DSPLIT[j]
                    dve.wait_ge(S_["h_hi"], i + 1)
                    V.tensor_tensor(hT[1][0:m, mt, n0:n0 + n], val[0:m, i % 2, 0:n], hT[0][0:m, mt, n0:n0 + n],
                                    ALU.subtract).then_inc(S_["h_lo"], 1)
                if mt == 6:
                    norms_ready(3)
                    link(V.tensor_copy(bound[:, W2_:W2_ + 1], norms[:, W2_:W2_ + 1]))
                    pow2(slice(W2_, W2_ + 1), link)
                    V.tensor_copy(coef[:, 5:6], coef[:, 5:6]).then_inc(S_["w2_scaled"], 1)
                for k in W2_AT.get(mt, ()):
                    split_lo(n2[k])

            norms_ready(4)
            zc = slice(Z_, Z_ + 1)
            link(V.scalar_tensor_tensor(bound[:, zc], norms[:, H_:H_ + 1], ipw[:, H_:H_ + 1], norms[:, W2_:W2_ + 1],
                                        ALU.mult, ALU.mult))
            pow2(zc, link)
            link(V.tensor_tensor(coef[:, 6:7], ipw[:, H_:H_ + 1], ipw[:, W2_:W2_ + 1], ALU.mult))
            link(V.tensor_tensor(coef[:, 6:7], coef[:, 6:7], pw[:, zc], ALU.mult))
            V.tensor_scalar(zcoef, isd, coef[:, 6:7], None, ALU.mult).then_inc(S_["z_coef"], 1)
            link(V.tensor_scalar(ocoef, isd, ipw[:, zc], None, ALU.mult))
            for t in range(NT):
                m = rows(t, N)
                for j in range(2):
                    i = 2 * t + j
                    dve.wait_ge(S_["z_hi"], i + 1)
                    V.tensor_tensor(z[1][0:m, t, j * 512:(j + 1) * 512], val[0:m, i % 2, :],
                                    z[0][0:m, t, j * 512:(j + 1) * 512], ALU.subtract).then_inc(S_["z_lo"], 1)
            norms_ready(5)
            link(V.tensor_copy(bound[:, PD_:WW_ + 1], norms[:, PD_:WW_ + 1]))
            link(V.tensor_scalar(bound[:, G_:G_ + 1], norms[:, PD_:PD_ + 1], 32.0, None, ALU.mult))
            pow2(slice(G_, G_ + 1), link)
            pow2(slice(PD_, WW_ + 1), link)
            V.tensor_scalar(coef[:, C_P:C_P + 1], ipw[:, PD_:PD_ + 1], 1.0 / X_SCALE, None, ALU.mult)
            V.tensor_scalar(coef[:, C_B:C_B + 1], ipw[:, WW_:WW_ + 1], 1.0 / X_SCALE, None, ALU.mult)\
                .then_inc(S_["f_coef"], 1)

            def x2_tile(t):
                m = rows(t, N)
                dve.wait_ge(S_["o_mm"], t + 1)
                dve.wait_ge(S_["x2_b"], t + 1)
                for j in range(2):
                    o = x2[0:m, t, j * 512:(j + 1) * 512]
                    ins = V.scalar_tensor_tensor(o, bank[2 * ((t + 1) % 3) + j][0:m, :], ocoef[0:m, t:t + 1], o,
                                                 ALU.mult, ALU.add)
                    if j == 1:
                        ins.then_inc(S_["x2_done"], 1)
                dve.wait_ge(S_["x2_done"], t + 1)
                for j in range(2):
                    ins = V.bn_stats(stats[0:m, 6 * j:6 * j + 6], x2[0:m, t, j * 512:(j + 1) * 512])
                link(ins)
                V.bn_aggr(mv[0:m, :], stats[0:m, :].rearrange("p (a b) -> p a b", a=2)).then_inc(S_["ln_var"], 1)
                dve.wait_ge(S_["ln_std"], t + 1)
                link(V.reciprocal(lnr[0:m, 1:2], lnr[0:m, 0:1]))
                link(V.tensor_scalar(mv[0:m, 1:2], mv[0:m, 1:2], 1e-5, None, ALU.add))
                tmp, inv = ntmp[0:m, 0:1], lnr[0:m, 1:2]
                link(V.tensor_tensor(tmp, inv, inv, ALU.mult))
                link(V.tensor_tensor(tmp, tmp, mv[0:m, 1:2], ALU.mult))
                link(V.tensor_scalar(tmp, tmp, -0.5, 1.5, ALU.mult, ALU.add))
                link(V.tensor_tensor(inv, inv, tmp, ALU.mult))
                link(V.tensor_scalar(lnr[0:m, 2:3], lnr[0:m, 1:2], X_SCALE, None, ALU.mult))
                V.scalar_tensor_tensor(lnr[0:m, 3:4], mv[0:m, 0:1], -1.0, lnr[0:m, 2:3], ALU.mult, ALU.mult)\
                    .then_inc(S_["ln_coef"], 1)

            def yT_lo_tile(t):
                m = rows(t, N)
                for j in range(2):
                    dve.wait_ge(S_["yt_hi"], 2 * t + j + 1)
                    V.tensor_tensor(yT_lo[:, 4 * j:4 * j + 4, t * P:t * P + m],
                                    bank[6 + j][:, :].rearrange("p (k d) -> p k d", k=4)[:, :, 0:m],
                                    yT_hi[:, 4 * j:4 * j + 4, t * P:t * P + m], ALU.subtract)\
                        .then_inc(S_["yt_lo"], 1)

            npd = [i for i, l in enumerate(loads) if l[0] == "split" and l[1] == "Wpd"]
            for t in range(NT):
                x2_tile(t)
                if t >= 1:
                    yT_lo_tile(t - 1)
                if t < 4:
                    for k in (2 * t, 2 * t + 1):
                        split_lo(npd[k])
                if t == 5:
                    dve.wait_ge(S_["sim_norm"], 1)
                    link(V.tensor_scalar(simss, simr, 1e-12, None, ALU.max))
                    link(V.reciprocal(simss, simss))
                    for e in range(NEXP):
                        ins = V.tensor_scalar(sim_bc[:, e, :], sim_bc[:, e, :], simss[:, e:e + 1], None, ALU.mult)
                    link(ins)
                    link(V.tensor_scalar(tempv, temp_c, CLAMP_MAX, None, ALU.min))
            yT_lo_tile(NT - 1)

            def sim_products(t):
                m = rows(t, N)
                dve.wait_ge(S_["p_val"], t + 1)
                for e in range(NEXP):
                    V.tensor_tensor_reduce(out=scratch[0:m, :], in0=pr[0:m, t, :], in1=sim_bc[0:m, e, :],
                                           scale=1.0, scalar=0.0, op0=ALU.mult, op1=ALU.add,
                                           accum_out=dots[0:m, t, e:e + 1]).then_inc(S_["dots_made"], 1)
                    dve.wait_ge(S_["dots_made"], NEXP * t + e + 1)

            dve.wait_ge(S_["o_mm"], NT)
            V.memset(down[:, NT - 1, :], 0.0)
            nw = [i for i, l in enumerate(loads) if l[0] == "split" and l[1] == "W"]
            for t in range(NT):
                m = rows(t, N)
                b = bank[(t + 4) % 6]
                if t < FT // 2:
                    for k in (2 * t, 2 * t + 1):
                        split_lo(nw[k])
                dve.wait_ge(S_["p_mm"], t + 1)
                V.scalar_tensor_tensor(pr[0:m, t, :], b[0:m, 0:PROJ], coef[0:m, C_P:C_P + 1], bp_bc[0:m, :],
                                       ALU.mult, ALU.add).then_inc(S_["p_val"], 1)
                V.tensor_scalar(down[0:m, t, :], b[0:m, PROJ:PD], coef[0:m, C_P:C_P + 1], None, ALU.mult)\
                    .then_inc(S_["p_used"], 1)
                if t >= FT // 2:
                    sim_products(t - FT // 2)
            for t in range(NT - FT // 2, NT):
                sim_products(t)

            dve.wait_ge(S_["dots_made"], NT * NEXP)
            dve.wait_ge(S_["p_norm"], 1)

            def each(v):
                return v.unsqueeze(2).to_broadcast([P, NT, NEXP])

            link(V.tensor_scalar(pnorm, pnorm, 1e-12, None, ALU.max))
            link(V.reciprocal(pscale, pnorm))
            dve.wait_ge(S_["temp_exp"], 1)
            link(V.tensor_tensor(logit, dots, each(pscale), ALU.mult))
            link(V.tensor_scalar(logit, logit, tempe, None, ALU.mult))
            link(V.tensor_reduce(gmax, logit, AX_X, ALU.max))
            V.tensor_tensor(logit, logit, each(gmax), ALU.subtract).then_inc(S_["exp_in"], 1)
            dve.wait_ge(S_["exp_out"], 1)
            link(V.tensor_reduce(gsum, ex, AX_X, ALU.add))
            link(V.reciprocal(gsum, gsum))
            link(V.tensor_tensor(prob, ex, each(gsum), ALU.mult))
            link(V.tensor_reduce(gmax, prob, AX_X, ALU.max))
            link(V.tensor_tensor(hit, prob, each(gmax), ALU.is_equal))
            link(V.memset(keep, 1.0))
            for e in range(1, NEXP):
                link(V.tensor_tensor(keep[:, :, e], keep[:, :, e - 1], hit[:, :, e - 1], ALU.is_gt))
            link(V.tensor_tensor(pick, hit, keep, ALU.mult))
            link(V.tensor_tensor(pick, pick, prob, ALU.mult))
            link(V.tensor_scalar(pick, pick, pw[:, G_:G_ + 1], None, ALU.mult))
            r0 = 0
            for e, r in enumerate(RANKS):
                ins = V.tensor_tensor(gated[:, :, r0:r0 + r], down[:, :, r0:r0 + r],
                                      pick[:, :, e:e + 1].to_broadcast([P, NT, r]), ALU.mult)
                r0 += r
            link(ins)
            dve.wait_ge(S_["link_p"], 2)
            V.tensor_copy(g_rows[:, :, 32:32 + R], gated)
            link(V.tensor_copy(g_rows[:, :, 0:R], gated))
            V.tensor_tensor(g_rows[:, :, 64:64 + R], gated, g_rows[:, :, 0:R], ALU.subtract).then_inc(S_["g_made"], 1)
            norms_ready(6)
            link(V.tensor_copy(bound[:, WU_:WU_ + 1], norms[:, WU_:WU_ + 1]))
            pow2(slice(WU_, WU_ + 1), link)
            link(V.tensor_tensor(coef[:, C_L:C_L + 1], ipw[:, WU_:WU_ + 1], ipw[:, G_:G_ + 1], ALU.mult))
            link(V.tensor_scalar(wu_raw[0:GP, :], wu_raw[0:GP, :], pw[0:GP, WU_:WU_ + 1], None, ALU.mult))
            link(V.tensor_copy(wu[0:GP, :], wu_raw[0:GP, :]))
            V.tensor_tensor(wu[32:64, :], wu_raw[32:64, :], wu[32:64, :], ALU.subtract).then_inc(S_["wu_done"], 1)
            dve.wait_ge(S_["gt_mm"], 1)
            for j in range(2):
                ins = V.tensor_copy(gT[0:GP, 5 * j:5 * j + 5, :],
                                    bank[6 + j][:, :].bitcast(F16)[0:GP, 0:5 * P].rearrange("p (t d) -> p t d", t=5))
            ins.then_inc(S_["gt_made"], 1)

            for t in range(NT):
                m = rows(t, N)
                dve.wait_ge(S_["b_mm"], t + 1)
                if t >= 2:
                    dve.wait_ge(out_done[t % 2], 16 * (t // 2))
                q = 4 * ((t + 1) % 2)
                for j in range(2):
                    V.scalar_tensor_tensor(res[t % 2][0:m, j * 512:(j + 1) * 512], bank[q + j][0:m, :],
                                           coef[0:m, C_B:C_B + 1], x2[0:m, t, j * 512:(j + 1) * 512],
                                           ALU.mult, ALU.add).then_inc(S_["res_half"], 1)
                dve.wait_ge(S_["res_half"], 2 * t + 2)
                dve.wait_ge(S_["l_mm"], t + 1)
                for j in range(2):
                    o = res[t % 2][0:m, j * 512:(j + 1) * 512]
                    ins = V.scalar_tensor_tensor(o, bank[q + 2 + j][0:m, :], coef[0:m, C_L:C_L + 1], o,
                                                 ALU.mult, ALU.add)
                ins.then_inc(S_["res_made"], 1)

        @block.scalar
        def _(act):
            A = nc.scalar.activation
            link = Link(act, "link_a")
            last_note = [None]

            def note_free():
                if last_note[0]:
                    act.wait_ge(S_[last_note[0][0]], last_note[0][1])

            def noted(name, value):
                last_note[0] = (name, value)

            def x_stats(t, link):
                m = rows(t, N)
                act.wait_ge(x_in[t], 16)
                if t == 0:
                    act.wait_ge(S_["cleared"], 6)
                note_free()
                link(A(junk[0:m, :], x_raw[0:m, t, :], ACT.Copy, accum_out=xsum[0:m, t:t + 1]))
                link(A(nmean[0:m, t:t + 1], xsum[0:m, t:t + 1], ACT.Copy, scale=-1.0 / D))
                A(junk[0:m, :], x_raw[0:m, t, :], ACT.Square, bias=nmean[0:m, t:t + 1],
                  accum_out=xss[0:m, t:t + 1]).then_inc(S_["x_ss"], 1)
                noted("x_ss", t + 1)

            def square(i):
                kind, a, k, c0, n = loads[i]
                m = rows(k, nrows[a])
                ss = {"W1": w1_ss, "W2": w2_ss, "W": w_ss, "Wpd": wpd_ss}[a]
                q = 2 * k + c0 // HALF if a == "W1" else k
                act.wait_ge(stage_in[i % 2], 16 * (i // 2 + 1))
                note_free()
                A(junk[0:m, 0:n], stage[0:m, i % 2, 0:n], ACT.Square, accum_out=ss[0:m, q:q + 1])\
                    .then_inc(S_["stage_sq"], 1)
                noted("stage_sq", squares[i + 1])

            def add_up(q, v):
                note_free()
                last_note[0] = None
                return A(junk[:, 0:v.shape[1]], v, ACT.Copy, accum_out=sums[:, q:q + 1])

            def norm(n, q0, q1):
                act.wait_ge(S_["norm_sum"], n)
                A(norms[:, q0:q1], bank[7][:, 0:q1 - q0], ACT.Sqrt).then_inc(S_["norm_done"], 1)

            def split_hi(i):
                kind, a, k, c0, n = loads[i]
                m = rows(k, nrows[a])
                act.wait_ge(stage_in[i % 2], 16 * (i // 2 + 1))
                hi, lo, p = places(a, k, c0)
                src = stage[0:m, i % 2, 0:n]
                if a == "W1":
                    src = src.rearrange("p (s n) -> p s n", n=P)
                A(hi[0:m], src, ACT.Copy, scale=pw[0:m, p:p + 1]).then_inc(S_["stage_hi"], 1)

            def degree_out(g):
                act.wait_ge(S_["deg_done"], g + 1)
                if g >= LAST:
                    A(last_root[:, g - LAST:g - LAST + 1], bank[7][:, g:g + 1], ACT.Sqrt)
                A(degv[:, g:g + 1], bank[7][:, g:g + 1], ACT.Copy).then_inc(S_["degree_out"], 1)

            def source_hi(g):
                m = rows(g, N)
                act.wait_ge(S_["xval_made"], g + 1)
                A(xs_hi[0:m, g, :], x_raw[0:m, g, :], ACT.Copy).then_inc(S_["xhi_made"], 1)

            def take(w, j=None):
                act.wait_ge(S_["win_done"], w + 1)
                b = bank[w % WPT if j is None else j]
                A(adj[:, :, bass.ds(w * W, W)], b[:, 0:KEYS].rearrange("p (t d) -> p t d", t=NT), ACT.Copy)\
                    .then_inc(S_["adj_made"], 1)

            def take_rest(w, j=None):
                act.wait_ge(S_["sub_done"], w + 1)
                b = bank[w % WPT if j is None else j]
                A(adj_rest[:, :, bass.ds(w * W, W)], b[:, 0:KEYS].rearrange("p (t d) -> p t d", t=NT), ACT.Copy)\
                    .then_inc(S_["rest_made"], 1)

            act.wait_ge(S_["cleared"], 6)
            A(warm, eps_c, ACT.Sqrt)
            act.wait_ge(S_["sources_cut"], 1)
            A(feat[:, :, 2, :], low_i, ACT.Copy).then_inc(S_["feat_made"], 1)
            act.wait_ge(S_["sources_cut"], 2)
            A(feat[:, :, 1, :], src_low, ACT.Copy).then_inc(S_["feat_made"], 1)
            act.wait_ge(S_["dst_cut"], 1)
            A(keys[:, 1], win_i, ACT.Copy, scale=float(KEYS)).then_inc(S_["keys_ready"], 1)

            act.wait_ge(S_["flag_set"], 1)
            bad = act.value_load(flag_i[0:1, 0:1], min_val=0, max_val=2 * NWIN)
            with act.If(bad == 0):
                flink = Link(act, "link_fast_a")

                def source_hots(g):
                    n = min(KG, NSLOT - KG * g)
                    if g * KG >= SRING:
                        act.wait_ge(S_["key_used"], g - SRING // KG + 1)
                    act.wait_ge(S_["score_made"], g + 1)
                    q = KG * g % SRING
                    A(src_hot[:, q:q + n, :].rearrange("p s n -> p (s n)"), bank[5 + g % 2][:, 0:n * P], ACT.Relu)\
                        .then_inc(S_["src_made"], 1)

                for b in range(NBLK):
                    m = rows(b, NSLOT)
                    act.wait_ge(S_["feat_mm"], b + 1)
                    A(feat_blk[0:m, b].rearrange("p k e -> p (k e)"), bank[b][0:m, 0:3 * P], ACT.Copy)\
                        .then_inc(S_["feat_out"], 1)
                for g in range(AHEAD):
                    source_hots(g)
                for w in range(NWIN):
                    for n in range(WFIRST[w], WFIRST[w + 1]):
                        if n % KG == 0:
                            g = n // KG
                            if g + AHEAD < NG:
                                source_hots(g + AHEAD)
                            for t in STATS_AT.get(g, ()):
                                x_stats(t, flink)
                            for t in OUT_AT.get(g, ()):
                                degree_out(t)
                            for t in HI_AT.get(g, ()):
                                source_hi(t)
                            for i in SQ_AT.get(g, ()):
                                square(i)
                    take(w)
                    if w - 1 in REST_WINS:
                        act.wait_ge(S_["rest_zero"], 1)
                        take_rest(w - 1)
                for t in OUT_AT[NG]:
                    degree_out(t)
                for t in HI_AT[NG]:
                    source_hi(t)
                note_free()
            with act.Else():
                last_note[0] = None
                slink = Link(act, "link_slow_a")
                act.wait_ge(S_["rest_zero"], 1)
                with act.Fori(0, NT) as g:
                    for j in range(WPT):
                        take(WPT * g + j, j)
                        take_rest(WPT * g + j, j)
                for t in range(ACT_STATS):
                    x_stats(t, slink)
                for i in range(SQ_A):
                    square(i)
                for g in range(NT):
                    degree_out(g)
                for g in range(NT):
                    source_hi(g)
                note_free()
            last_note[0] = None

            for j in range(3):
                act.wait_ge(S_["bcast_made"], j + 1)
                n = min(512, NT * P - 512 * j)
                A(row_bc[:, 512 * j:512 * j + n], bank[6 + j % 2][:, 0:n], ACT.Copy, scale=T1_SCALE / X_SCALE)\
                    .then_inc(S_["bcast_used"], 1)
            n1 = [i for i, l in enumerate(loads) if l[0] == "split" and l[1] == "W1"]
            for f in range(FT):
                for j in range(3):
                    i, (n0, n) = 3 * f + j, DSPLIT[j]
                    act.wait_ge(S_["t1_val"], i + 1)
                    A(t1T[0][:, f, n0:n0 + n], val[:, i % 2, 0:n], ACT.Copy).then_inc(S_["t1_hi"], 1)
                    act.wait_ge(S_["t1_hi"], i + 1)
                    note_free()
                    A(junk[:, 0:n], t1T[0][:, f, n0:n0 + n], ACT.Square, accum_out=t1_ss[:, i:i + 1])\
                        .then_inc(S_["t1_sq"], 1)
                    noted("t1_sq", i + 1)
                for i in SQ1_AT.get(f, ()):
                    square(i)
                if f == 2:
                    act.wait_ge(S_["stage_sq"], 2 * FT)
                    link(add_up(W1_, w1_ss))
                    act.wait_ge(S_["b1_in"], 16)
                    A(junk[:, 0:MT], b1c, ACT.Square, accum_out=sums[:, B1_:B1_ + 1]).then_inc(S_["norm_in"], 1)
                    noted("norm_in", 1)
                if f == 3:
                    norm(1, W1_, B1_ + 1)
                    act.wait_ge(S_["w1_scaled"], 1)
                for i in W1_AT.get(f, ()):
                    split_hi(n1[i])
            act.wait_ge(S_["t1_sq"], 3 * FT)
            add_up(T1_, t1_ss).then_inc(S_["norm_in"], 1)
            noted("norm_in", 2)
            norm(2, T1_, T1_ + 1)
            act.wait_ge(S_["h_coef"], 1)

            n2 = [i for i, l in enumerate(loads) if l[0] == "split" and l[1] == "W2"]
            s2 = [i for i, l in enumerate(loads) if l[0] == "sq" and l[1] == "W2"]
            for mt in range(MT):
                m = rows(mt, MID)
                act.wait_ge(S_["h_mm"], mt + 1)
                if mt == 0:
                    act.wait_ge(S_["t1_lo"], 3 * FT)
                    act.wait_ge(S_["spilled"], 16)
                for j in range(3):
                    i, (n0, n) = 3 * mt + j, DSPLIT[j]
                    if i >= 2:
                        act.wait_ge(S_["h_lo"], i - 1)
                    A(val[0:m, i % 2, 0:n], bank[3 * (mt % 2) + j][0:m, 0:n], ACT.Relu, bias=b1s[0:m, mt:mt + 1],
                      scale=coef[0:m, C_H:C_H + 1]).then_inc(S_["h_val"], 1)
                    act.wait_ge(S_["h_val"], i + 1)
                    A(hT[0][0:m, mt, n0:n0 + n], val[0:m, i % 2, 0:n], ACT.Copy).then_inc(S_["h_hi"], 1)
                    act.wait_ge(S_["h_hi"], i + 1)
                    note_free()
                    A(junk[0:m, 0:n], hT[0][0:m, mt, n0:n0 + n], ACT.Square, accum_out=h_ss[0:m, i:i + 1])\
                        .then_inc(S_["h_sq"], 1)
                    noted("h_sq", i + 1)
                if mt < 6:
                    for k in (2 * mt, 2 * mt + 1):
                        square(s2[k])
                if mt == 5:
                    act.wait_ge(S_["stage_sq"], squares[s2[-1] + 1])
                    add_up(W2_, w2_ss).then_inc(S_["norm_in"], 1)
                    noted("norm_in", 3)
                if mt == 6:
                    norm(3, W2_, W2_ + 1)
                    act.wait_ge(S_["w2_scaled"], 1)
                for k in W2_AT.get(mt, ()):
                    act.wait_ge(S_["h_mm"], k)
                    split_hi(n2[k])
            act.wait_ge(S_["h_sq"], 3 * MT)
            add_up(H_, h_ss).then_inc(S_["norm_in"], 1)
            noted("norm_in", 4)
            norm(4, H_, H_ + 1)
            act.wait_ge(S_["z_coef"], 1)

            spd = [i for i, l in enumerate(loads) if l[0] == "sq" and l[1] == "Wpd"]
            sw = [i for i, l in enumerate(loads) if l[0] == "sq" and l[1] == "W"]
            for t in range(NT):
                m = rows(t, N)
                act.wait_ge(S_["z_mm"], t + 1)
                if t == 0:
                    act.wait_ge(S_["h_lo"], 3 * MT)
                for j in range(2):
                    i = 2 * t + j
                    if i >= 2:
                        act.wait_ge(S_["z_lo"], i - 1)
                    A(val[0:m, i % 2, :], bank[2 * (t % 3) + j][0:m, :], ACT.Copy, scale=zcoef[0:m, t:t + 1])\
                        .then_inc(S_["z_val"], 1)
                    act.wait_ge(S_["z_val"], i + 1)
                    A(z[0][0:m, t, j * 512:(j + 1) * 512], val[0:m, i % 2, :], ACT.Copy).then_inc(S_["z_hi"], 1)
                if t < 4:
                    for k in (2 * t, 2 * t + 1):
                        square(spd[k])
                for k in {4: (0, 1, 2), 5: (3, 4, 5), 6: (6, 7)}.get(t, ()):
                    square(sw[k])
                if t == 6:
                    act.wait_ge(S_["stage_sq"], squares[-1])
                    link(add_up(PD_, wpd_ss))
                    add_up(WW_, w_ss).then_inc(S_["norm_in"], 1)
                    noted("norm_in", 5)
            norm(5, PD_, WW_ + 1)
            act.wait_ge(S_["f_coef"], 1)

            def yT_hi_tile(t):
                m = rows(t, N)
                for j in range(2):
                    act.wait_ge(S_["yt_mm"], 2 * t + j + 1)
                    A(yT_hi[:, 4 * j:4 * j + 4, t * P:t * P + m],
                      bank[6 + j][:, :].rearrange("p (k d) -> p k d", k=4)[:, :, 0:m], ACT.Copy)\
                        .then_inc(S_["yt_hi"], 1)

            npd = [i for i, l in enumerate(loads) if l[0] == "split" and l[1] == "Wpd"]
            for t in range(NT):
                m = rows(t, N)
                act.wait_ge(S_["ln_var"], t + 1)
                A(lnr[0:m, 0:1], mv[0:m, 1:2], ACT.Sqrt, bias=eps_c[0:m, :]).then_inc(S_["ln_std"], 1)
                act.wait_ge(S_["ln_coef"], t + 1)
                if t == 0:
                    act.wait_ge(S_["z_lo"], 2 * NT)
                else:
                    act.wait_ge(S_["yt_mm"], 2 * t)
                A(val[0:m, :, :].rearrange("p a b -> p (a b)"), x2[0:m, t, :], ACT.Identity, bias=lnr[0:m, 3:4],
                  scale=lnr[0:m, 2:3]).then_inc(S_["y_made"], 1)
                if t >= 1:
                    yT_hi_tile(t - 1)
                if t < 4:
                    for k in (2 * t, 2 * t + 1):
                        split_hi(npd[k])
                if t == 4:
                    act.wait_ge(S_["sim_in"], 48)
                    note_free()
                    for e in range(NEXP):
                        link(A(junk[:, 0:PROJ], sim_bc[:, e, :], ACT.Square, accum_out=simss[:, e:e + 1]))
                    last_note[0] = None
                    A(simr, simss, ACT.Sqrt).then_inc(S_["sim_norm"], 1)
            yT_hi_tile(NT - 1)

            nw = [i for i, l in enumerate(loads) if l[0] == "split" and l[1] == "W"]
            act.wait_ge(S_["o_mm"], NT)
            for t in range(NT):
                m = rows(t, N)
                if t < FT // 2:
                    for k in (2 * t, 2 * t + 1):
                        split_hi(nw[k])
                act.wait_ge(S_["p_val"], t + 1)
                note_free()
                A(junk[0:m, 0:PROJ], pr[0:m, t, :], ACT.Square, accum_out=pss[0:m, t:t + 1])\
                    .then_inc(S_["p_sq"], 1)
                noted("p_sq", t + 1)
                if t == FT:
                    act.wait_ge(S_["wu_in"], 48)
                    note_free()
                    A(junk[0:R, 0:D], wu_raw[0:R, :], ACT.Square, accum_out=sums[0:R, WU_:WU_ + 1])\
                        .then_inc(S_["norm_in"], 1)
                    noted("norm_in", 6)
            act.wait_ge(S_["p_sq"], NT)
            A(pnorm, pss, ACT.Sqrt).then_inc(S_["p_norm"], 1)
            A(tempe, tempv, ACT.Exp).then_inc(S_["temp_exp"], 1)
            act.wait_ge(S_["exp_in"], 1)
            A(ex, logit, ACT.Exp).then_inc(S_["exp_out"], 1)
            norm(6, WU_, WU_ + 1)

        @block.tensor
        def _(pe):
            T = nc.tensor

            pe.wait_ge(S_["consts"], NCONST)
            pe.wait_ge(S_["chunk_ends"], 1)
            for k in range(2):
                for j in range(CG):
                    ins = T.matmul(bank[5 + k][0:NWIN, j * P:(j + 1) * P],
                                   ends16[:, k, j:j + 1].to_broadcast([P, NWIN]), ident16[:], start=True, stop=True)
            ins.then_inc(S_["range_done"], 1)
            pe.wait_ge(S_["member_in"], 16)
            pe.wait_ge(S_["start_made"], 1)
            T.matmul(bank[4][:, 0:NSLOT], start16[0:NWIN + 1, 0:1].to_broadcast([NWIN + 1, P]),
                     member_sb[0:NWIN + 1, :], start=True, stop=True).then_inc(S_["slot_rows"], 1)
            pe.wait_ge(S_["range_cols"], 1)
            T.matmul(bank[7][0:1, 0:1], badc[0:NWIN, 0:1], ones[0:NWIN, 0:1], start=True, stop=True)\
                .then_inc(S_["flag_sum"], 1)

            def close_window(j, t):
                T.matmul(bank[j][:, bass.ds(t * W, W)], ident16[:], ident16[:, j * W:(j + 1) * W],
                         start=False, stop=True, skip_group_check=True).then_inc(S_["win_done"], 1)

            def open_window(j):
                T.matmul(bank[j][:, 0:W], ident16[:], zero16[:], start=True, stop=False, skip_group_check=True)

            def subtract(w, j):
                pe.wait_ge(S_["adj_made"], w + 1)
                T.matmul(bank[j][:, 0:KEYS], minus16[:], adj[:, :, bass.ds(w * W, W)], start=False, stop=True,
                         skip_group_check=True).then_inc(S_["sub_done"], 1)

            def degrees(g, parts):
                if len(parts) == 2:
                    pe.wait_ge(S_["rest_made"], WPT * (g + 1))
                else:
                    pe.wait_ge(S_["adj_made"], WPT * (g + 1))
                if g:
                    pe.wait_ge(S_["degree_out"], g)
                for i, a in enumerate(parts):
                    for t in range(NT):
                        ins = T.matmul(bank[7][:, g:g + 1], a[:, t, g * P:(g + 1) * P], ones16[:, 0:1],
                                       start=(i == 0 and t == 0), stop=(i == len(parts) - 1 and t == NT - 1))
                ins.then_inc(S_["deg_done"], 1)

            pe.wait_ge(S_["flag_set"], 1)
            bad = pe.value_load(flag_i[0:1, 0:1], min_val=0, max_val=2 * NWIN)
            with pe.If(bad == 0):
                def gather_features(b):
                    m = rows(b, NSLOT)
                    for j in range(CG):
                        ins = T.matmul(bank[b][0:m, 0:3 * P], pick_slot[:, j, b * P:b * P + m],
                                       feat[:, j].rearrange("p k e -> p (k e)"), start=(j == 0), stop=(j == CG - 1))
                    ins.then_inc(S_["feat_mm"], 1)

                feat_count = [0, 0]

                def scores(g):
                    i = KG * g // FSLOT
                    if KG * g % FSLOT == 0:
                        feat_count[i % 2] += 3 * len(feature_pieces(i))
                        pe.wait_ge(feat_in[i % 2], 16 * feat_count[i % 2])
                    if g >= 2:
                        pe.wait_ge(S_["src_made"], g - 1)
                    for c in range(KG * g, min(KG * g + KG, NSLOT)):
                        q = c % KG * P
                        f = (c - i * FSLOT) * P
                        ins = T.matmul(bank[5 + g % 2][:, q:q + P], feat_rows[:, i % 2, f:f + P], line16[:],
                                       start=True, stop=True)
                    ins.then_inc(S_["score_made"], 1)

                pe.wait_ge(S_["feat_made"], 3)
                pe.wait_ge(S_["slots_picked"], 1)
                gather_features(0)
                pe.wait_ge(S_["keys_ready"], 2)
                for h in range(2):
                    for j in range(CG):
                        ins = T.matmul(bank[4][:, 0:NSLOT], keys[:, h, j, :], pick_slot[:, j, :],
                                       start=(h == 0 and j == 0), stop=(h == 1 and j == CG - 1))
                ins.then_inc(S_["turned"], 1)
                for b in range(1, NBLK):
                    gather_features(b)
                pe.wait_ge(S_["line_in"], 16)
                pe.wait_ge(S_["feat_out"], NBLK)
                for g in range(AHEAD):
                    scores(g)
                for w in range(NWIN):
                    j = w % WPT
                    if w >= WPT:
                        pe.wait_ge(S_["adj_made"], w - WPT + 1)
                        if w - WPT in REST_WINS:
                            pe.wait_ge(S_["rest_made"], w - WPT + 1)
                    for n in range(WFIRST[w], WFIRST[w + 1]):
                        if n % KG == 0:
                            if n // KG + AHEAD < NG:
                                scores(n // KG + AHEAD)
                            for g in DEG_AT.get(n // KG, ()):
                                degrees(g, (adj, adj_rest) if g < REST_TILES else (adj,))
                            pe.wait_ge(S_["src_made"], n // KG + 1)
                            pe.wait_ge(S_["key_made"], n // KG + 1)
                        ins = T.matmul(bank[j][:, 0:KEYS], src_hot[:, n % SRING, :], key_hot[:, n % KRING, :],
                                       start=(n == WFIRST[w]), stop=False, skip_group_check=True)
                        if n % KG == KG - 1:
                            ins.then_inc(S_["key_used"], 1)
                    close_window(j, w // WPT)
                    if w - 1 in REST_WINS:
                        subtract(w - 1, (w - 1) % WPT)
                for g in DEG_AT[NG]:
                    degrees(g, (adj,))
                pe.wait_ge(S_["rest_zero"], 1)
                pe.wait_ge(S_["adj_made"], NWIN)
                pe.wait_ge(S_["rest_made"], len(REST_WINS))
            with pe.Else():
                pe.wait_ge(S_["feat_made"], 3)
                pe.wait_ge(S_["keys_ready"], 2)
                pe.wait_ge(S_["slots_picked"], 1)
                for i, parts in enumerate(((keys[:, 0], keys[:, 1]), (feat[:, :, 2],))):
                    for j in range(CG):
                        for h, v in enumerate(parts):
                            ins = T.matmul(bank[4 + i][:, j * P:(j + 1) * P], v[:, j, :], ident16[:],
                                           start=(h == 0), stop=(h == len(parts) - 1))
                    ins.then_inc(S_["turned"], 1)
                pe.sem_inc(S_["slow_used"], 1)

                def slow_windows(g):
                    for j in range(WPT):
                        w = WPT * g + j
                        open_window(j)
                        with pe.Fori(0, NCH) as c:
                            pe.wait_ge(S_["slow_made"], w * NCH + c + 1)
                            T.matmul(bank[j][:, 0:KEYS], src_hot[:, 0, :], key_hot[:, 0, :], start=False, stop=True,
                                     skip_group_check=True).then_inc(S_["slow_used"], 1)
                        close_window(j, g)
                        subtract(w, j)

                slow_windows(0)
                with pe.Fori(1, NT) as g:
                    pe.wait_ge(S_["rest_made"], WPT * g)
                    slow_windows(g)
                for g in range(NT):
                    degrees(g, (adj, adj_rest))
                pe.wait_ge(S_["rest_made"], NWIN)

            def norm_mm(n, q0, q1):
                pe.wait_ge(S_["norm_in"], n)
                if n == 1:
                    pe.wait_ge(S_["bcast_used"], 3)
                else:
                    pe.wait_ge(S_["norm_done"], n - 1)
                T.matmul(bank[7][:, 0:q1 - q0], ones[:], sums[:, q0:q1], start=True, stop=True)\
                    .then_inc(S_["norm_sum"], 1)

            def t1_group(f, t, last=False):
                m = rows(t, N)
                for p, xp in enumerate((xs_hi, xs_lo)):
                    for j, (n0, n) in enumerate(DSPLIT):
                        ins = T.matmul(bank[3 * (f % 2) + j][:, 0:n], xp[0:m, t, f * P:(f + 1) * P],
                                       adj[0:m, t, n0:n0 + n], start=(t == 0 and p == 0), stop=(last and p == 1),
                                       skip_group_check=True)
                return ins

            def t1_rest(f):
                with pe.If(big > 0):
                    for t in range(NT):
                        m = rows(t, N)
                        for xp in (xs_hi, xs_lo):
                            for j, (n0, n) in enumerate(DSPLIT):
                                T.matmul(bank[3 * (f % 2) + j][:, 0:n], xp[0:m, t, f * P:(f + 1) * P],
                                         adj_rest[0:m, t, n0:n0 + n], start=False, stop=False, skip_group_check=True)

            big = None
            for f in range(FT):
                if f >= 2:
                    pe.wait_ge(S_["t1_val"], 3 * (f - 1))
                for t in range(NT):
                    if f == 0:
                        if t < POOL_LO:
                            pe.wait_ge(S_["xlo_made"], t + 1)
                        else:
                            pe.wait_ge(S_["xlo_made_v"], t + 1 - POOL_LO)
                    if f == 0 and t == 5:
                        pe.wait_ge(S_["big_col"], 1)
                        T.matmul(bank[6][0:1, 0:1], bigc[:, 0:1], ones[:, 0:1], start=True, stop=True)\
                            .then_inc(S_["big_sum"], 1)
                    if t == NT - 1:
                        if f == 0:
                            pe.wait_ge(S_["big_set"], 1)
                            big = pe.value_load(flag_i[0:1, 1:2], min_val=0, max_val=P)
                        t1_rest(f)
                    ins = t1_group(f, t, t == NT - 1)
                ins.then_inc(S_["t1_mm"], 1)
                if f == 0:
                    for j in range(3):
                        pe.wait_ge(S_["diag_made"], j + 1)
                        if j == 2:
                            pe.wait_ge(S_["bcast_used"], 1)
                        for i in range(4 * j, min(4 * j + 4, NT)):
                            q = (i % 4) * P
                            ins = T.matmul(bank[6 + j % 2][:, q:q + P], ones[:], val[:, j % 2, q:q + P],
                                           start=True, stop=True)
                        ins.then_inc(S_["bcast_made"], 1)
                if f == 3:
                    norm_mm(1, W1_, B1_ + 1)

            for mt in range(MT):
                m = rows(mt, MID)
                if mt < 2:
                    pe.wait_ge(S_["t1_val"], 3 * (FT - 1 + mt))
                else:
                    pe.wait_ge(S_["h_val"], 3 * (mt - 1))
                for k in range(FT):
                    if mt == 0:
                        pe.wait_ge(S_["t1_lo"], 3 * (k + 1))
                        pe.wait_ge(S_["stage_lo"], 2 * (k + 1))
                    for q, (wp, tp) in enumerate(((0, 0), (0, 1), (1, 0))):
                        for j, (n0, n) in enumerate(DSPLIT):
                            ins = T.matmul(bank[3 * (mt % 2) + j][0:m, 0:n], w1_slot[mt][:, wp, k, 0:m],
                                           t1T[tp][:, k, n0:n0 + n], start=(k == 0 and q == 0),
                                           stop=(k == FT - 1 and q == 2))
                ins.then_inc(S_["h_mm"], 1)
                if mt == 0:
                    norm_mm(2, T1_, T1_ + 1)
                if mt == 6:
                    norm_mm(3, W2_, W2_ + 1)

            for t in range(NT):
                m = rows(t, N)
                if t < 3:
                    pe.wait_ge(S_["h_val"], 3 * (MT - 1 + min(t, 1)))
                else:
                    pe.wait_ge(S_["z_val"], 2 * (t - 2))
                for k in range(MT):
                    K = rows(k, MID)
                    if t == 0:
                        pe.wait_ge(S_["h_lo"], 3 * (k + 1))
                        pe.wait_ge(S_["stage_lo"], 2 * FT + k + 1)
                    for q, (hp, wp) in enumerate(((0, 0), (0, 1), (1, 0))):
                        for j in range(2):
                            ins = T.matmul(bank[2 * (t % 3) + j][0:m, :], hT[hp][0:K, k, t * P:t * P + m],
                                           w2_slot[k][0:K, wp, j * 512:(j + 1) * 512], start=(k == 0 and q == 0),
                                           stop=(k == MT - 1 and q == 2))
                ins.then_inc(S_["z_mm"], 1)
                if t == 0:
                    norm_mm(4, H_, H_ + 1)
                if t == 8:
                    norm_mm(5, PD_, WW_ + 1)

            def turn(t):
                m = rows(t, N)
                pe.wait_ge(S_["y_made"], t + 1)
                if t == 0:
                    pe.wait_ge(S_["norm_done"], 5)
                for j in range(2):
                    if t >= 1:
                        pe.wait_ge(S_["yt_lo"], 2 * (t - 1) + j + 1)
                    for i in range(4):
                        k = 4 * j + i
                        ins = T.transpose(bank[6 + j][:, i * P:i * P + m], val[0:m, k // 4, i * P:(i + 1) * P],
                                          ident[0:m, 0:m])
                    ins.then_inc(S_["yt_mm"], 1)

            def conv2(t, s, a, first, last):
                m, K = rows(t, N), rows(s, N)
                for p in range(2):
                    for j in range(2):
                        ins = T.matmul(bank[2 * ((t + 1) % 3) + j][0:m, :], a[0:K, s, t * P:t * P + m],
                                       z[p][0:K, s, j * 512:(j + 1) * 512], start=(first and p == 0),
                                       stop=(last and p == 1), skip_group_check=True)
                return ins

            for t in range(NT):
                if t < 3:
                    pe.wait_ge(S_["z_val"], 2 * (NT - 2 + t))
                else:
                    pe.wait_ge(S_["x2_done"], t - 2)
                for s in range(NT):
                    if t == 0:
                        pe.wait_ge(S_["z_lo"], 2 * s + 2)
                    if s == NT - 1:
                        with pe.If(big > 0):
                            pe.wait_ge(S_["rest_in"], 16)
                            for s2 in range(NT):
                                conv2(t, s2, rest2, False, False)
                    ins = conv2(t, s, adj, s == 0, s == NT - 1)
                ins.then_inc(S_["o_mm"], 1)
                if t >= 1:
                    turn(t - 1)

            def project(t):
                m = rows(t, N)
                b = bank[(t + 4) % 6]
                pe.wait_ge(S_["x2_done"], min(NT, 8 + t // 2))
                if t >= 6:
                    pe.wait_ge(S_["p_used"], t - 5)
                pe.wait_ge(S_["yt_lo"], 2 * t + 2)
                for k in range(FT):
                    for q, (yp, wp) in enumerate(((yT_hi, wpd_hi), (yT_hi, wpd_lo), (yT_lo, wpd_hi))):
                        ins = T.matmul(b[0:m, 0:PD], yp[:, k, t * P:t * P + m], wp[:, k, :],
                                       start=(k == 0 and q == 0), stop=(k == FT - 1 and q == 2))
                ins.then_inc(S_["p_mm"], 1)

            pe.wait_ge(S_["stage_lo"], 2 * FT + MT + FT)
            for t in range(NT):
                if t == 2:
                    turn(NT - 1)
                project(t)

            def base(t):
                m = rows(t, N)
                q0 = 4 * ((t + 1) % 2)
                if t < 2:
                    pe.wait_ge(S_["p_used"], (8, NT)[t])
                else:
                    pe.wait_ge(S_["res_half"], 2 * (t - 1))
                for k in range(FT):
                    if t == 0:
                        pe.wait_ge(S_["stage_lo"], 2 * FT + MT + FT + k + 1)
                    for q, (yp, wp) in enumerate(((yT_hi, w_hi), (yT_hi, w_lo), (yT_lo, w_hi))):
                        for j in range(2):
                            ins = T.matmul(bank[q0 + j][0:m, :], yp[:, k, t * P:t * P + m],
                                           wp[:, k, j * 512:(j + 1) * 512], start=(k == 0 and q == 0),
                                           stop=(k == FT - 1 and q == 2))
                ins.then_inc(S_["b_mm"], 1)

            def low_rank(t):
                m = rows(t, N)
                q0 = 4 * ((t + 1) % 2)
                if t >= 2:
                    pe.wait_ge(S_["res_made"], t - 1)
                for j in range(2):
                    ins = T.matmul(bank[q0 + 2 + j][0:m, :], gT[0:GP, t, 0:m], wu[0:GP, j * 512:(j + 1) * 512],
                                   start=True, stop=True)
                ins.then_inc(S_["l_mm"], 1)

            base(0)
            norm_mm(6, WU_, WU_ + 1)
            base(1)
            pe.wait_ge(S_["norm_done"], 6)
            pe.wait_ge(S_["g_made"], 1)
            pe.wait_ge(S_["yt_lo"], 2 * NT)
            for i in range(NT):
                ins = T.transpose(bank[6 + i // 5][:, :].bitcast(F16)[0:GP, (i % 5) * P:(i % 5 + 1) * P],
                                  g_rows[:, i, :], ident16[:])
            ins.then_inc(S_["gt_mm"], 1)
            pe.wait_ge(S_["gt_made"], 1)
            pe.wait_ge(S_["wu_done"], 1)
            low_rank(0)
            low_rank(1)
            for t in range(2, NT):
                base(t)
                low_rank(t)


def square_line():
    l = np.arange(P)
    out = np.zeros((P, P), np.float16)
    out[0], out[1], out[2], out[3], out[4] = -1, -1, 2 * l, -(l * l // 16 * 16), 1 - l * l % 16
    return out


def slot_members():
    out = np.zeros((NWIN + 1, NSLOT), np.float16)
    for w in range(NWIN):
        out[w, WFIRST[w]:WFIRST[w + 1]] = 1
        out[NWIN, WFIRST[w]:WFIRST[w + 1]] = np.arange(WSLOTS[w])
    return out


def kernel(**inputs):
    import concourse.bacc as _bacc
    from concourse.bass_utils import run_bass_kernel_spmd as _run

    g = {k: np.asarray(v) for k, v in inputs.items()}
    pad = CROWS * P - E
    w1 = np.zeros((D, MIDP), np.float32)
    w1[:, :MID] = g["L0_gnn_W1"]
    b1 = np.zeros(MIDP, np.float32)
    b1[:MID] = g["L0_gnn_b1"]
    arrays = {
        "x": g["x"],
        "src": np.concatenate([g["src"], np.zeros(pad, g["src"].dtype)]).reshape(CROWS, P),
        "dst": np.concatenate([g["dst"], np.full(pad, NWIN * W, g["dst"].dtype)]).reshape(CROWS, P),
        "ranges": np.array([[n + CROWS] for n in WSLOTS], np.float32),
        "line": square_line(),
        "member": slot_members(),
        "W1": w1, "b1": b1.reshape(MT, P).T, "W2": g["L0_gnn_W2"], "b2": g["L0_gnn_b2"],
        "WT": g["L0_ffn_W"].T,
        "WpdT": np.concatenate([g["L0_ffn_Wp"]] + [g[f"L0_ffn_Wd{i}"] for i in range(NEXP)]).T,
        "bp": g["L0_ffn_bp"], "simT": g["L0_ffn_sim"].T, "temp": g["L0_ffn_temp"],
        "WuT": np.concatenate([g[f"L0_ffn_Wu{i}"].T for i in range(NEXP)]),
    }
    arrays = {k: np.ascontiguousarray(v) for k, v in arrays.items()}
    nc = _bacc.Bacc("TRN2", target_bir_lowering=False, num_devices=1)
    args = [nc.dram_tensor("in_" + k, v.shape, mybir.dt.from_np(v.dtype), kind="ExternalInput").ap()
            for k, v in arrays.items()]
    o = nc.dram_tensor("out", (N, D), F32, kind="ExternalOutput").ap()
    build(nc, *args, o)
    r = _run(nc, [{"in_" + k: v for k, v in arrays.items()}], core_ids=[0])
    return r.results[0]["out"]
```

```python
from contextlib import ExitStack
from math import sqrt

import numpy as np
import concourse.bass as bass
from concourse import mybir

ALU = mybir.AluOpType
ACT = mybir.ActivationFunctionType
F32 = mybir.dt.float32
F16 = mybir.dt.float16
I32 = mybir.dt.int32
AX_X = mybir.AxisListType.X

P = 128
N = 1250
D = 1024
MID = 1500
E = 40000
PROJ = 256
RANKS = (1, 2, 4, 8)
NEXP = len(RANKS)
R = sum(RANKS)
PD = PROJ + R
CLAMP_MAX = float(np.log(1.0 / 0.01))

NT = -(-N // P)
FT = D // P
MT = -(-MID // P)
W = 32
NWIN = NT * P // W
WPT = P // W
KEYS = NT * W
NCH = -(-E // P)
CG = -(-NCH // P)
CROWS = CG * P
DSPLIT = [(0, 417), (417, 417), (834, 416)]
MIDP = MT * P
HALF = MIDP // 2
GP = 96

X_SCALE = 1024.0
T1_SCALE = 8.0

KG = 4
KRING = 16
SRING = 48
SLOTS = MT + 1


def rows(t, n):
    return min(P, n - t * P)


def window_slots():
    out = []
    for w in range(NWIN):
        u0, u1 = (min(1.0, sqrt(v * W / N)) for v in (w, w + 1))
        p = u1 - u0
        out.append(int(E * p + 5 * sqrt(E * p * (1 - p)) + P - 2) // P + 1)
    return out


WSLOTS = window_slots()
WFIRST = [sum(WSLOTS[:w]) for w in range(NWIN + 1)]
NSLOT = WFIRST[NWIN]
assert NSLOT <= 512
WBANKS = 3
NG = -(-NSLOT // KG)
NBLK = -(-NSLOT // P)
REST_WINS = [w for w in range(NWIN) if P * WSLOTS[w] + 1 > 2048]
REST_TILES = 1 + max(REST_WINS) // WPT
assert REST_WINS == list(range(WPT * REST_TILES))

FSLOT = 24
NF = -(-NSLOT // FSLOT)
SG = 8
NSG = -(-NSLOT // SG)
AHEAD = 2


def feature_pieces(i):
    out, c, end = [], i * FSLOT, min((i + 1) * FSLOT, NSLOT)
    while c < end:
        n = min(end - c, P - c % P)
        out.append((c // P, c % P, n, (c - i * FSLOT) * P))
        c += n
    return out


def by_group(pairs):
    out = {NG: []}
    for group, item in pairs:
        out.setdefault(min(group, NG), []).append(item)
    return out


def tile_ends(tiles, later):
    return [(WFIRST[WPT * g + WPT + (g < REST_TILES)] // KG + later, g) for g in tiles]


ACT_STATS = 5
STATS_AT = by_group((2 + 7 * t, t) for t in range(ACT_STATS))
BN_AT = by_group((4 + 7 * (t - ACT_STATS), t) for t in range(ACT_STATS, NT))
STATS_END = 38
POOL_LO = 6
BATCHES = ((0, 2), (2, 4), (4, 6), (6, 8))
LAST = 8
DEG_AT = by_group(tile_ends(range(NT), 3))
OUT_AT = by_group(tile_ends(range(NT), 4))
HI_AT = by_group((max(STATS_END + 8, group) + 3 * (g - b0), g) for b0, b1 in BATCHES for g in range(b0, b1)
                 for group, _ in tile_ends([b1 - 1], 10))
HI_AT[NG] += range(LAST, NT)
SQ_A = 2
SQ_GROUPS = [60 + 16 * i for i in range(SQ_A)]
SQ_AT = by_group((group, i) for i, group in enumerate(SQ_GROUPS))
LOAD_AT = {}
for i, group in enumerate(SQ_GROUPS):
    LOAD_AT.setdefault(min(NF - 1, group // (FSLOT // KG) + 2), []).append(i + 2)
SIM_LATER = 5
SQ1_AT = {0: range(SQ_A, SQ_A + 4), 1: range(SQ_A + 4, SQ_A + 9), 2: range(SQ_A + 9, 2 * FT)}
W1_AT = {f: range(*v) for f, v in {3: (0, 2), 4: (2, 5), 5: (5, 9), 6: (9, 12), 7: (12, 16)}.items()}
W2_AT = {7: (0, 1, 2), 8: (3, 4, 5), 9: (6, 7, 8), 10: (9, 10), 11: (11,)}


def build(nc, x, src_rows, dst_rows, ranges, line, member, W1, b1, W2, b2, WT, WpdT, bp, simT, temp, WuT, out):
    with ExitStack() as ctx:
        def sb(name, shape, dt):
            return ctx.enter_context(nc.sbuf_tensor(name, shape, dt))

        def sem(name):
            return ctx.enter_context(nc.semaphore(name))

        adj = sb("adj", [P, NT, NT * P], F16)
        arena2 = sb("arena2", [P, 2 * NT * D + NT * NT * P], F16)
        arena3 = sb("arena3", [P, SLOTS * 2048], F16)
        arena4 = sb("arena4", [P, 2 * NT * D], F16)

        class Carve:
            def __init__(self, arena, size):
                self.arena, self.at, self.size = arena, 0, size

            def take(self, n, dt=F16):
                words = n * (2 if dt != F16 else 1)
                v = self.arena[:, self.at:self.at + words]
                self.at += words
                assert self.at <= self.size, (self.at, self.size)
                return v if dt == F16 else v.bitcast(dt)

        A2, A3, A4 = 2 * NT * D + NT * NT * P, SLOTS * 2048, 2 * NT * D
        adj_flat = adj[:, :, :].rearrange("p t d -> p (t d)")
        pr = adj_flat[:, 0:2 * NT * PROJ].bitcast(F32).rearrange("p (t n) -> p t n", t=NT)
        extra = [adj_flat[:, 2 * NT * PROJ + 2 * D * i:2 * NT * PROJ + 2 * D * (i + 1)].bitcast(F32) for i in range(3)]
        c = Carve(arena2, A2)
        xs_hi = c.take(NT * D).rearrange("p (t f) -> p t f", t=NT)
        xs_lo = c.take(NT * D).rearrange("p (t f) -> p t f", t=NT)
        adj_rest = c.take(NT * NT * P).rearrange("p (t d) -> p t d", t=NT)
        c = Carve(arena2, A2)
        hT = [c.take(MT * N).rearrange("p (m d) -> p m d", m=MT) for _ in range(2)]
        c = Carve(arena2, A2)
        x2 = c.take(NT * D, F32).rearrange("p (t f) -> p t f", t=NT)
        yT_hi = c.take(FT * NT * P).rearrange("p (k d) -> p k d", k=FT)
        wpd_hi = c.take(FT * PD).rearrange("p (k n) -> p k n", k=FT)
        c = Carve(arena3, A3)
        x_raw = c.take(NT * D, F32).rearrange("p (t f) -> p t f", t=NT)
        feat_rows = c.take(2 * FSLOT * P).rearrange("p (s n) -> p s n", s=2)
        slots = arena3[:, :].rearrange("p (s n) -> p s n", s=SLOTS)
        w1_slot = [slots[:, m + 1, :].rearrange("p (h k n) -> p h k n", h=2, k=FT) for m in range(MT)]
        w2_slot = [slots[:, k, :].rearrange("p (h n) -> p h n", h=2) for k in range(MT)]
        c = Carve(arena3, A3)
        yT_lo = c.take(FT * NT * P).rearrange("p (k d) -> p k d", k=FT)
        wpd_lo = c.take(FT * PD + 8)[:, 0:FT * PD].rearrange("p (k n) -> p k n", k=FT)
        at = c.at
        rest2 = c.take(NT * NT * P).rearrange("p (t d) -> p t d", t=NT)
        c.at = at
        w_hi = c.take(FT * D).rearrange("p (k n) -> p k n", k=FT)
        c = Carve(arena4, A4)
        src_hot = c.take(SRING * P).rearrange("p (s n) -> p s n", s=SRING)
        key_hot = c.take(KRING * KEYS).rearrange("p (g n s) -> p g n s", s=KG, n=KEYS)
        feat = c.take(3 * CROWS).rearrange("p (j k e) -> p j k e", j=CG, k=3)
        feat_blk = c.take(3 * NBLK * P).rearrange("p (b k e) -> p b k e", b=NBLK, k=3)
        keys = c.take(2 * CROWS).rearrange("p (h j e) -> p h j e", h=2, j=CG)
        pick_slot = c.take(CG * NSLOT).rearrange("p (j s) -> p j s", j=CG)
        member_sb = c.take(NSLOT + NSLOT % 2 + 2)[:, 0:NSLOT + 1]
        start16, ends16 = c.take(2), c.take(2 * CG).rearrange("p (k j) -> p k j", k=2)
        slot_key = c.take(NG * KG)
        key_iota = c.take(KG * KEYS).rearrange("p (n s) -> p n s", s=KG)
        key_col = c.take(CROWS, F32)
        src_col = c.take(CROWS, F32)
        c = Carve(arena4, A4)
        chunk_up, chunk_down = (c.take(CROWS, F32) for _ in range(2))
        touch = [c.take(CROWS, F32) for _ in range(3)]
        src_i, dst_i, up_i, low_i, win_i, sq_i = (c.take(CROWS, I32).rearrange("p (j e) -> p j e", j=CG)
                                                  for _ in range(6))
        c = Carve(arena4, A4)
        t1T = [c.take(FT * N).rearrange("p (k d) -> p k d", k=FT) for _ in range(2)]
        c = Carve(arena4, A4)
        z = [c.take(NT * D).rearrange("p (t f) -> p t f", t=NT) for _ in range(2)]
        c = Carve(arena4, A4)
        w_lo = c.take(FT * D).rearrange("p (k n) -> p k n", k=FT)
        g_rows = c.take(NT * GP).rearrange("p (t r) -> p t r", t=NT)
        gT = c.take(NT * P).rearrange("p (t d) -> p t d", t=NT)
        res = [c.take(D, F32) for _ in range(2)]
        scratch = c.take(NEXP * PROJ, F32).rearrange("p (e n) -> p e n", e=NEXP)
        down = c.take(NT * R, F32).rearrange("p (t r) -> p t r", t=NT)
        gated = c.take(NT * R, F32).rearrange("p (t r) -> p t r", t=NT)
        wu_raw = c.take(D, F32)
        wu = c.take(D)

        stage = sb("stage", [P, 2, D], F32)
        junk = sb("junk", [P, D], mybir.dt.bfloat16)
        src_low = junk[:, 0:2 * CROWS].bitcast(I32).rearrange("p (j e) -> p j e", j=CG)
        val = sb("val", [P, 2, 512], F32)
        row_bc = sb("row_bc", [P, 1280], F32)
        sim_bc = row_bc[:, 0:D].rearrange("p (e n) -> p e n", e=NEXP)
        bp_bc = row_bc[:, D:D + PROJ]
        ident = sb("ident", [P, P], F32)
        ident16 = sb("ident16", [P, P], F16)
        minus16 = sb("minus16", [P, P], F16)
        ones = sb("ones", [P, P], F32)
        ones16 = sb("ones16", [P, NWIN], F16)
        zero16 = sb("zero16", [P, W], F16)
        line16 = sb("line16", [P, P], F16)
        win_key = sb("win_key", [P, NWIN], F32)
        win_edge = sb("win_edge", [P, 2], F32)
        chunk_row = sb("chunk_row", [P, CG], F32)
        rng_sb = sb("rng_sb", [P, 1], F32)
        flag_i = sb("flag_i", [1, 2], I32)
        cols = sb("cols", [P, 176], F32)
        used_cols = [0]

        def col(n):
            used_cols[0] += n
            assert used_cols[0] <= 176
            return cols[:, used_cols[0] - n:used_cols[0]]

        cmin, cmax, bcol, badc = col(CG), col(CG), col(2), col(2)
        xsum, xss, nmean, rstd = col(NT), col(NT), col(NT), col(NT)
        isd, xscale, xbias = col(NT), col(NT), col(NT)
        degv, ntmp, minus_half, last_root, warm = col(NT), col(5), col(NT), col(NT - LAST), col(1)
        eps_c, bigc, temp_c, tempe = col(1), col(2), col(1), col(1)
        b1c, b1s = col(MT), col(MT)
        small = sb("small", [P, 320], F32)
        used_small = [0]

        def sm(n):
            used_small[0] += n
            assert used_small[0] <= 320
            return small[:, used_small[0] - n:used_small[0]]

        w1_ss, w2_ss, w_ss, wpd_ss = sm(2 * FT), sm(MT), sm(FT), sm(FT)
        t1_ss, h_ss = sm(3 * FT), sm(3 * MT)
        sums = sm(8)
        norms = sm(8)
        bound, pw, ipw, coef = sm(8), sm(8), sm(8), sm(8)
        zcoef, ocoef = sm(NT), sm(NT)
        stats, mv, lnr = sm(12), sm(2), sm(4)
        W1_, B1_, T1_, W2_, H_, PD_, WW_, WU_ = range(8)
        Z_, G_ = B1_, T1_
        C_H, C_P, C_B, C_L = range(4)
        gate = sb("gate", [P, 13, NT, NEXP], F32)
        dots, logit, ex, prob, hit, keep, pick = (gate[:, i] for i in range(7))
        pss, pnorm, gmax, gsum, pscale = (gate[:, 7 + i].rearrange("p t e -> p (t e)")[:, 0:NT] for i in range(5))
        simss, simr, tempv = gate[:, 12, 0], gate[:, 12, 1], gate[:, 12, 2, 0:1]

        psum = ctx.enter_context(nc.psum_tensor("psum", [P, 8 * 512], F32))
        bank = [psum[:, i * 512:(i + 1) * 512] for i in range(8)]
        score = [psum[:, i * 512:(i + 2) * 512] for i in (5, 3)]
        rest_dram = nc.dram_tensor("adj_rest_dram", (P, NT * NT * P), F16, kind="Internal").ap()

        S = {}

        class Sems:
            def __getitem__(self, name):
                if name not in S:
                    S[name] = sem(name)
                return S[name]

        S_ = Sems()
        x_in = [sem(f"x_in{t}") for t in range(NT)]
        xr_in = [sem(f"xr_in{t}") for t in range(NT)]
        feat_in = [sem(f"feat_in{i}") for i in range(2)]
        stage_in = [sem(f"stage_in{i}") for i in range(5)]
        out_done = [sem(f"out_done{i}") for i in range(2)]

        class Link:
            def __init__(self, eng, s):
                self.eng, self.s, self.n = eng, S_[s], 0

            def __call__(self, ins):
                self.n += 1
                ins.then_inc(self.s, 1)
                self.eng.wait_ge(self.s, self.n)

        loads = [("sq", "W1", k, h * HALF, HALF) for k in range(FT) for h in range(2)]
        loads += [("split", "W1", k, h * HALF, HALF) for k in range(FT) for h in range(2)]
        loads += [("sq", "W2", k, 0, D) for k in range(MT)]
        loads += [("split", "W2", k, 0, D) for k in range(MT)]
        loads += [("sq", "Wpd", k, 0, PD) for k in range(FT)]
        loads += [("sq", "W", k, 0, D) for k in range(FT)]
        loads += [("split", "Wpd", k, 0, PD) for k in range(FT)]
        loads += [("split", "W", k, 0, D) for k in range(FT)]
        dram = {"W1": W1, "W2": W2, "Wpd": WpdT, "W": WT}
        nrows = {"W1": D, "W2": MID, "Wpd": D, "W": D}
        squares = [0]
        for kind, *_ in loads:
            squares.append(squares[-1] + (kind == "sq"))

        last_w = next(i for i, l in enumerate(loads) if l[:2] == ("split", "W"))
        buffers = [stage[:, 0, :], stage[:, 1, :]] + extra
        at_buffer, before = [], []
        for i in range(len(loads)):
            b = i % 2
            if i >= last_w:
                b = (last_w % 2, 1 - last_w % 2, 2, 3, 4, last_w % 2, 1 - last_w % 2, 2)[i - last_w]
            same = [k for k, (b2, _) in enumerate(at_buffer) if b2 == b]
            at_buffer.append((b, len(same) + 1))
            before.append(same[-1] if same else None)

        def loaded(eng, i):
            b, number = at_buffer[i]
            eng.wait_ge(stage_in[b], 16 * number)
            return buffers[b]

        def stage_freed(eng, i):
            if loads[i][0] == "sq":
                eng.wait_ge(S_["stage_sq"], squares[i + 1])
            else:
                eng.wait_ge(S_["stage_lo"], i + 1 - squares[i + 1])

        def places(a, k, c0):
            if a == "W1":
                v = arena3[:, :].rearrange("p (s h k n) -> p s h k n", s=SLOTS, h=2, k=FT)
                q = slice(1 + c0 // P, 1 + (c0 + HALF) // P)
                return v[:, q, 0, k, :], v[:, q, 1, k, :], W1_
            if a == "W2":
                return w2_slot[k][:, 0, :], w2_slot[k][:, 1, :], W2_
            if a == "Wpd":
                return wpd_hi[:, k, :], wpd_lo[:, k, :], PD_
            return w_hi[:, k, :], w_lo[:, k, :], WW_

        def invert_root(eng, link, square, out, tmp, root=None):
            if root is None:
                link(eng.tensor_tensor(out, square, minus_half[:, 0:square.shape[1]], ALU.pow))
            else:
                link(eng.reciprocal(out, root))
            link(eng.tensor_tensor(tmp, out, out, ALU.mult))
            link(eng.tensor_tensor(tmp, tmp, square, ALU.mult))
            link(eng.tensor_scalar(tmp, tmp, -0.5, 1.5, ALU.mult, ALU.add))
            link(eng.tensor_tensor(out, out, tmp, ALU.mult))

        def factors(eng, link, g0, g1, root=None):
            c, tmp = slice(g0, g1), ntmp[:, 2 * (g0 >= LAST):2 * (g0 >= LAST) + g1 - g0]
            if root is not None:
                eng.tensor_scalar(root, root, 1.0, None, ALU.max)
            link(eng.tensor_scalar(degv[:, c], degv[:, c], 1.0, None, ALU.max))
            invert_root(eng, link, degv[:, c], isd[:, c], tmp, root)
            link(eng.tensor_tensor(xscale[:, c], isd[:, c], rstd[:, c], ALU.mult))
            link(eng.tensor_scalar(xscale[:, c], xscale[:, c], X_SCALE, None, ALU.mult))
            return eng.tensor_tensor(xbias[:, c], xscale[:, c], nmean[:, c], ALU.mult)

        NCONST = 11
        block = ctx.enter_context(nc.Block())

        @block.sync
        def _(sp):
            sp.dma_start(dst_i[:], dst_rows.rearrange("(j p) e -> p j e", p=P)).then_inc(S_["edges_in"], 16)
            sp.dma_start(src_i[:], src_rows.rearrange("(j p) e -> p j e", p=P)).then_inc(S_["edges_in"], 16)
            sp.dma_start(rng_sb[0:NWIN, :], ranges).then_inc(S_["ranges_in"], 16)
            sp.dma_start(member_sb[0:NWIN + 1, :], member).then_inc(S_["member_in"], 16)
            sp.dma_start(line16[:], line).then_inc(S_["line_in"], 16)
            for t in range(NT):
                m = rows(t, N)
                sp.dma_start(x_raw[0:m, t, :], x[t * P:t * P + m, :]).then_inc(x_in[t], 16)

            def load(i):
                kind, a, k, c0, n = loads[i]
                b = at_buffer[i][0]
                if before[i] is not None:
                    stage_freed(sp, before[i])
                elif b >= 2:
                    sp.wait_ge(S_["o_mm"], NT)
                m = rows(k, nrows[a])
                sp.dma_start(buffers[b][0:m, 0:n], dram[a][k * P:k * P + m, c0:c0 + n])\
                    .then_inc(stage_in[b], 16)

            for i in range(2):
                load(i)
            sp.wait_ge(S_["feat_ones"], 1)
            sp.wait_ge(S_["flag_set"], 1)
            bad = sp.value_load(flag_i[0:1, 0:1], min_val=0, max_val=2 * NWIN)
            with sp.If(bad == 0):
                for i in range(NF):
                    if i >= 2:
                        sp.wait_ge(S_["score_made"], FSLOT // SG * (i - 1))
                    for b, r0, n, at in feature_pieces(i):
                        sp.wait_ge(S_["feat_out"], b + 1)
                        for k in range(3):
                            sp.dma_start(feat_rows[k:k + 1, i % 2, at:at + n * P], feat_blk[r0:r0 + n, b, k, :])\
                                .then_inc(feat_in[i % 2], 16)
                    for k in LOAD_AT.get(i, ()):
                        load(k)
            with sp.Else():
                for i in range(2, SQ_A + 2):
                    load(i)
            second_x = [i for i, l in enumerate(loads) if l[:2] == ("split", "Wpd")][2]
            for i in range(SQ_A + 2, len(loads)):
                if i == second_x:
                    sp.wait_ge(S_["z_mm"], NT)
                    for t in range(NT):
                        m = rows(t, N)
                        sp.dma_start(x2[0:m, t, :], x[t * P:t * P + m, :]).then_inc(xr_in[t], 16)
                load(i)

        @block.gpsimd
        def _(gp):
            gp.memset(ident[:], 0.0).then_inc(S_["consts_z"], 1)
            gp.memset(ident16[:], 0.0).then_inc(S_["consts_z"], 1)
            gp.memset(minus16[:], 0.0).then_inc(S_["consts_z"], 1)
            gp.wait_ge(S_["consts_z"], 3)
            for m, v in ((ident, 1.0), (ident16, 1.0), (minus16, -1.0)):
                gp.affine_select(out=m[:], in_=m[:], compare_op=ALU.not_equal, fill=v, base=0,
                                 pattern=[[-1, P]], channel_multiplier=1).then_inc(S_["consts"], 1)
            for o, pattern, base, mult in ((win_edge[:], [[W, 2]], 0, W), (chunk_row[:], [[P, CG]], 0, 1),
                                           (chunk_up, [[1, CROWS]], 1, 0), (chunk_down, [[-1, CROWS]], CROWS, 0),
                                           (win_key[:], [[KEYS, NWIN]], 0, 0)):
                gp.iota(o, pattern, base=base, channel_multiplier=mult,
                        allow_small_or_imprecise_dtypes=True).then_inc(S_["consts"], 1)
            for o, v in ((zero16[:], 0.0), (ones16[:], 1.0), (ones[:], 1.0)):
                gp.memset(o, v).then_inc(S_["consts"], 1)
            gp.iota(key_iota, [[1, KEYS], [0, KG]], base=0, channel_multiplier=0,
                    allow_small_or_imprecise_dtypes=True).then_inc(S_["iota_made"], 1)
            gp.wait_ge(S_["cleared"], 6)
            gp.dma_start(b1c, b1).then_inc(S_["b1_in"], 16)
            gp.memset(feat_rows, 1.0).then_inc(S_["feat_ones"], 1)
            gp.wait_ge(S_["feat_ones"], 1)

            def source_lo(g):
                m = rows(g, N)
                gp.wait_ge(S_["xhi_made"], g + 1)
                gp.tensor_tensor(xs_lo[0:m, g, :], x_raw[0:m, g, :], xs_hi[0:m, g, :], ALU.subtract)\
                    .then_inc(S_["xlo_made"], 1)

            def invert_std(glink):
                gp.wait_ge(S_["x_ss"], ACT_STATS)
                gp.wait_ge(S_["bn_made"], NT - ACT_STATS)
                glink(gp.tensor_scalar(xss, xss, 1.0 / D, 1e-5, ALU.mult, ALU.add))
                invert_root(gp, glink, xss, rstd, xsum)

            def x_val(g):
                m = rows(g, N)
                gp.tensor_scalar(x_raw[0:m, g, :], x_raw[0:m, g, :], xscale[0:m, g:g + 1], xbias[0:m, g:g + 1],
                                 ALU.mult, ALU.add).then_inc(S_["xval_made"], 1)

            def sources(glink):
                invert_std(glink)
                lo = 0
                for b, (first, _) in enumerate(BATCHES):
                    gp.wait_ge(S_["degree_out"], BATCHES[b][1])
                    glink(factors(gp, glink, *BATCHES[b]))
                    for g in range(*BATCHES[b]):
                        x_val(g)
                    while lo < min(first - 1, POOL_LO):
                        source_lo(lo)
                        lo += 1
                for g in range(lo, POOL_LO):
                    source_lo(g)

            rest_f32 = adj_rest.rearrange("p t d -> p (t d)").bitcast(F32)
            gp.memset(rest_f32, 0.0).then_inc(S_["rest_zero"], 1)
            gp.wait_ge(S_["flag_set"], 1)
            bad = gp.value_load(flag_i[0:1, 0:1], min_val=0, max_val=2 * NWIN)
            with gp.If(bad == 0):
                sources(Link(gp, "link_g"))
                gp.wait_ge(S_["rest_made"], len(REST_WINS))
            with gp.Else():
                gp.wait_ge(S_["rest_made"], NWIN)
                sources(Link(gp, "link_g_slow"))
            gp.wait_ge(S_["rest_zero"], 1)
            gp.dma_start(rest_dram, adj_rest.rearrange("p t d -> p (t d)")).then_inc(S_["spilled"], 16)
            gp.wait_ge(S_["t1_lo"], 3 * FT)
            gp.dma_start(row_bc[:, 0:D], b2.partition_broadcast(P)).then_inc(S_["b2_in"], 16)
            gp.wait_ge(S_["z_mm"], NT)
            gp.wait_ge(S_["spilled"], 16)
            gp.dma_start(rest2.rearrange("p t d -> p (t d)"), rest_dram).then_inc(S_["rest_in"], 16)
            gp.wait_ge(S_["b2_in"], 16)
            for t in range(NT):
                m = rows(t, N)
                gp.wait_ge(xr_in[t], 16)
                gp.tensor_tensor(x2[0:m, t, :], x2[0:m, t, :], row_bc[0:m, 0:D], ALU.add).then_inc(S_["x2_b"], 1)
            gp.wait_ge(S_["x2_b"], NT)
            gp.dma_start(sim_bc[:], simT.partition_broadcast(P)).then_inc(S_["sim_in"], 16)
            gp.dma_start(bp_bc[:], bp.partition_broadcast(P)).then_inc(S_["sim_in"], 16)
            gp.dma_start(temp_c, temp.partition_broadcast(P)).then_inc(S_["sim_in"], 16)
            gp.wait_ge(S_["o_mm"], NT)
            gp.memset(wu_raw[0:GP, :], 0.0).then_inc(S_["link_p"], 1)
            gp.memset(g_rows[:], 0.0).then_inc(S_["link_p"], 1)
            gp.wait_ge(S_["link_p"], 2)
            for q in range(3):
                gp.dma_start(wu_raw[32 * q:32 * q + R, :], WuT).then_inc(S_["wu_in"], 16)
            gp.wait_ge(S_["wu_in"], 48)
            gp.wait_ge(S_["wu_scaled"], 1)
            ulink = Link(gp, "link_u")
            ulink(gp.tensor_scalar(wu_raw[0:GP, :], wu_raw[0:GP, :], pw[0:GP, WU_:WU_ + 1], None, ALU.mult))
            ulink(gp.tensor_copy(wu[0:GP, :], wu_raw[0:GP, :]))
            gp.tensor_tensor(wu[32:64, :], wu_raw[32:64, :], wu[32:64, :], ALU.subtract).then_inc(S_["wu_done"], 1)
            for t in range(NT - 1):
                gp.wait_ge(S_["res_made"], t + 1)
                gp.dma_start(out[t * P:t * P + P, :], res[t % 2]).then_inc(out_done[t % 2], 16)
            t = NT - 1
            m = rows(t, N)
            for j in range(2):
                c = slice(j * 512, (j + 1) * 512)
                gp.wait_ge(S_["res_made"], NT + j)
                gp.dma_start(out[t * P:t * P + m, c], res[t % 2][0:m, c]).then_inc(out_done[t % 2], 16)
            gp.wait_ge(out_done[(t + 1) % 2], 16 * (NT // 2))
            gp.wait_ge(out_done[t % 2], 16 * (NT // 2 + 1))

        @block.vector
        def _(dve):
            V = nc.vector
            link = Link(dve, "link_v")

            for o, v in ((cols[:], 0.0), (small[:], 0.0), (gate[:], 0.0), (start16, 1.0)):
                V.memset(o, v).then_inc(S_["cleared"], 1)
            dve.wait_ge(S_["cleared"], 4)
            V.memset(eps_c, 1e-5).then_inc(S_["cleared"], 1)
            V.memset(minus_half, -0.5).then_inc(S_["cleared"], 1)
            dve.wait_ge(S_["edges_in"], 32)
            V.tensor_reduce(cmin, dst_i, AX_X, ALU.min)
            link(V.tensor_reduce(cmax, dst_i, AX_X, ALU.max))
            V.tensor_copy(ends16[:, 0, :], cmin)
            V.tensor_copy(ends16[:, 1, :], cmax).then_inc(S_["chunk_ends"], 1)
            link(V.tensor_scalar(low_i, src_i, P - 1, None, ALU.bitwise_and))
            V.tensor_tensor(sq_i, low_i, low_i, ALU.mult).then_inc(S_["sources_cut"], 1)

            dve.wait_ge(S_["consts"], NCONST)
            dve.wait_ge(S_["range_done"], 1)
            q = slice(0, NWIN)
            link(V.tensor_scalar(touch[0][q, :], bank[5][q, 0:CROWS], win_edge[q, 1:2], None, ALU.is_lt))
            link(V.scalar_tensor_tensor(touch[1][q, :], bank[6][q, 0:CROWS], win_edge[q, 0:1], touch[0][q, :],
                                        ALU.is_ge, ALU.mult))
            V.tensor_tensor(touch[0][q, :], touch[1][q, :], chunk_down[q, :], ALU.mult)
            link(V.tensor_tensor(touch[2][q, :], touch[1][q, :], chunk_up[q, :], ALU.mult))
            link(V.tensor_reduce(bcol[q, 1:2], touch[0][q, :], AX_X, ALU.max))
            V.tensor_scalar(start16[q, 0:1], bcol[q, 1:2], -1.0, float(CROWS), ALU.mult, ALU.add)\
                .then_inc(S_["start_made"], 1)
            link(V.tensor_reduce(bcol[q, 0:1], touch[2][q, :], AX_X, ALU.max))
            dve.wait_ge(S_["ranges_in"], 16)
            V.scalar_tensor_tensor(badc[q, 0:1], bcol[q, 0:1], bcol[q, 1:2], rng_sb[q, :], ALU.add, ALU.is_gt)\
                .then_inc(S_["range_cols"], 1)
            dve.wait_ge(S_["flag_sum"], 1)
            V.tensor_copy(flag_i[0:1, 0:1], bank[7][0:1, 0:1]).then_inc(S_["flag_set"], 1)
            dve.wait_ge(S_["sources_cut"], 1)
            V.tensor_scalar(src_low, sq_i, 15, None, ALU.bitwise_and).then_inc(S_["sources_cut"], 1)
            dve.wait_ge(S_["sources_cut"], 2)
            V.tensor_tensor(feat[:, :, 0, :], sq_i, src_low, ALU.subtract).then_inc(S_["feat_made"], 1)
            dve.wait_ge(S_["slot_rows"], 1)
            for j in range(CG):
                ins = V.tensor_scalar(pick_slot[:, j, :], bank[4][:, 0:NSLOT], float(CROWS - 1),
                                      chunk_row[:, j:j + 1], ALU.min, ALU.is_equal)
            ins.then_inc(S_["slots_picked"], 1)
            V.tensor_scalar(win_i, dst_i, W.bit_length() - 1, None, ALU.logical_shift_right).then_inc(S_["dst_cut"], 1)
            V.tensor_scalar(up_i, src_i, P.bit_length() - 1, None, ALU.logical_shift_right)
            link(V.tensor_scalar(dst_i, dst_i, W - 1, None, ALU.bitwise_and))
            V.scalar_tensor_tensor(keys[:, 0], up_i, float(W), dst_i, ALU.mult, ALU.add).then_inc(S_["keys_ready"], 1)
            dve.wait_ge(S_["flag_set"], 1)

            def x_val(g):
                m = rows(g, N)
                V.tensor_scalar(x_raw[0:m, g, :], x_raw[0:m, g, :], xscale[0:m, g:g + 1], xbias[0:m, g:g + 1],
                                ALU.mult, ALU.add).then_inc(S_["xval_made_v"], 1)

            def source_lo(g):
                m = rows(g, N)
                dve.wait_ge(S_["xhi_made"], g + 1)
                V.tensor_tensor(xs_lo[0:m, g, :], x_raw[0:m, g, :], xs_hi[0:m, g, :], ALU.subtract)\
                    .then_inc(S_["xlo_made_v"], 1)

            def x_stats(t, link):
                m = rows(t, N)
                dve.wait_ge(x_in[t], 16)
                for j in range(2):
                    ins = V.bn_stats(stats[0:m, 6 * j:6 * j + 6], x_raw[0:m, t, j * 512:(j + 1) * 512])
                link(ins)
                link(V.bn_aggr(mv[0:m, :], stats[0:m, :].rearrange("p (a b) -> p a b", a=2)))
                V.tensor_scalar(nmean[0:m, t:t + 1], mv[0:m, 0:1], -1.0, None, ALU.mult)
                V.tensor_scalar(xss[0:m, t:t + 1], mv[0:m, 1:2], float(D), None, ALU.mult).then_inc(S_["bn_made"], 1)

            def short_path():
                link = Link(dve, "link_fast")
                dve.wait_ge(S_["turned"], 1)
                if NG * KG > NSLOT:
                    V.memset(slot_key[:, NSLOT:], 0.0)
                V.tensor_copy(slot_key[:, 0:NSLOT], bank[4][:, 0:NSLOT]).then_inc(S_["turned_used"], 1)
                dve.wait_ge(S_["turned_used"], 1)
                for g in range(NG):
                    for t in BN_AT.get(g, ()):
                        x_stats(t, link)
                    if g * KG >= KRING:
                        dve.wait_ge(S_["key_used"], g - KRING // KG + 1)
                    V.tensor_tensor(key_hot[:, g % (KRING // KG)], key_iota,
                                    slot_key[:, KG * g:KG * g + KG].unsqueeze(1).to_broadcast([P, KEYS, KG]),
                                    ALU.is_equal).then_inc(S_["key_made"], 1)

            def long_path():
                link = Link(dve, "link_slow")
                for i, c in enumerate((key_col, src_col)):
                    dve.wait_ge(S_["turned"], i + 1)
                    V.tensor_copy(c[:, 0:CROWS], bank[4 + i][:, 0:CROWS]).then_inc(S_["turned_used"], 1)
                dve.wait_ge(S_["turned_used"], 2)
                with dve.Fori(0, NWIN) as w:
                    with dve.Fori(0, NCH) as c:
                        dve.wait_ge(S_["slow_used"], w * NCH + c + 1)
                        V.tensor_scalar(src_hot[:, 0, :], key_iota[:, 0:P, 0], src_col[:, bass.ds(c, 1)], None,
                                        ALU.is_equal)
                        V.tensor_scalar(key_hot[:, 0, :, 0], key_iota[:, :, 0], win_key[:, bass.ds(w, 1)],
                                        key_col[:, bass.ds(c, 1)], ALU.add, ALU.is_equal)\
                            .then_inc(S_["slow_made"], 1)
                for t in range(ACT_STATS, NT):
                    x_stats(t, link)

            dve.wait_ge(S_["iota_made"], 1)
            bad = dve.value_load(flag_i[0:1, 0:1], min_val=0, max_val=2 * NWIN)
            with dve.If(bad == 0):
                short_path()
            with dve.Else():
                long_path()

            dve.wait_ge(S_["degree_out"], NT)
            dve.wait_ge(S_["xval_made"], LAST)
            link(factors(V, link, LAST, NT, last_root))
            link(V.tensor_scalar(xss, degv, 2048.0, None, ALU.is_gt))
            V.tensor_reduce(bigc[:, 0:1], xss, AX_X, ALU.max).then_inc(S_["big_col"], 1)
            for g in range(LAST, NT):
                x_val(g)
            for g in range(POOL_LO, NT):
                source_lo(g)
                if g == POOL_LO:
                    dve.wait_ge(S_["big_sum"], 1)
                    V.tensor_copy(flag_i[0:1, 1:2], bank[6][0:1, 0:1]).then_inc(S_["big_set"], 1)
            for j in range(3):
                if j == 2:
                    dve.wait_ge(S_["bcast_made"], 1)
                for i in range(4 * j, min(4 * j + 4, NT)):
                    ins = V.tensor_scalar(val[:, j % 2, (i % 4) * P:(i % 4 + 1) * P], ident[:], isd[:, i:i + 1],
                                          None, ALU.mult)
                ins.then_inc(S_["diag_made"], 1)

            def pow2(cs, link, signal=None):
                link(V.tensor_scalar(bound[:, cs], bound[:, cs], 1e-30, None, ALU.max))
                link(V.tensor_scalar(ipw.bitcast(I32)[:, cs], bound.bitcast(I32)[:, cs], 0x7F800000, None,
                                     ALU.bitwise_and))
                link(V.tensor_scalar(pw.bitcast(I32)[:, cs], ipw.bitcast(I32)[:, cs], -1.0, float(268 << 23),
                                     ALU.mult, ALU.add))
                ins = V.tensor_scalar(ipw.bitcast(I32)[:, cs], ipw.bitcast(I32)[:, cs], float(-(14 << 23)), None,
                                      ALU.add)
                if signal:
                    ins.then_inc(S_[signal], 1)
                    dve.wait_ge(S_[signal], 1)
                else:
                    link(ins)

            def split_lo(i):
                kind, a, k, c0, n = loads[i]
                m = rows(k, nrows[a])
                dve.wait_ge(S_["stage_hi"], i + 1 - squares[i + 1])
                hi, lo, p = places(a, k, c0)
                src = buffers[at_buffer[i][0]][0:m, 0:n]
                if a == "W1":
                    src = src.rearrange("p (s n) -> p s n", n=P)
                V.scalar_tensor_tensor(lo[0:m], src, pw[0:m, p:p + 1], hi[0:m], ALU.mult, ALU.subtract)\
                    .then_inc(S_["stage_lo"], 1)

            def norms_ready(n):
                dve.wait_ge(S_["norm_done"], n)

            def t1_val(i):
                f, (n0, n) = i // 3, DSPLIT[i % 3]
                if i % 3 == 0:
                    dve.wait_ge(S_["t1_mm"], f + 1)
                if i == 0:
                    dve.wait_ge(S_["bcast_used"], 3)
                if i >= 2:
                    dve.wait_ge(S_["t1_lo"], i - 1)
                V.tensor_tensor(val[:, i % 2, 0:n], bank[3 * (f % 2) + i % 3][:, 0:n], row_bc[:, n0:n0 + n], ALU.mult)\
                    .then_inc(S_["t1_val"], 1)

            def t1_lo(i):
                f, (n0, n) = i // 3, DSPLIT[i % 3]
                dve.wait_ge(S_["t1_hi"], i + 1)
                V.tensor_tensor(t1T[1][:, f, n0:n0 + n], val[:, i % 2, 0:n], t1T[0][:, f, n0:n0 + n], ALU.subtract)\
                    .then_inc(S_["t1_lo"], 1)

            n1 = [i for i, l in enumerate(loads) if l[0] == "split" and l[1] == "W1"]
            for f in range(FT):
                for j in range(3):
                    i = 3 * f + j
                    t1_val(i)
                    if i >= 1:
                        t1_lo(i - 1)
                if f == 3:
                    norms_ready(1)
                    link(V.tensor_copy(bound[:, 0:1], norms[:, W1_:W1_ + 1]))
                    pow2(slice(0, 1), link, "w1_scaled")
                for i in W1_AT.get(f, ()):
                    split_lo(n1[i])
            t1_lo(3 * FT - 1)

            norms_ready(2)
            link(V.tensor_tensor(bound[:, H_:H_ + 1], norms[:, T1_:T1_ + 1], norms[:, W1_:W1_ + 1], ALU.mult))
            link(V.scalar_tensor_tensor(bound[:, H_:H_ + 1], bound[:, H_:H_ + 1], 1.0 / T1_SCALE,
                                        norms[:, B1_:B1_ + 1], ALU.mult, ALU.add))
            pow2(slice(H_, H_ + 1), link)
            link(V.scalar_tensor_tensor(coef[:, C_H:C_H + 1], ipw[:, W1_:W1_ + 1], 1.0 / T1_SCALE, pw[:, H_:H_ + 1],
                                        ALU.mult, ALU.mult))
            V.tensor_scalar(b1s, b1c, pw[:, H_:H_ + 1], None, ALU.mult).then_inc(S_["h_coef"], 1)
            n2 = [i for i, l in enumerate(loads) if l[0] == "split" and l[1] == "W2"]
            for mt in range(MT):
                m = rows(mt, MID)
                for j in range(3):
                    i, (n0, n) = 3 * mt + j, DSPLIT[j]
                    dve.wait_ge(S_["h_hi"], i + 1)
                    V.tensor_tensor(hT[1][0:m, mt, n0:n0 + n], val[0:m, i % 2, 0:n], hT[0][0:m, mt, n0:n0 + n],
                                    ALU.subtract).then_inc(S_["h_lo"], 1)
                if mt == 6:
                    norms_ready(3)
                    link(V.tensor_copy(bound[:, W2_:W2_ + 1], norms[:, W2_:W2_ + 1]))
                    pow2(slice(W2_, W2_ + 1), link, "w2_scaled")
                for k in W2_AT.get(mt, ()):
                    split_lo(n2[k])

            norms_ready(4)
            zc = slice(Z_, Z_ + 1)
            link(V.scalar_tensor_tensor(bound[:, zc], norms[:, H_:H_ + 1], ipw[:, H_:H_ + 1], norms[:, W2_:W2_ + 1],
                                        ALU.mult, ALU.mult))
            pow2(zc, link)
            link(V.tensor_tensor(coef[:, 6:7], ipw[:, H_:H_ + 1], ipw[:, W2_:W2_ + 1], ALU.mult))
            link(V.tensor_tensor(coef[:, 6:7], coef[:, 6:7], pw[:, zc], ALU.mult))
            V.tensor_scalar(zcoef, isd, coef[:, 6:7], None, ALU.mult).then_inc(S_["z_coef"], 1)
            link(V.tensor_scalar(ocoef, isd, ipw[:, zc], None, ALU.mult))
            for t in range(NT):
                m = rows(t, N)
                for j in range(2):
                    i = 2 * t + j
                    dve.wait_ge(S_["z_hi"], i + 1)
                    V.tensor_tensor(z[1][0:m, t, j * 512:(j + 1) * 512], val[0:m, i % 2, :],
                                    z[0][0:m, t, j * 512:(j + 1) * 512], ALU.subtract).then_inc(S_["z_lo"], 1)
            norms_ready(5)
            link(V.tensor_copy(bound[:, PD_:WW_ + 1], norms[:, PD_:WW_ + 1]))
            link(V.tensor_scalar(bound[:, G_:G_ + 1], norms[:, PD_:PD_ + 1], 32.0, None, ALU.mult))
            pow2(slice(G_, G_ + 1), link)
            pow2(slice(PD_, WW_ + 1), link)
            V.tensor_scalar(coef[:, C_P:C_P + 1], ipw[:, PD_:PD_ + 1], 1.0 / X_SCALE, None, ALU.mult)
            V.tensor_scalar(coef[:, C_B:C_B + 1], ipw[:, WW_:WW_ + 1], 1.0 / X_SCALE, None, ALU.mult)\
                .then_inc(S_["f_coef"], 1)

            def x2_tile(t):
                m = rows(t, N)
                dve.wait_ge(S_["o_mm"], t + 1)
                dve.wait_ge(S_["x2_b"], t + 1)
                for j in range(2):
                    o = x2[0:m, t, j * 512:(j + 1) * 512]
                    ins = V.scalar_tensor_tensor(o, bank[2 * ((t + 1) % 3) + j][0:m, :], ocoef[0:m, t:t + 1], o,
                                                 ALU.mult, ALU.add)
                    if j == 1:
                        ins.then_inc(S_["x2_done"], 1)
                dve.wait_ge(S_["x2_done"], t + 1)
                for j in range(2):
                    ins = V.bn_stats(stats[0:m, 6 * j:6 * j + 6], x2[0:m, t, j * 512:(j + 1) * 512])
                link(ins)
                V.bn_aggr(mv[0:m, :], stats[0:m, :].rearrange("p (a b) -> p a b", a=2)).then_inc(S_["ln_var"], 1)
                dve.wait_ge(S_["ln_std"], t + 1)
                link(V.reciprocal(lnr[0:m, 1:2], lnr[0:m, 0:1]))
                link(V.tensor_scalar(mv[0:m, 1:2], mv[0:m, 1:2], 1e-5, None, ALU.add))
                tmp, inv = ntmp[0:m, 0:1], lnr[0:m, 1:2]
                link(V.tensor_tensor(tmp, inv, inv, ALU.mult))
                link(V.tensor_tensor(tmp, tmp, mv[0:m, 1:2], ALU.mult))
                link(V.tensor_scalar(tmp, tmp, -0.5, 1.5, ALU.mult, ALU.add))
                link(V.tensor_tensor(inv, inv, tmp, ALU.mult))
                link(V.tensor_scalar(lnr[0:m, 2:3], lnr[0:m, 1:2], X_SCALE, None, ALU.mult))
                V.scalar_tensor_tensor(lnr[0:m, 3:4], mv[0:m, 0:1], -1.0, lnr[0:m, 2:3], ALU.mult, ALU.mult)\
                    .then_inc(S_["ln_coef"], 1)

            def yT_lo_tile(t):
                m = rows(t, N)
                for j in range(2):
                    dve.wait_ge(S_["yt_hi"], 2 * t + j + 1)
                    V.tensor_tensor(yT_lo[:, 4 * j:4 * j + 4, t * P:t * P + m],
                                    bank[6 + j][:, :].rearrange("p (k d) -> p k d", k=4)[:, :, 0:m],
                                    yT_hi[:, 4 * j:4 * j + 4, t * P:t * P + m], ALU.subtract)\
                        .then_inc(S_["yt_lo"], 1)

            npd = [i for i, l in enumerate(loads) if l[0] == "split" and l[1] == "Wpd"]
            for t in range(NT):
                x2_tile(t)
                if t >= 1:
                    yT_lo_tile(t - 1)
                if t < 4:
                    for k in (2 * t, 2 * t + 1):
                        split_lo(npd[k])
                if t == 5:
                    dve.wait_ge(S_["sim_norm"], 1)
                    link(V.tensor_scalar(simss, simr, 1e-12, None, ALU.max))
                    link(V.reciprocal(simss, simss))
                    for e in range(NEXP):
                        ins = V.tensor_scalar(sim_bc[:, e, :], sim_bc[:, e, :], simss[:, e:e + 1], None, ALU.mult)
                    link(ins)
                    link(V.tensor_scalar(tempv, temp_c, CLAMP_MAX, None, ALU.min))
            yT_lo_tile(NT - 1)

            def sim_products(t):
                m = rows(t, N)
                dve.wait_ge(S_["p_val"], t + 1)
                for e in range(NEXP):
                    if t:
                        dve.wait_ge(S_["dots_made"], NEXP * (t - 1) + e + 1)
                    V.tensor_tensor_reduce(out=scratch[0:m, e, :], in0=pr[0:m, t, :], in1=sim_bc[0:m, e, :],
                                           scale=1.0, scalar=0.0, op0=ALU.mult, op1=ALU.add,
                                           accum_out=dots[0:m, t, e:e + 1]).then_inc(S_["dots_made"], 1)

            dve.wait_ge(S_["o_mm"], NT)
            V.memset(down[:, NT - 1, :], 0.0)
            nw = [i for i, l in enumerate(loads) if l[0] == "split" and l[1] == "W"]
            for t in range(NT):
                m = rows(t, N)
                b = bank[(t + 4) % 6]
                if t < FT // 2:
                    for k in (2 * t, 2 * t + 1):
                        split_lo(nw[k])
                dve.wait_ge(S_["p_mm"], t + 1)
                V.scalar_tensor_tensor(pr[0:m, t, :], b[0:m, 0:PROJ], coef[0:m, C_P:C_P + 1], bp_bc[0:m, :],
                                       ALU.mult, ALU.add).then_inc(S_["p_val"], 1)
                V.tensor_scalar(down[0:m, t, :], b[0:m, PROJ:PD], coef[0:m, C_P:C_P + 1], None, ALU.mult)\
                    .then_inc(S_["p_used"], 1)
                if t >= SIM_LATER:
                    sim_products(t - SIM_LATER)
            for t in range(NT - SIM_LATER, NT):
                if t == NT - 2:
                    norms_ready(6)
                    link(V.tensor_copy(bound[:, WU_:WU_ + 1], norms[:, WU_:WU_ + 1]))
                    pow2(slice(WU_, WU_ + 1), link, "wu_scaled")
                    link(V.tensor_tensor(coef[:, C_L:C_L + 1], ipw[:, WU_:WU_ + 1], ipw[:, G_:G_ + 1], ALU.mult))
                sim_products(t)

            dve.wait_ge(S_["dots_made"], NT * NEXP)
            dve.wait_ge(S_["p_norm"], 1)

            def each(v):
                return v.unsqueeze(2).to_broadcast([P, NT, NEXP])

            link(V.tensor_scalar(pnorm, pnorm, 1e-12, None, ALU.max))
            link(V.reciprocal(pscale, pnorm))
            dve.wait_ge(S_["temp_exp"], 1)
            link(V.tensor_tensor(logit, dots, each(pscale), ALU.mult))
            link(V.tensor_scalar(logit, logit, tempe, None, ALU.mult))
            link(V.tensor_reduce(gmax, logit, AX_X, ALU.max))
            V.tensor_tensor(logit, logit, each(gmax), ALU.subtract).then_inc(S_["exp_in"], 1)
            dve.wait_ge(S_["exp_out"], 1)
            link(V.tensor_reduce(gsum, ex, AX_X, ALU.add))
            link(V.reciprocal(gsum, gsum))
            link(V.tensor_tensor(prob, ex, each(gsum), ALU.mult))
            link(V.tensor_reduce(gmax, prob, AX_X, ALU.max))
            link(V.tensor_tensor(hit, prob, each(gmax), ALU.is_equal))
            link(V.memset(keep, 1.0))
            for e in range(1, NEXP):
                link(V.tensor_tensor(keep[:, :, e], keep[:, :, e - 1], hit[:, :, e - 1], ALU.is_gt))
            link(V.tensor_tensor(pick, hit, keep, ALU.mult))
            link(V.tensor_tensor(pick, pick, prob, ALU.mult))
            link(V.tensor_scalar(pick, pick, pw[:, G_:G_ + 1], None, ALU.mult))
            r0 = 0
            for e, r in enumerate(RANKS):
                ins = V.tensor_tensor(gated[:, :, r0:r0 + r], down[:, :, r0:r0 + r],
                                      pick[:, :, e:e + 1].to_broadcast([P, NT, r]), ALU.mult)
                r0 += r
            link(ins)
            dve.wait_ge(S_["link_p"], 2)
            V.tensor_copy(g_rows[:, :, 32:32 + R], gated)
            link(V.tensor_copy(g_rows[:, :, 0:R], gated))
            V.tensor_tensor(g_rows[:, :, 64:64 + R], gated, g_rows[:, :, 0:R], ALU.subtract).then_inc(S_["g_made"], 1)
            def add_product(t, product, first):
                m = rows(t, N)
                q = 4 * ((t + 1) % 2) + (2 if product == "l_mm" else 0)
                scale = coef[0:m, C_L:C_L + 1] if product == "l_mm" else coef[0:m, C_B:C_B + 1]
                if first and t >= 2:
                    dve.wait_ge(out_done[t % 2], 16 * (t // 2))
                if not first:
                    dve.wait_ge(S_["res_half"], 2 * t + 2)
                dve.wait_ge(S_[product], t + 1)
                for j in range(2):
                    if t == NT - 1 and j == 1 and not first:
                        dve.wait_ge(S_["b_mm"], NT + 1)
                    o = res[t % 2][0:m, j * 512:(j + 1) * 512]
                    ins = V.scalar_tensor_tensor(o, bank[q + j][0:m, :], scale,
                                                 x2[0:m, t, j * 512:(j + 1) * 512] if first else o,
                                                 ALU.mult, ALU.add)
                    if first:
                        ins.then_inc(S_["res_half"], 1)
                    elif j == 1 or t == NT - 1:
                        ins.then_inc(S_["res_made"], 1)

            add_product(0, "b_mm", True)
            dve.wait_ge(S_["gt_mm"], 1)
            for j in range(2):
                ins = V.tensor_copy(gT[0:GP, 5 * j:5 * j + 5, :],
                                    bank[6 + j][:, :].bitcast(F16)[0:GP, 0:5 * P].rearrange("p (t d) -> p t d", t=5))
            ins.then_inc(S_["gt_made"], 1)

            for t in range(NT):
                first, second = ("b_mm", "l_mm") if t < 2 else ("l_mm", "b_mm")
                if t:
                    add_product(t, first, True)
                add_product(t, second, False)

        @block.scalar
        def _(act):
            A = nc.scalar.activation
            link = Link(act, "link_a")
            last_note = [None]

            def note_free():
                if last_note[0]:
                    act.wait_ge(S_[last_note[0][0]], last_note[0][1])

            def noted(name, value):
                last_note[0] = (name, value)

            def x_stats(t, link):
                m = rows(t, N)
                act.wait_ge(x_in[t], 16)
                if t == 0:
                    act.wait_ge(S_["cleared"], 6)
                note_free()
                link(A(junk[0:m, :], x_raw[0:m, t, :], ACT.Copy, accum_out=xsum[0:m, t:t + 1]))
                link(A(nmean[0:m, t:t + 1], xsum[0:m, t:t + 1], ACT.Copy, scale=-1.0 / D))
                A(junk[0:m, :], x_raw[0:m, t, :], ACT.Square, bias=nmean[0:m, t:t + 1],
                  accum_out=xss[0:m, t:t + 1]).then_inc(S_["x_ss"], 1)
                noted("x_ss", t + 1)

            def square(i):
                kind, a, k, c0, n = loads[i]
                m = rows(k, nrows[a])
                ss = {"W1": w1_ss, "W2": w2_ss, "W": w_ss, "Wpd": wpd_ss}[a]
                q = 2 * k + c0 // HALF if a == "W1" else k
                src = loaded(act, i)
                note_free()
                A(junk[0:m, 0:n], src[0:m, 0:n], ACT.Square, accum_out=ss[0:m, q:q + 1])\
                    .then_inc(S_["stage_sq"], 1)
                noted("stage_sq", squares[i + 1])

            def add_up(q, v):
                note_free()
                last_note[0] = None
                return A(junk[:, 0:v.shape[1]], v, ACT.Copy, accum_out=sums[:, q:q + 1])

            def norm(n, q0, q1):
                act.wait_ge(S_["norm_sum"], n)
                A(norms[:, q0:q1], bank[7][:, 0:q1 - q0], ACT.Sqrt).then_inc(S_["norm_done"], 1)

            def split_hi(i):
                kind, a, k, c0, n = loads[i]
                m = rows(k, nrows[a])
                hi, lo, p = places(a, k, c0)
                src = loaded(act, i)[0:m, 0:n]
                if a == "W1":
                    src = src.rearrange("p (s n) -> p s n", n=P)
                A(hi[0:m], src, ACT.Copy, scale=pw[0:m, p:p + 1]).then_inc(S_["stage_hi"], 1)

            def degree_out(g):
                act.wait_ge(S_["deg_done"], g + 1)
                if g >= LAST:
                    A(last_root[:, g - LAST:g - LAST + 1], bank[7][:, g:g + 1], ACT.Sqrt)
                A(degv[:, g:g + 1], bank[7][:, g:g + 1], ACT.Copy).then_inc(S_["degree_out"], 1)

            def source_hi(g):
                m = rows(g, N)
                if g < LAST:
                    act.wait_ge(S_["xval_made"], g + 1)
                else:
                    act.wait_ge(S_["xval_made_v"], g + 1 - LAST)
                A(xs_hi[0:m, g, :], x_raw[0:m, g, :], ACT.Copy).then_inc(S_["xhi_made"], 1)

            def take(w, j=None):
                act.wait_ge(S_["win_done"], w + 1)
                b = bank[w % WBANKS if j is None else j]
                A(adj[:, :, bass.ds(w * W, W)], b[:, 0:KEYS].rearrange("p (t d) -> p t d", t=NT), ACT.Copy)\
                    .then_inc(S_["adj_made"], 1)

            def take_rest(w, j=None):
                act.wait_ge(S_["sub_done"], w + 1)
                b = bank[w % WBANKS if j is None else j]
                A(adj_rest[:, :, bass.ds(w * W, W)], b[:, 0:KEYS].rearrange("p (t d) -> p t d", t=NT), ACT.Copy)\
                    .then_inc(S_["rest_made"], 1)

            act.wait_ge(S_["cleared"], 6)
            A(warm, eps_c, ACT.Sqrt)
            act.wait_ge(S_["sources_cut"], 1)
            A(feat[:, :, 2, :], low_i, ACT.Copy).then_inc(S_["feat_made"], 1)
            act.wait_ge(S_["sources_cut"], 2)
            A(feat[:, :, 1, :], src_low, ACT.Copy).then_inc(S_["feat_made"], 1)
            act.wait_ge(S_["dst_cut"], 1)
            A(keys[:, 1], win_i, ACT.Copy, scale=float(KEYS)).then_inc(S_["keys_ready"], 1)

            act.wait_ge(S_["flag_set"], 1)
            bad = act.value_load(flag_i[0:1, 0:1], min_val=0, max_val=2 * NWIN)
            with act.If(bad == 0):
                flink = Link(act, "link_fast_a")

                def source_hots(g):
                    n = min(SG, NSLOT - SG * g)
                    if g * SG >= SRING:
                        act.wait_ge(S_["key_used"], (g * SG - SRING + SG) // KG)
                    act.wait_ge(S_["score_made"], g + 1)
                    q = SG * g % SRING
                    A(src_hot[:, q:q + n, :].rearrange("p s n -> p (s n)"), score[g % 2][:, 0:n * P], ACT.Relu)\
                        .then_inc(S_["src_made"], 1)

                for b in range(NBLK):
                    m = rows(b, NSLOT)
                    act.wait_ge(S_["feat_mm"], b + 1)
                    A(feat_blk[0:m, b].rearrange("p k e -> p (k e)"), bank[b][0:m, 0:3 * P], ACT.Copy)\
                        .then_inc(S_["feat_out"], 1)
                for g in range(AHEAD):
                    source_hots(g)
                for w in range(NWIN):
                    for n in range(WFIRST[w], WFIRST[w + 1]):
                        if n % KG == 0:
                            g = n // KG
                            if n % SG == 0 and n // SG + AHEAD < NSG:
                                source_hots(n // SG + AHEAD)
                            for t in STATS_AT.get(g, ()):
                                x_stats(t, flink)
                            for t in OUT_AT.get(g, ()):
                                degree_out(t)
                            for t in HI_AT.get(g, ()):
                                source_hi(t)
                            for i in SQ_AT.get(g, ()):
                                square(i)
                    take(w)
                    if w - 1 in REST_WINS:
                        act.wait_ge(S_["rest_zero"], 1)
                        take_rest(w - 1)
                for t in OUT_AT[NG]:
                    degree_out(t)
                for t in HI_AT[NG]:
                    source_hi(t)
                note_free()
            with act.Else():
                last_note[0] = None
                slink = Link(act, "link_slow_a")
                act.wait_ge(S_["rest_zero"], 1)
                with act.Fori(0, NT) as g:
                    for j in range(WPT):
                        take(WPT * g + j, j)
                        take_rest(WPT * g + j, j)
                for t in range(ACT_STATS):
                    x_stats(t, slink)
                for i in range(SQ_A):
                    square(i)
                for g in range(NT):
                    degree_out(g)
                for g in range(NT):
                    source_hi(g)
                note_free()
            last_note[0] = None

            for j in range(3):
                act.wait_ge(S_["bcast_made"], j + 1)
                n = min(512, NT * P - 512 * j)
                A(row_bc[:, 512 * j:512 * j + n], bank[6 + j % 2][:, 0:n], ACT.Copy, scale=T1_SCALE / X_SCALE)\
                    .then_inc(S_["bcast_used"], 1)
            n1 = [i for i, l in enumerate(loads) if l[0] == "split" and l[1] == "W1"]
            for f in range(FT):
                for j in range(3):
                    i, (n0, n) = 3 * f + j, DSPLIT[j]
                    act.wait_ge(S_["t1_val"], i + 1)
                    A(t1T[0][:, f, n0:n0 + n], val[:, i % 2, 0:n], ACT.Copy).then_inc(S_["t1_hi"], 1)
                    act.wait_ge(S_["t1_hi"], i + 1)
                    note_free()
                    A(junk[:, 0:n], t1T[0][:, f, n0:n0 + n], ACT.Square, accum_out=t1_ss[:, i:i + 1])\
                        .then_inc(S_["t1_sq"], 1)
                    noted("t1_sq", i + 1)
                for i in SQ1_AT.get(f, ()):
                    square(i)
                if f == 2:
                    act.wait_ge(S_["stage_sq"], 2 * FT)
                    link(add_up(W1_, w1_ss))
                    act.wait_ge(S_["b1_in"], 16)
                    A(junk[:, 0:MT], b1c, ACT.Square, accum_out=sums[:, B1_:B1_ + 1]).then_inc(S_["norm_in"], 1)
                    noted("norm_in", 1)
                if f == 3:
                    norm(1, W1_, B1_ + 1)
                    act.wait_ge(S_["w1_scaled"], 1)
                for i in W1_AT.get(f, ()):
                    split_hi(n1[i])
            act.wait_ge(S_["t1_sq"], 3 * FT)
            add_up(T1_, t1_ss).then_inc(S_["norm_in"], 1)
            noted("norm_in", 2)
            norm(2, T1_, T1_ + 1)
            act.wait_ge(S_["h_coef"], 1)

            n2 = [i for i, l in enumerate(loads) if l[0] == "split" and l[1] == "W2"]
            s2 = [i for i, l in enumerate(loads) if l[0] == "sq" and l[1] == "W2"]
            for mt in range(MT):
                m = rows(mt, MID)
                act.wait_ge(S_["h_mm"], mt + 1)
                if mt == 0:
                    act.wait_ge(S_["t1_lo"], 3 * FT)
                    act.wait_ge(S_["spilled"], 16)
                for j in range(3):
                    i, (n0, n) = 3 * mt + j, DSPLIT[j]
                    if i >= 2:
                        act.wait_ge(S_["h_lo"], i - 1)
                    A(val[0:m, i % 2, 0:n], bank[3 * (mt % 2) + j][0:m, 0:n], ACT.Relu, bias=b1s[0:m, mt:mt + 1],
                      scale=coef[0:m, C_H:C_H + 1]).then_inc(S_["h_val"], 1)
                    act.wait_ge(S_["h_val"], i + 1)
                    A(hT[0][0:m, mt, n0:n0 + n], val[0:m, i % 2, 0:n], ACT.Copy).then_inc(S_["h_hi"], 1)
                    act.wait_ge(S_["h_hi"], i + 1)
                    note_free()
                    A(junk[0:m, 0:n], hT[0][0:m, mt, n0:n0 + n], ACT.Square, accum_out=h_ss[0:m, i:i + 1])\
                        .then_inc(S_["h_sq"], 1)
                    noted("h_sq", i + 1)
                if mt < 6:
                    for k in (2 * mt, 2 * mt + 1):
                        square(s2[k])
                if mt == 5:
                    act.wait_ge(S_["stage_sq"], squares[s2[-1] + 1])
                    add_up(W2_, w2_ss).then_inc(S_["norm_in"], 1)
                    noted("norm_in", 3)
                if mt == 6:
                    norm(3, W2_, W2_ + 1)
                    act.wait_ge(S_["w2_scaled"], 1)
                for k in W2_AT.get(mt, ()):
                    act.wait_ge(S_["h_mm"], k)
                    split_hi(n2[k])
            act.wait_ge(S_["h_sq"], 3 * MT)
            add_up(H_, h_ss).then_inc(S_["norm_in"], 1)
            noted("norm_in", 4)
            norm(4, H_, H_ + 1)
            act.wait_ge(S_["z_coef"], 1)

            spd = [i for i, l in enumerate(loads) if l[0] == "sq" and l[1] == "Wpd"]
            sw = [i for i, l in enumerate(loads) if l[0] == "sq" and l[1] == "W"]
            for t in range(NT):
                m = rows(t, N)
                act.wait_ge(S_["z_mm"], t + 1)
                if t == 0:
                    act.wait_ge(S_["h_lo"], 3 * MT)
                for j in range(2):
                    i = 2 * t + j
                    if i >= 2:
                        act.wait_ge(S_["z_lo"], i - 1)
                    A(val[0:m, i % 2, :], bank[2 * (t % 3) + j][0:m, :], ACT.Copy, scale=zcoef[0:m, t:t + 1])\
                        .then_inc(S_["z_val"], 1)
                    act.wait_ge(S_["z_val"], i + 1)
                    A(z[0][0:m, t, j * 512:(j + 1) * 512], val[0:m, i % 2, :], ACT.Copy).then_inc(S_["z_hi"], 1)
                if t < 4:
                    for k in (2 * t, 2 * t + 1):
                        square(spd[k])
                for k in {4: (0, 1, 2), 5: (3, 4, 5), 6: (6, 7)}.get(t, ()):
                    square(sw[k])
                if t == 6:
                    act.wait_ge(S_["stage_sq"], squares[-1])
                    link(add_up(PD_, wpd_ss))
                    add_up(WW_, w_ss).then_inc(S_["norm_in"], 1)
                    noted("norm_in", 5)
            norm(5, PD_, WW_ + 1)
            act.wait_ge(S_["f_coef"], 1)

            def yT_hi_tile(t):
                m = rows(t, N)
                for j in range(2):
                    act.wait_ge(S_["yt_mm"], 2 * t + j + 1)
                    A(yT_hi[:, 4 * j:4 * j + 4, t * P:t * P + m],
                      bank[6 + j][:, :].rearrange("p (k d) -> p k d", k=4)[:, :, 0:m], ACT.Copy)\
                        .then_inc(S_["yt_hi"], 1)

            npd = [i for i, l in enumerate(loads) if l[0] == "split" and l[1] == "Wpd"]
            for t in range(NT):
                m = rows(t, N)
                act.wait_ge(S_["ln_var"], t + 1)
                A(lnr[0:m, 0:1], mv[0:m, 1:2], ACT.Sqrt, bias=eps_c[0:m, :]).then_inc(S_["ln_std"], 1)
                act.wait_ge(S_["ln_coef"], t + 1)
                if t == 0:
                    act.wait_ge(S_["z_lo"], 2 * NT)
                else:
                    act.wait_ge(S_["yt_mm"], 2 * t)
                A(val[0:m, :, :].rearrange("p a b -> p (a b)"), x2[0:m, t, :], ACT.Identity, bias=lnr[0:m, 3:4],
                  scale=lnr[0:m, 2:3]).then_inc(S_["y_made"], 1)
                if t >= 1:
                    yT_hi_tile(t - 1)
                if t < 4:
                    for k in (2 * t, 2 * t + 1):
                        split_hi(npd[k])
                if t == 4:
                    act.wait_ge(S_["sim_in"], 48)
                    note_free()
                    for e in range(NEXP):
                        link(A(junk[:, 0:PROJ], sim_bc[:, e, :], ACT.Square, accum_out=simss[:, e:e + 1]))
                    last_note[0] = None
                    A(simr, simss, ACT.Sqrt).then_inc(S_["sim_norm"], 1)
            yT_hi_tile(NT - 1)

            nw = [i for i, l in enumerate(loads) if l[0] == "split" and l[1] == "W"]
            act.wait_ge(S_["o_mm"], NT)
            for t in range(NT):
                m = rows(t, N)
                if t < FT // 2:
                    for k in (2 * t, 2 * t + 1):
                        split_hi(nw[k])
                act.wait_ge(S_["p_val"], t + 1)
                note_free()
                A(junk[0:m, 0:PROJ], pr[0:m, t, :], ACT.Square, accum_out=pss[0:m, t:t + 1])\
                    .then_inc(S_["p_sq"], 1)
                noted("p_sq", t + 1)
                if t == FT:
                    act.wait_ge(S_["wu_in"], 48)
                    note_free()
                    A(junk[0:R, 0:D], wu_raw[0:R, :], ACT.Square, accum_out=sums[0:R, WU_:WU_ + 1])\
                        .then_inc(S_["norm_in"], 1)
                    noted("norm_in", 6)
            norm(6, WU_, WU_ + 1)
            act.wait_ge(S_["p_sq"], NT)
            A(pnorm, pss, ACT.Sqrt).then_inc(S_["p_norm"], 1)
            A(tempe, tempv, ACT.Exp).then_inc(S_["temp_exp"], 1)
            act.wait_ge(S_["exp_in"], 1)
            A(ex, logit, ACT.Exp).then_inc(S_["exp_out"], 1)

        @block.tensor
        def _(pe):
            T = nc.tensor

            pe.wait_ge(S_["consts"], NCONST)
            pe.wait_ge(S_["chunk_ends"], 1)
            for k in range(2):
                for j in range(CG):
                    ins = T.matmul(bank[5 + k][0:NWIN, j * P:(j + 1) * P],
                                   ends16[:, k, j:j + 1].to_broadcast([P, NWIN]), ident16[:], start=True, stop=True)
            ins.then_inc(S_["range_done"], 1)
            pe.wait_ge(S_["member_in"], 16)
            pe.wait_ge(S_["start_made"], 1)
            T.matmul(bank[4][:, 0:NSLOT], start16[0:NWIN + 1, 0:1].to_broadcast([NWIN + 1, P]),
                     member_sb[0:NWIN + 1, 0:NSLOT], start=True, stop=True).then_inc(S_["slot_rows"], 1)
            pe.wait_ge(S_["range_cols"], 1)
            T.matmul(bank[7][0:1, 0:1], badc[0:NWIN, 0:1], ones[0:NWIN, 0:1], start=True, stop=True)\
                .then_inc(S_["flag_sum"], 1)

            def close_window(j, i, t):
                T.matmul(bank[j][:, bass.ds(t * W, W)], ident16[:], ident16[:, i * W:(i + 1) * W],
                         start=False, stop=True, skip_group_check=True).then_inc(S_["win_done"], 1)

            def open_window(j):
                T.matmul(bank[j][:, 0:W], ident16[:], zero16[:], start=True, stop=False, skip_group_check=True)

            def subtract(w, j):
                pe.wait_ge(S_["adj_made"], w + 1)
                T.matmul(bank[j][:, 0:KEYS], minus16[:], adj[:, :, bass.ds(w * W, W)], start=False, stop=True,
                         skip_group_check=True).then_inc(S_["sub_done"], 1)

            def degrees(g, parts):
                if len(parts) == 2:
                    pe.wait_ge(S_["rest_made"], WPT * (g + 1))
                else:
                    pe.wait_ge(S_["adj_made"], WPT * (g + 1))
                if g:
                    pe.wait_ge(S_["degree_out"], g)
                for i, a in enumerate(parts):
                    for t in range(NT):
                        ins = T.matmul(bank[7][:, g:g + 1], a[:, t, g * P:(g + 1) * P], ones16[:, 0:1],
                                       start=(i == 0 and t == 0), stop=(i == len(parts) - 1 and t == NT - 1))
                ins.then_inc(S_["deg_done"], 1)

            pe.wait_ge(S_["flag_set"], 1)
            bad = pe.value_load(flag_i[0:1, 0:1], min_val=0, max_val=2 * NWIN)
            with pe.If(bad == 0):
                def gather_features(b):
                    m = rows(b, NSLOT)
                    for j in range(CG):
                        ins = T.matmul(bank[b][0:m, 0:3 * P], pick_slot[:, j, b * P:b * P + m],
                                       feat[:, j].rearrange("p k e -> p (k e)"), start=(j == 0), stop=(j == CG - 1))
                    ins.then_inc(S_["feat_mm"], 1)

                feat_count = [0, 0]

                def scores(g):
                    i = SG * g // FSLOT
                    if SG * g % FSLOT == 0:
                        feat_count[i % 2] += 3 * len(feature_pieces(i))
                        pe.wait_ge(feat_in[i % 2], 16 * feat_count[i % 2])
                    if g >= 2:
                        pe.wait_ge(S_["src_made"], g - 1)
                    elif g == 1:
                        pe.wait_ge(S_["turned_used"], 1)
                    for c in range(SG * g, min(SG * g + SG, NSLOT)):
                        q = c % SG * P
                        f = (c - i * FSLOT) * P
                        ins = T.matmul(score[g % 2][:, q:q + P], feat_rows[:, i % 2, f:f + P], line16[:],
                                       start=True, stop=True)
                    ins.then_inc(S_["score_made"], 1)

                pe.wait_ge(S_["feat_made"], 3)
                pe.wait_ge(S_["slots_picked"], 1)
                gather_features(0)
                pe.wait_ge(S_["keys_ready"], 2)
                for h in range(2):
                    for j in range(CG):
                        ins = T.matmul(bank[4][:, 0:NSLOT], keys[:, h, j, :], pick_slot[:, j, :],
                                       start=(h == 0 and j == 0), stop=False, skip_group_check=True)
                T.matmul(bank[4][:, 0:NSLOT], member_sb[0:NWIN + 1, NSLOT:NSLOT + 1].to_broadcast([NWIN + 1, P]),
                         member_sb[0:NWIN + 1, 0:NSLOT], start=False, stop=True, skip_group_check=True)\
                    .then_inc(S_["turned"], 1)
                for b in range(1, NBLK):
                    gather_features(b)
                pe.wait_ge(S_["line_in"], 16)
                pe.wait_ge(S_["feat_out"], NBLK)
                for g in range(AHEAD):
                    scores(g)
                for w in range(NWIN):
                    j = w % WBANKS
                    if w >= WBANKS:
                        pe.wait_ge(S_["adj_made"], w - WBANKS + 1)
                        if w - WBANKS in REST_WINS:
                            pe.wait_ge(S_["rest_made"], w - WBANKS + 1)
                    for n in range(WFIRST[w], WFIRST[w + 1]):
                        if n % KG == 0:
                            if n % SG == 0 and n // SG + AHEAD < NSG:
                                scores(n // SG + AHEAD)
                            for g in DEG_AT.get(n // KG, ()):
                                degrees(g, (adj, adj_rest) if g < REST_TILES else (adj,))
                            pe.wait_ge(S_["src_made"], n // SG + 1)
                            pe.wait_ge(S_["key_made"], n // KG + 1)
                        ins = T.matmul(bank[j][:, 0:KEYS], src_hot[:, n % SRING, :],
                                       key_hot[:, n % KRING // KG, :, n % KG],
                                       start=(n == WFIRST[w]), stop=False, skip_group_check=True)
                        if n % KG == KG - 1:
                            ins.then_inc(S_["key_used"], 1)
                    close_window(j, w % WPT, w // WPT)
                    if w - 1 in REST_WINS:
                        subtract(w - 1, (w - 1) % WBANKS)
                for g in DEG_AT[NG]:
                    degrees(g, (adj,))
                pe.wait_ge(S_["rest_zero"], 1)
                pe.wait_ge(S_["adj_made"], NWIN)
                pe.wait_ge(S_["rest_made"], len(REST_WINS))
            with pe.Else():
                pe.wait_ge(S_["feat_made"], 3)
                pe.wait_ge(S_["keys_ready"], 2)
                pe.wait_ge(S_["slots_picked"], 1)
                for i, parts in enumerate(((keys[:, 0], keys[:, 1]), (feat[:, :, 2],))):
                    for j in range(CG):
                        for h, v in enumerate(parts):
                            ins = T.matmul(bank[4 + i][:, j * P:(j + 1) * P], v[:, j, :], ident16[:],
                                           start=(h == 0), stop=(h == len(parts) - 1))
                    ins.then_inc(S_["turned"], 1)
                pe.sem_inc(S_["slow_used"], 1)

                def slow_windows(g):
                    for j in range(WPT):
                        w = WPT * g + j
                        open_window(j)
                        with pe.Fori(0, NCH) as c:
                            pe.wait_ge(S_["slow_made"], w * NCH + c + 1)
                            T.matmul(bank[j][:, 0:KEYS], src_hot[:, 0, :], key_hot[:, 0, :, 0], start=False, stop=True,
                                     skip_group_check=True).then_inc(S_["slow_used"], 1)
                        close_window(j, j, g)
                        subtract(w, j)

                slow_windows(0)
                with pe.Fori(1, NT) as g:
                    pe.wait_ge(S_["rest_made"], WPT * g)
                    slow_windows(g)
                for g in range(NT):
                    degrees(g, (adj, adj_rest))
                pe.wait_ge(S_["rest_made"], NWIN)

            def norm_mm(n, q0, q1):
                pe.wait_ge(S_["norm_in"], n)
                if n == 1:
                    pe.wait_ge(S_["bcast_used"], 3)
                else:
                    pe.wait_ge(S_["norm_done"], n - 1)
                T.matmul(bank[7][:, 0:q1 - q0], ones[:], sums[:, q0:q1], start=True, stop=True)\
                    .then_inc(S_["norm_sum"], 1)

            def t1_group(f, t, last=False):
                m = rows(t, N)
                for p, xp in enumerate((xs_hi, xs_lo)):
                    for j, (n0, n) in enumerate(DSPLIT):
                        ins = T.matmul(bank[3 * (f % 2) + j][:, 0:n], xp[0:m, t, f * P:(f + 1) * P],
                                       adj[0:m, t, n0:n0 + n], start=(t == 0 and p == 0), stop=(last and p == 1),
                                       skip_group_check=True)
                return ins

            def t1_rest(f):
                with pe.If(big > 0):
                    for t in range(NT):
                        m = rows(t, N)
                        for xp in (xs_hi, xs_lo):
                            for j, (n0, n) in enumerate(DSPLIT):
                                T.matmul(bank[3 * (f % 2) + j][:, 0:n], xp[0:m, t, f * P:(f + 1) * P],
                                         adj_rest[0:m, t, n0:n0 + n], start=False, stop=False, skip_group_check=True)

            big = None
            for f in range(FT):
                if f >= 2:
                    pe.wait_ge(S_["t1_val"], 3 * (f - 1))
                for t in range(NT):
                    if f == 0:
                        if t < POOL_LO:
                            pe.wait_ge(S_["xlo_made"], t + 1)
                        else:
                            pe.wait_ge(S_["xlo_made_v"], t + 1 - POOL_LO)
                    if f == 0 and t == 5:
                        pe.wait_ge(S_["big_col"], 1)
                        T.matmul(bank[6][0:1, 0:1], bigc[:, 0:1], ones[:, 0:1], start=True, stop=True)\
                            .then_inc(S_["big_sum"], 1)
                    if t == NT - 1:
                        if f == 0:
                            pe.wait_ge(S_["big_set"], 1)
                            big = pe.value_load(flag_i[0:1, 1:2], min_val=0, max_val=P)
                        t1_rest(f)
                    ins = t1_group(f, t, t == NT - 1)
                ins.then_inc(S_["t1_mm"], 1)
                if f == 0:
                    for j in range(3):
                        pe.wait_ge(S_["diag_made"], j + 1)
                        if j == 2:
                            pe.wait_ge(S_["bcast_used"], 1)
                        for i in range(4 * j, min(4 * j + 4, NT)):
                            q = (i % 4) * P
                            ins = T.matmul(bank[6 + j % 2][:, q:q + P], ones[:], val[:, j % 2, q:q + P],
                                           start=True, stop=True)
                        ins.then_inc(S_["bcast_made"], 1)
                if f == 3:
                    norm_mm(1, W1_, B1_ + 1)

            for mt in range(MT):
                m = rows(mt, MID)
                if mt < 2:
                    pe.wait_ge(S_["t1_val"], 3 * (FT - 1 + mt))
                else:
                    pe.wait_ge(S_["h_val"], 3 * (mt - 1))
                for k in range(FT):
                    if mt == 0:
                        pe.wait_ge(S_["t1_lo"], 3 * (k + 1))
                        pe.wait_ge(S_["stage_lo"], 2 * (k + 1))
                    for q, (wp, tp) in enumerate(((0, 0), (0, 1), (1, 0))):
                        for j, (n0, n) in enumerate(DSPLIT):
                            ins = T.matmul(bank[3 * (mt % 2) + j][0:m, 0:n], w1_slot[mt][:, wp, k, 0:m],
                                           t1T[tp][:, k, n0:n0 + n], start=(k == 0 and q == 0),
                                           stop=(k == FT - 1 and q == 2))
                ins.then_inc(S_["h_mm"], 1)
                if mt == 0:
                    norm_mm(2, T1_, T1_ + 1)
                if mt == 6:
                    norm_mm(3, W2_, W2_ + 1)

            for t in range(NT):
                m = rows(t, N)
                if t < 3:
                    pe.wait_ge(S_["h_val"], 3 * (MT - 1 + min(t, 1)))
                else:
                    pe.wait_ge(S_["z_val"], 2 * (t - 2))
                for k in range(MT):
                    K = rows(k, MID)
                    if t == 0:
                        pe.wait_ge(S_["h_lo"], 3 * (k + 1))
                        pe.wait_ge(S_["stage_lo"], 2 * FT + k + 1)
                    for q, (hp, wp) in enumerate(((0, 0), (0, 1), (1, 0))):
                        for j in range(2):
                            ins = T.matmul(bank[2 * (t % 3) + j][0:m, :], hT[hp][0:K, k, t * P:t * P + m],
                                           w2_slot[k][0:K, wp, j * 512:(j + 1) * 512], start=(k == 0 and q == 0),
                                           stop=(k == MT - 1 and q == 2))
                ins.then_inc(S_["z_mm"], 1)
                if t == 0:
                    norm_mm(4, H_, H_ + 1)
                if t == 8:
                    norm_mm(5, PD_, WW_ + 1)

            def turn(t):
                m = rows(t, N)
                pe.wait_ge(S_["y_made"], t + 1)
                if t == 0:
                    pe.wait_ge(S_["norm_done"], 5)
                for j in range(2):
                    if t >= 1:
                        pe.wait_ge(S_["yt_lo"], 2 * (t - 1) + j + 1)
                    for i in range(4):
                        k = 4 * j + i
                        ins = T.transpose(bank[6 + j][:, i * P:i * P + m], val[0:m, k // 4, i * P:(i + 1) * P],
                                          ident[0:m, 0:m])
                    ins.then_inc(S_["yt_mm"], 1)

            def conv2(t, s, a, first, last):
                m, K = rows(t, N), rows(s, N)
                for p in range(2):
                    for j in range(2):
                        ins = T.matmul(bank[2 * ((t + 1) % 3) + j][0:m, :], a[0:K, s, t * P:t * P + m],
                                       z[p][0:K, s, j * 512:(j + 1) * 512], start=(first and p == 0),
                                       stop=(last and p == 1), skip_group_check=True)
                return ins

            for t in range(NT):
                if t < 3:
                    pe.wait_ge(S_["z_val"], 2 * (NT - 2 + t))
                else:
                    pe.wait_ge(S_["x2_done"], t - 2)
                for s in range(NT):
                    if t == 0:
                        pe.wait_ge(S_["z_lo"], 2 * s + 2)
                    if s == NT - 1:
                        with pe.If(big > 0):
                            pe.wait_ge(S_["rest_in"], 16)
                            for s2 in range(NT):
                                conv2(t, s2, rest2, False, False)
                    ins = conv2(t, s, adj, s == 0, s == NT - 1)
                ins.then_inc(S_["o_mm"], 1)
                if t >= 1:
                    turn(t - 1)

            def project(t):
                m = rows(t, N)
                b = bank[(t + 4) % 6]
                pe.wait_ge(S_["x2_done"], min(NT, 8 + t // 2))
                if t >= 6:
                    pe.wait_ge(S_["p_used"], t - 5)
                pe.wait_ge(S_["yt_lo"], 2 * t + 2)
                for k in range(FT):
                    for q, (yp, wp) in enumerate(((yT_hi, wpd_hi), (yT_hi, wpd_lo), (yT_lo, wpd_hi))):
                        ins = T.matmul(b[0:m, 0:PD], yp[:, k, t * P:t * P + m], wp[:, k, :],
                                       start=(k == 0 and q == 0), stop=(k == FT - 1 and q == 2))
                ins.then_inc(S_["p_mm"], 1)

            pe.wait_ge(S_["stage_lo"], 2 * FT + MT + FT)
            for t in range(NT):
                if t == 2:
                    turn(NT - 1)
                project(t)

            def base(t):
                m = rows(t, N)
                q0 = 4 * ((t + 1) % 2)
                if t < 2:
                    pe.wait_ge(S_["p_used"], (8, NT)[t])
                elif t < 4:
                    pe.wait_ge(S_["res_half"], 2 * (t - 1))
                else:
                    pe.wait_ge(S_["res_made"], t - 1)
                last = t == NT - 1
                for js in ((0,), (1,)) if last else ((0, 1),):
                    for k in range(FT):
                        if t == 0:
                            pe.wait_ge(S_["stage_lo"], 2 * FT + MT + FT + k + 1)
                            if k == FT // 2:
                                norm_mm(6, WU_, WU_ + 1)
                        for q, (yp, wp) in enumerate(((yT_hi, w_hi), (yT_hi, w_lo), (yT_lo, w_hi))):
                            for j in js:
                                ins = T.matmul(bank[q0 + j][0:m, :], yp[:, k, t * P:t * P + m],
                                               wp[:, k, j * 512:(j + 1) * 512], start=(k == 0 and q == 0),
                                               stop=(k == FT - 1 and q == 2))
                    ins.then_inc(S_["b_mm"], 1)

            def low_rank(t):
                m = rows(t, N)
                q0 = 4 * ((t + 1) % 2)
                if t >= 4:
                    pe.wait_ge(S_["res_half"], 2 * (t - 1))
                elif t >= 2:
                    pe.wait_ge(S_["res_made"], t - 1)
                for j in range(2):
                    ins = T.matmul(bank[q0 + 2 + j][0:m, :], gT[0:GP, t, 0:m], wu[0:GP, j * 512:(j + 1) * 512],
                                   start=True, stop=True)
                ins.then_inc(S_["l_mm"], 1)

            base(0)
            base(1)
            pe.wait_ge(S_["norm_done"], 6)
            pe.wait_ge(S_["g_made"], 1)
            pe.wait_ge(S_["yt_lo"], 2 * NT)
            for i in range(NT):
                ins = T.transpose(bank[6 + i // 5][:, :].bitcast(F16)[0:GP, (i % 5) * P:(i % 5 + 1) * P],
                                  g_rows[:, i, :], ident16[:])
            ins.then_inc(S_["gt_mm"], 1)
            pe.wait_ge(S_["gt_made"], 1)
            pe.wait_ge(S_["wu_done"], 1)
            low_rank(0)
            low_rank(1)
            for t in range(2, NT):
                for part in (base, low_rank) if t < 4 else (low_rank, base):
                    part(t)


def square_line():
    l = np.arange(P)
    out = np.zeros((P, P), np.float16)
    out[0], out[1], out[2], out[3], out[4] = -1, -1, 2 * l, -(l * l // 16 * 16), 1 - l * l % 16
    return out


def slot_members():
    out = np.zeros((NWIN + 1, NSLOT + 1), np.float16)
    out[:NWIN, NSLOT] = -KEYS * np.arange(NWIN)
    for w in range(NWIN):
        out[w, WFIRST[w]:WFIRST[w + 1]] = 1
        out[NWIN, WFIRST[w]:WFIRST[w + 1]] = np.arange(WSLOTS[w])
    return out


def kernel(**inputs):
    import concourse.bacc as _bacc
    from concourse.bass_utils import run_bass_kernel_spmd as _run

    g = {k: np.asarray(v) for k, v in inputs.items()}
    pad = CROWS * P - E
    w1 = np.zeros((D, MIDP), np.float32)
    w1[:, :MID] = g["L0_gnn_W1"]
    b1 = np.zeros(MIDP, np.float32)
    b1[:MID] = g["L0_gnn_b1"]
    arrays = {
        "x": g["x"],
        "src": np.concatenate([g["src"], np.zeros(pad, g["src"].dtype)]).reshape(CROWS, P),
        "dst": np.concatenate([g["dst"], np.full(pad, NWIN * W, g["dst"].dtype)]).reshape(CROWS, P),
        "ranges": np.array([[n + CROWS] for n in WSLOTS], np.float32),
        "line": square_line(),
        "member": slot_members(),
        "W1": w1, "b1": b1.reshape(MT, P).T, "W2": g["L0_gnn_W2"], "b2": g["L0_gnn_b2"],
        "WT": g["L0_ffn_W"].T,
        "WpdT": np.concatenate([g["L0_ffn_Wp"]] + [g[f"L0_ffn_Wd{i}"] for i in range(NEXP)]).T,
        "bp": g["L0_ffn_bp"], "simT": g["L0_ffn_sim"].T, "temp": g["L0_ffn_temp"],
        "WuT": np.concatenate([g[f"L0_ffn_Wu{i}"].T for i in range(NEXP)]),
    }
    arrays = {k: np.ascontiguousarray(v) for k, v in arrays.items()}
    nc = _bacc.Bacc("TRN2", target_bir_lowering=False, num_devices=1)
    args = [nc.dram_tensor("in_" + k, v.shape, mybir.dt.from_np(v.dtype), kind="ExternalInput").ap()
            for k, v in arrays.items()]
    o = nc.dram_tensor("out", (N, D), F32, kind="ExternalOutput").ap()
    build(nc, *args, o)
    r = _run(nc, [{"in_" + k: v for k, v in arrays.items()}], core_ids=[0])
    return r.results[0]["out"]
```
